# Optimizing a Trainium2 kernel written in Bass

```python
import numpy as np
import jax
import jax.numpy as jnp

def _softmax(x, axis=-1):
    return jax.nn.softmax(x, axis=axis)
def _gelu(x):
    return jax.nn.gelu(x, approximate=True)
def _silu(x):
    return jax.nn.silu(x)
def _sigmoid(x):
    return jax.nn.sigmoid(x)
def _layernorm(x, axis=-1, eps=1e-5):
    m = jnp.mean(x, axis=axis, keepdims=True)
    v = jnp.var(x, axis=axis, keepdims=True)
    return (x - m) / jnp.sqrt(v + eps)
def _scatter_add(tgt, idx, src, axis=0):
    return tgt.at[idx].add(src)
def _segment_sum(src, seg, n):
    return jax.ops.segment_sum(src, seg, n)

kernel_name = 'mk_conv_seq_d2_conv_nchw384_ce5685'

def setup_inputs(seed: int = 0):
    np.random.seed(seed)
    _w = jnp.asarray
    def _rec_inputs():
        import jax
        import jax.numpy as jnp
        _gk = jax.random.key(seed)
        x = -0.0005058 + 1 * jax.random.normal(jax.random.fold_in(_gk, 1), (4, 384, 48, 48), jnp.float32)
        return x
    x = _rec_inputs()
    def _L0_conv_setup():
        import jax, jax.numpy as jnp
        import numpy as np
        from jax import lax
        DIM = 384
        NUM_HEADS = 8
        HEAD_DIM = DIM // NUM_HEADS
        KS = 7
        LN_EPS = 1e-06
        BN_EPS = 1e-05

        def _layernorm(t, g, b):
            mu = jnp.mean(t, axis=-1, keepdims=True)
            var = jnp.mean(jnp.square(t - mu), axis=-1, keepdims=True)
            return (t - mu) * lax.rsqrt(var + LN_EPS) * g + b
        key = jax.random.key(seed)
        ks = jax.random.split(key, 8)
        B, C, H, W = (4, DIM, 48, 48)
        x = jax.random.normal(ks[0], (B, C, H, W), dtype=jnp.float32)
        conv_w = jax.random.normal(ks[1], (C, 1, KS, KS), dtype=jnp.float32) * (1.0 / KS)
        bn_gamma = jnp.ones((C,), jnp.float32)
        bn_beta = jnp.zeros((C,), jnp.float32)
        bn_mean = jnp.zeros((C,), jnp.float32)
        bn_var = jnp.ones((C,), jnp.float32)
        ln_gamma = jnp.ones((C,), jnp.float32)
        ln_beta = jnp.zeros((C,), jnp.float32)
        qkv_w = jax.random.normal(ks[2], (3 * C, C), dtype=jnp.float32) * C ** (-0.5)
        qkv_b = jnp.zeros((3 * C,), jnp.float32)
        proj_w = jax.random.normal(ks[3], (C, C), dtype=jnp.float32) * C ** (-0.5)
        proj_b = jnp.zeros((C,), jnp.float32)
        return dict(x=x, conv_w=conv_w, bn_gamma=bn_gamma, bn_beta=bn_beta, bn_mean=bn_mean, bn_var=bn_var, ln_gamma=ln_gamma, ln_beta=ln_beta, qkv_w=qkv_w, qkv_b=qkv_b, proj_w=proj_w, proj_b=proj_b)
    _L0_conv_all = _L0_conv_setup()
    _L0_conv_in = {k: v for k, v in _L0_conv_all.items() if k in ('conv_w', 'bn_gamma', 'bn_beta', 'bn_mean', 'bn_var', 'ln_gamma', 'ln_beta', 'qkv_w', 'qkv_b', 'proj_w', 'proj_b', )}
    del _L0_conv_all

    def _L1_conv_setup():
        import jax, jax.numpy as jnp
        import numpy as np
        C = 384
        H = 4 * C
        EPS_LN = 1e-06
        EPS_GRN = 1e-06
        key = jax.random.key(seed)
        ks = jax.random.split(key, 8)
        x = jax.random.normal(ks[0], (32, C, 28, 28), dtype=jnp.float32)
        dw_w = jax.random.normal(ks[1], (C, 1, 7, 7), dtype=jnp.float32) * 0.02
        dw_b = jnp.zeros((C,), dtype=jnp.float32)
        ln_g = jnp.ones((C,), dtype=jnp.float32)
        ln_b = jnp.zeros((C,), dtype=jnp.float32)
        w1 = jax.random.normal(ks[2], (C, H), dtype=jnp.float32) * 0.02
        b1 = jnp.zeros((H,), dtype=jnp.float32)
        grn_g = jnp.zeros((H,), dtype=jnp.float32)
        grn_b = jnp.zeros((H,), dtype=jnp.float32)
        w2 = jax.random.normal(ks[3], (H, C), dtype=jnp.float32) * 0.02
        b2 = jnp.zeros((C,), dtype=jnp.float32)
        return {'x': x, 'dw_w': dw_w, 'dw_b': dw_b, 'ln_g': ln_g, 'ln_b': ln_b, 'w1': w1, 'b1': b1, 'grn_g': grn_g, 'grn_b': grn_b, 'w2': w2, 'b2': b2}
    _L1_conv_all = _L1_conv_setup()
    _L1_conv_in = {k: v for k, v in _L1_conv_all.items() if k in ('dw_w', 'dw_b', 'ln_g', 'ln_b', 'w1', 'b1', 'grn_g', 'grn_b', 'w2', 'b2', )}
    del _L1_conv_all

    return {
        "x": x,
        "L0_conv_conv_w": _L0_conv_in["conv_w"],
        "L0_conv_bn_gamma": _L0_conv_in["bn_gamma"],
        "L0_conv_bn_beta": _L0_conv_in["bn_beta"],
        "L0_conv_bn_mean": _L0_conv_in["bn_mean"],
        "L0_conv_bn_var": _L0_conv_in["bn_var"],
        "L0_conv_ln_gamma": _L0_conv_in["ln_gamma"],
        "L0_conv_ln_beta": _L0_conv_in["ln_beta"],
        "L0_conv_qkv_w": _L0_conv_in["qkv_w"],
        "L0_conv_qkv_b": _L0_conv_in["qkv_b"],
        "L0_conv_proj_w": _L0_conv_in["proj_w"],
        "L0_conv_proj_b": _L0_conv_in["proj_b"],
        "L1_conv_dw_w": _L1_conv_in["dw_w"],
        "L1_conv_dw_b": _L1_conv_in["dw_b"],
        "L1_conv_ln_g": _L1_conv_in["ln_g"],
        "L1_conv_ln_b": _L1_conv_in["ln_b"],
        "L1_conv_w1": _L1_conv_in["w1"],
        "L1_conv_b1": _L1_conv_in["b1"],
        "L1_conv_grn_g": _L1_conv_in["grn_g"],
        "L1_conv_grn_b": _L1_conv_in["grn_b"],
        "L1_conv_w2": _L1_conv_in["w2"],
        "L1_conv_b2": _L1_conv_in["b2"],
    }

def reference(x, L0_conv_conv_w, L0_conv_bn_gamma, L0_conv_bn_beta, L0_conv_bn_mean, L0_conv_bn_var, L0_conv_ln_gamma, L0_conv_ln_beta, L0_conv_qkv_w, L0_conv_qkv_b, L0_conv_proj_w, L0_conv_proj_b, L1_conv_dw_w, L1_conv_dw_b, L1_conv_ln_g, L1_conv_ln_b, L1_conv_w1, L1_conv_b1, L1_conv_grn_g, L1_conv_grn_b, L1_conv_w2, L1_conv_b2):
    import jax
    import jax.numpy as jnp
    def _L0_conv_ref(x, conv_w, bn_gamma, bn_beta, bn_mean, bn_var, ln_gamma, ln_beta, qkv_w, qkv_b, proj_w, proj_b):
        import jax, jax.numpy as jnp
        import numpy as np
        from jax import lax
        DIM = 384
        NUM_HEADS = 8
        HEAD_DIM = DIM // NUM_HEADS
        KS = 7
        LN_EPS = 1e-06
        BN_EPS = 1e-05

        def _layernorm(t, g, b):
            mu = jnp.mean(t, axis=-1, keepdims=True)
            var = jnp.mean(jnp.square(t - mu), axis=-1, keepdims=True)
            return (t - mu) * lax.rsqrt(var + LN_EPS) * g + b
        B, C, H, W = x.shape
        N = H * W
        nh, hd = (NUM_HEADS, HEAD_DIM)
        scale = hd ** (-0.5)
        x_flat = x.reshape(B, C, N).transpose(0, 2, 1)
        local = lax.conv_general_dilated(x, conv_w, window_strides=(1, 1), padding='SAME', dimension_numbers=('NCHW', 'OIHW', 'NCHW'), feature_group_count=C)
        inv = bn_gamma * lax.rsqrt(bn_var + BN_EPS)
        local = local * inv[None, :, None, None] + (bn_beta - bn_mean * inv)[None, :, None, None]
        local_flat = local.reshape(B, C, N).transpose(0, 2, 1)
        x_norm = _layernorm(x_flat, ln_gamma, ln_beta)
        qkv = x_norm @ qkv_w.T + qkv_b
        qkv = qkv.reshape(B, N, 3, nh, hd).transpose(2, 0, 3, 1, 4)
        q, k, v = (qkv[0], qkv[1], qkv[2])
        local_q = _layernorm(local_flat, ln_gamma, ln_beta).reshape(B, N, nh, hd).transpose(0, 2, 1, 3)
        q = q + local_q
        attn = jax.nn.softmax(jnp.einsum('bhnd,bhmd->bhnm', q, k) * scale, axis=-1)
        out = jnp.einsum('bhnm,bhmd->bhnd', attn, v)
        out = out.transpose(0, 2, 1, 3).reshape(B, N, C)
        out = out @ proj_w.T + proj_b
        out = x_flat + out
        return out.transpose(0, 2, 1).reshape(B, C, H, W)

    def _L1_conv_ref(x, dw_w, dw_b, ln_g, ln_b, w1, b1, grn_g, grn_b, w2, b2):
        import jax, jax.numpy as jnp
        import numpy as np
        C = 384
        H = 4 * C
        EPS_LN = 1e-06
        EPS_GRN = 1e-06
        residual = x
        y = jax.lax.conv_general_dilated(x, dw_w, window_strides=(1, 1), padding=[(3, 3), (3, 3)], dimension_numbers=('NCHW', 'OIHW', 'NCHW'), feature_group_count=C)
        y = y + dw_b[None, :, None, None]
        y = jnp.transpose(y, (0, 2, 3, 1))
        mu = jnp.mean(y, axis=-1, keepdims=True)
        var = jnp.mean(jnp.square(y - mu), axis=-1, keepdims=True)
        y = (y - mu) * jax.lax.rsqrt(var + EPS_LN) * ln_g + ln_b
        y = jnp.einsum('bhwc,cf->bhwf', y, w1) + b1
        y = jax.nn.gelu(y, approximate=False)
        gx = jnp.sqrt(jnp.sum(jnp.square(y), axis=(1, 2), keepdims=True))
        nx = gx / (jnp.mean(gx, axis=-1, keepdims=True) + EPS_GRN)
        y = grn_g * (y * nx) + grn_b + y
        y = jnp.einsum('bhwf,fc->bhwc', y, w2) + b2
        y = jnp.transpose(y, (0, 3, 1, 2))
        return residual + y

    def _gn(v, G=32, eps=1e-5):
        B_, C_, H_, W_ = v.shape
        g = v.reshape(B_, G, C_ // G, H_, W_)
        m = jnp.mean(g, axis=(2, 3, 4), keepdims=True)
        s = jnp.var(g, axis=(2, 3, 4), keepdims=True)
        return ((g - m) / jnp.sqrt(s + eps)).reshape(v.shape)

    def _ln_c(v, eps=1e-6):
        m = jnp.mean(v, axis=1, keepdims=True)
        s = jnp.var(v, axis=1, keepdims=True)
        return (v - m) / jnp.sqrt(s + eps)

    def _ln_t(v, eps=1e-5):
        m = jnp.mean(v, axis=-1, keepdims=True)
        s = jnp.var(v, axis=-1, keepdims=True)
        return (v - m) / jnp.sqrt(s + eps)

    def _to_tokens(v):
        B_, C_, H_, W_ = v.shape
        return v.reshape(B_, C_, H_ * W_).transpose(0, 2, 1)
    def _from_tokens(t, like):
        B_, C_, H_, W_ = like.shape
        return t.transpose(0, 2, 1).reshape(B_, C_, H_, W_)

    x = _L0_conv_ref(x, L0_conv_conv_w, L0_conv_bn_gamma, L0_conv_bn_beta, L0_conv_bn_mean, L0_conv_bn_var, L0_conv_ln_gamma, L0_conv_ln_beta, L0_conv_qkv_w, L0_conv_qkv_b, L0_conv_proj_w, L0_conv_proj_b)
    x = _L1_conv_ref(x, L1_conv_dw_w, L1_conv_dw_b, L1_conv_ln_g, L1_conv_ln_b, L1_conv_w1, L1_conv_b1, L1_conv_grn_g, L1_conv_grn_b, L1_conv_w2, L1_conv_b2)
    return x


_drawn_inputs = setup_inputs


def setup_inputs(seed=0):
    import zlib

    import numpy as np

    out = dict(_drawn_inputs(seed))
    spreads = {'L0_conv_bn_gamma': (1.0, 0.6),
     'L0_conv_bn_beta': (0.0, 0.8),
     'L0_conv_bn_mean': (0.0, 0.8),
     'L0_conv_bn_var': (1.0, 0.6),
     'L0_conv_ln_gamma': (1.0, 0.2),
     'L0_conv_ln_beta': (0.0, 0.1),
     'L0_conv_qkv_b': (0.0, 0.1),
     'L0_conv_proj_b': (0.0, 0.1),
     'L1_conv_dw_b': (0.0, 0.1),
     'L1_conv_ln_g': (1.0, 0.2),
     'L1_conv_ln_b': (0.0, 0.463),
     'L1_conv_b1': (0.0, 0.1),
     'L1_conv_grn_g': (0.0, 0.282),
     'L1_conv_grn_b': (0.0, 0.1),
     'L1_conv_b2': (0.0, 0.1)}
    factors = {}
    for name, (base, spread) in spreads.items():
        noise = np.random.default_rng([zlib.crc32(name.encode()), seed]).standard_normal(out[name].shape)
        drawn = base * np.exp(spread * noise) if base else spread * noise
        out[name] = jnp.asarray(drawn.astype(out[name].dtype))
    for name, factor in factors.items():
        out[name] = (out[name] * factor).astype(out[name].dtype)
    return out
```

```python
from contextlib import ExitStack

import numpy as np

import concourse.bass as bass
from concourse import mybir
from concourse.alu_op_type import AluOpType as ALU

F32 = mybir.dt.float32
F32R = mybir.dt.float32r
ACT = mybir.ActivationFunctionType
AX = mybir.AxisListType

B, C, H, W = 4, 384, 48, 48
N = H * W
P = 128
CT = C // P
HEADS, HD = 8, 48
CHUNK = 384
NCH = N // CHUNK
TT = 96
FH = 4 * C
FT = FH // P
QR = 4
GC = P // QR
NG = C // GC
HB = H // QR
KS = 7
NU = KS + 2 * QR - 3


def f32(ap):
    return ap.bitcast(F32)


def shared_consts(nc, ctx):
    ident = ctx.enter_context(nc.sbuf_tensor("ident", [P, P], F32))
    cmask = ctx.enter_context(nc.sbuf_tensor("cmask", [P, GC], F32))
    ones = ctx.enter_context(nc.sbuf_tensor("ones", [P, P], F32))
    made = ctx.enter_context(nc.semaphore("consts_made"))
    with nc.Block() as block:
        @block.gpsimd
        def _(pool):
            pool.memset(ident[:], 0.0).then_inc(made, 1)
            pool.memset(ones[:], 1.0).then_inc(made, 1)
            pool.wait_ge(made, 2)
            pool.affine_select(out=ident[:], in_=ident[:], compare_op=ALU.not_equal, fill=1.0, base=0,
                               pattern=[[-1, P]], channel_multiplier=1).then_inc(made, 1)
            pool.wait_ge(made, 3)
            pool.tensor_tensor(cmask[:], ident[:, 0:GC], ident[:, GC:2 * GC], ALU.add).then_inc(made, 1)
            for r in range(2, QR):
                pool.wait_ge(made, 2 + r)
                pool.tensor_tensor(cmask[:], cmask[:], ident[:, r * GC:(r + 1) * GC], ALU.add).then_inc(made, 1)
    return ident, cmask, ones


def segments(total, edges):
    cuts = sorted({0, total, *[e for e in edges if 0 < e < total]})
    return list(zip(cuts[:-1], cuts[1:]))


def conv_stage(nc, tag, ident, cmask, src, taps, affine, ln_g, ln_b, dst, nb=B):
    S = nb * NG
    LE = 2
    LN = NG + 2
    with ExitStack() as ctx:
        def sb(name, shape, dt=F32):
            return ctx.enter_context(nc.sbuf_tensor(f"{tag}_{name}", shape, dt))

        def psum(name, shape):
            return ctx.enter_context(nc.psum_tensor(f"{tag}_{name}", shape, F32))

        def sem(name):
            return ctx.enter_context(nc.semaphore(f"{tag}_{name}"))

        tap_raw = sb("tap_raw", [P, NG, NU, KS])
        tap_hi = sb("tap_hi", [P, NG, NU, KS], F32R)
        tap_lo = sb("tap_lo", [P, NG, NU, KS], F32R)
        band_hi = sb("band_hi", [P, 2, 3, KS, P], F32R)
        band_lo = sb("band_lo", [P, 2, 3, KS, P], F32R)
        x_raw = sb("x_raw", [P, 2, HB, W])
        x_hi = sb("x_hi", [P, 2, HB + 2, W + 6], F32R)
        x_lo = sb("x_lo", [P, 2, HB + 2, W + 6], F32R)
        par = sb("par", [P, 4, NG])
        scale = sb("scale", [P, NG])
        shift = sb("shift", [P, NG])
        tmp = sb("tmp", [P, 3, NG])
        local = sb("local", [P, 2, HB * W])
        tok = sb("tok", [TT, 2, 4 * NCH, C])
        gam = sb("gam", [TT, C])
        bet = sb("bet", [TT, C])
        st = sb("st", [TT, 2, 6])
        mv = sb("mv", [TT, 2, 2])
        sd = sb("sd", [TT, 2])
        rs = sb("rs", [TT, 2])
        idle = sb("idle", [TT, 1])
        eps = sb("eps", [P, 1])
        eps_bn = sb("eps_bn", [P, 1])
        cen = sb("cen", [TT, 2, C])
        nrm = sb("nrm", [TT, 2, 2, C])
        acc = psum("acc", [P, 4, 512])
        tps = psum("tps", [P, 2, 512])

        taps_in, par_in = sem("taps_in"), sem("par_in")
        zeroed, taps_hi, taps_lo = sem("zeroed"), sem("taps_hi"), sem("taps_lo")
        bn_sd, bn_dve = sem("bn_sd"), sem("bn_dve")
        x_in = sem("x_in")
        hi_made, lo_made, bands_made = sem("hi_made"), sem("lo_made"), sem("bands_made")
        conv_done, local_made, turned, tok_made = sem("conv_done"), sem("local_made"), sem("turned"), sem("tok_made")
        sd_made, dve_ln, nrm_made = sem("sd_made"), sem("dve_ln"), sem("nrm_made")
        stored = sem("stored")

        groups = src.rearrange("b (g c) (hb hi) w -> (b g) hi c hb w", c=GC, hi=QR)
        tap_src = taps.rearrange("(g c) one kh kw -> c g (one kh kw)", c=GC)
        tiles_out = dst.rearrange("b t p c -> (b t) p c")
        batch_norm = len(affine) == 4
        HALF = HB // 2 * W

        block = ctx.enter_context(nc.Block())

        @block.sync
        def _(sp):
            sp.wait_ge(zeroed, 1)
            for hi in range(QR):
                sp.dma_start(tap_raw[hi * GC:(hi + 1) * GC, :, hi + 1:hi + 1 + KS, :].rearrange("c g u d -> c g (u d)"),
                             tap_src).then_inc(taps_in, 16)
            for hi in range(QR):
                for k, v in enumerate(affine):
                    sp.dma_start(par[hi * GC:(hi + 1) * GC, k, :], v.rearrange("(g c) -> c g", c=GC),
                                 allow_slow_non_contiguous=True).then_inc(par_in, 16)
            sp.dma_start(gam[:], ln_g.partition_broadcast(TT)).then_inc(par_in, 16)
            sp.dma_start(bet[:], ln_b.partition_broadcast(TT)).then_inc(par_in, 16)
            for a, z in segments(S + LN + 1, [1, 2, S, LN + 1, LN + 2]):
                with sp.Fori(a, z) as it:
                    if a < S:
                        if a >= 2:
                            sp.wait_ge(lo_made, it - 1)
                        if a >= 1:
                            sp.wait_ge(x_in, it * 16 * QR)
                        for hi in range(QR):
                            sp.dma_start(x_raw[hi * GC:(hi + 1) * GC, it % 2, :, :],
                                         groups[it, hi]).then_inc(x_in, 16)
                    if a >= LN + 1:
                        s = it - (LN + 1)
                        if a >= LN + 2:
                            sp.wait_ge(stored, s * 16)
                        sp.wait_ge(nrm_made, s * 2 + 2)
                        sp.dma_start(tiles_out[bass.ds(s * 2, 2)].rearrange("t p c -> p t c"),
                                     nrm[:, s % 2]).then_inc(stored, 16)
            sp.wait_ge(stored, S * 16)

        @block.scalar
        def _(act):
            act.wait_ge(taps_in, 16 * QR)
            act.activation(tap_hi[:], tap_raw[:], ACT.Copy).then_inc(taps_hi, 1)
            act.wait_ge(zeroed, 4)
            act.wait_ge(par_in, 16 * (QR * len(affine) + 2))
            if batch_norm:
                act.activation(tmp[:, 0], par[:, 3], ACT.Sqrt, bias=eps_bn[:, 0:1]).then_inc(bn_sd, 1)
            act.wait_ge(bn_dve, 4 if batch_norm else 2)
            for a, z in segments(S + LN, [1, 2, 3, S, S + 1, LN]):
                with act.Fori(a, z) as it:
                    if a < S:
                        act.wait_ge(x_in, (it + 1) * 16 * QR)
                        if a >= 2:
                            act.wait_ge(conv_done, it - 1)
                        act.activation(x_hi[:, it % 2, 1:HB + 1, 3:3 + W], x_raw[:, it % 2], ACT.Copy).then_inc(hi_made, 1)
                    if 1 <= a < S + 1:
                        s = it - 1
                        act.wait_ge(conv_done, it)
                        if a >= 3:
                            act.wait_ge(turned, (it - 2) * 2)
                        for h in range(2):
                            act.activation(local[:, s % 2, h * HALF:(h + 1) * HALF],
                                           acc[:, bass.ds((s % 2) * 2 + h, 1), 0:HALF], ACT.Identity,
                                           scale=scale[:, bass.ds(s % NG, 1)],
                                           bias=shift[:, bass.ds(s % NG, 1)]).then_inc(local_made, 1)
                    if a >= LN:
                        s = it - LN
                        act.wait_ge(dve_ln, s * 7 + 4)
                        act.activation(sd[:], mv[:, :, 1], ACT.Sqrt, bias=eps[0:TT, 0:1]).then_inc(sd_made, 1)

        @block.vector
        def _(dve):
            dve.memset(tap_raw[:], 0.0).then_inc(zeroed, 1)
            dve.memset(eps[:], 1e-6).then_inc(zeroed, 1)
            dve.memset(eps_bn[:], 1e-5).then_inc(zeroed, 1)
            dve.memset(f32(x_hi[:]), 0.0)
            dve.memset(f32(x_lo[:]), 0.0).then_inc(zeroed, 1)
            dve.wait_ge(taps_hi, 1)
            dve.tensor_tensor(tap_lo[:], tap_raw[:], f32(tap_hi[:]), ALU.subtract).then_inc(taps_lo, 1)
            dve.wait_ge(par_in, 16 * (QR * len(affine) + 2))
            if batch_norm:
                dve.wait_ge(bn_sd, 1)
                dve.reciprocal(tmp[:, 1], tmp[:, 0]).then_inc(bn_dve, 1)
                dve.wait_ge(bn_dve, 1)
                dve.tensor_tensor(scale[:], par[:, 0], tmp[:, 1], ALU.mult).then_inc(bn_dve, 1)
                dve.wait_ge(bn_dve, 2)
                dve.tensor_tensor(tmp[:, 2], par[:, 2], scale[:], ALU.mult).then_inc(bn_dve, 1)
                dve.wait_ge(bn_dve, 3)
                dve.tensor_tensor(shift[:], par[:, 1], tmp[:, 2], ALU.subtract).then_inc(bn_dve, 1)
            else:
                dve.memset(scale[:], 1.0).then_inc(bn_dve, 1)
                dve.tensor_copy(shift[:], par[:, 0]).then_inc(bn_dve, 1)
            for a, z in segments(S + LN, [2, S, S + LE, LN, LN + 1, LN + 2]):
                with dve.Fori(a, z) as it:
                    if a < S:
                        dve.wait_ge(hi_made, it + 1)
                        if a >= 2:
                            dve.wait_ge(conv_done, it - 1)
                        dve.tensor_tensor(x_lo[:, it % 2, 1:HB + 1, 3:3 + W], x_raw[:, it % 2],
                                          f32(x_hi[:, it % 2, 1:HB + 1, 3:3 + W]), ALU.subtract).then_inc(lo_made, 1)
                    if a >= LN + 1:
                        dve.wait_ge(nrm_made, (it - LN) * 2)
                    if LE <= a < S + LE:
                        s = it - LE
                        for h in range(2):
                            dve.wait_ge(turned, s * 2 + h + 1)
                            dve.tensor_copy(
                                tok[:, (s // NG) % 2, 12 * h:12 * h + 12, bass.ds((s % NG) * GC, GC)],
                                tps[0:TT, h, 0:CHUNK].rearrange("p (t c) -> p t c", c=GC)).then_inc(tok_made, 1)
                    if a >= LN:
                        s = it - LN
                        slot = (s // NG) % 2
                        dve.wait_ge(tok_made, min(S, a - 1) * 2 if z - a == 1 or a >= S else (it - 1) * 2)
                        for t in range(2):
                            dve.bn_stats(st[:, t], tok[:, slot, bass.ds((s % NG) * 2 + t, 1), :]).then_inc(dve_ln, 1)
                        dve.wait_ge(dve_ln, s * 7 + 2)
                        dve.memset(idle[:], 0.0)
                        for t in range(2):
                            dve.bn_aggr(mv[:, t], st[:, t]).then_inc(dve_ln, 1)
                        dve.wait_ge(sd_made, s + 1)
                        dve.reciprocal(rs[:], sd[:]).then_inc(dve_ln, 1)
                        for t in range(2):
                            dve.scalar_tensor_tensor(out=cen[:, t], in0=tok[:, slot, bass.ds((s % NG) * 2 + t, 1), :],
                                                     scalar=mv[:, t, 0:1], in1=gam[:], op0=ALU.subtract,
                                                     op1=ALU.mult).then_inc(dve_ln, 1)
                        if a >= LN + 2:
                            dve.wait_ge(stored, (s - 1) * 16)
                        for t in range(2):
                            dve.wait_ge(dve_ln, s * 7 + 6 + t)
                            dve.scalar_tensor_tensor(out=nrm[:, s % 2, t], in0=cen[:, t], scalar=rs[:, t:t + 1],
                                                     in1=bet[:], op0=ALU.mult, op1=ALU.add).then_inc(nrm_made, 1)

        @block.gpsimd
        def _(pool):
            pool.wait_ge(taps_lo, 1)
            for a, z in segments(S, [2]):
                with pool.Fori(a, z) as it:
                    if a >= 2:
                        pool.wait_ge(conv_done, it - 1)
                    for band, tap in ((band_hi, tap_hi), (band_lo, tap_lo)):
                        for o in range(3):
                            u0 = 2 * QR - QR * o
                            taps_of = f32(tap[:, bass.ds(it % NG, 1), u0:u0 + QR, :]).rearrange("p one u d -> p (one d) u")
                            last = pool.tensor_tensor(
                                band[:, it % 2, o].rearrange("p d (u c) -> p d u c", c=GC),
                                taps_of.unsqueeze(3).to_broadcast([P, KS, QR, GC]),
                                cmask[:].unsqueeze(1).unsqueeze(1).to_broadcast([P, KS, QR, GC]), ALU.mult)
                    last.then_inc(bands_made, 1)

        @block.tensor
        def _(pe):
            def conv(s, k, wait_acc=True):
                pe.wait_ge(bands_made, s + 1)
                pe.wait_ge(lo_made, s + 1)
                if wait_acc:
                    pe.wait_ge(local_made, (s - 1) * 2)
                for o in range(3):
                    for d in range(KS):
                        first, end = o == 0 and d == 0, o == 2 and d == KS - 1
                        for band, xs in ((band_hi, (x_hi, x_lo)), (band_lo, (x_hi,))):
                            for h in range(2):
                                for x in xs:
                                    r0 = h * HB // 2 + o
                                    last = pe.matmul(acc[:, 2 * k + h, 0:HALF], band[:, k, o, d, :],
                                                     x[:, k, r0:r0 + HB // 2, d:d + W],
                                                     start=first and band is band_hi and x is x_hi,
                                                     stop=end and band is band_lo)
                last.then_inc(conv_done, 1)

            def turn(s, k, wait_tok=True):
                for h in range(2):
                    pe.wait_ge(local_made, s * 2 + h + 1)
                    if wait_tok:
                        pe.wait_ge(tok_made, s * 2 - 1 + h)
                    for t in range(3):
                        last = pe.transpose(tps[0:TT, h, t * P:(t + 1) * P],
                                            local[:, k, h * HALF + t * TT:h * HALF + (t + 1) * TT], ident[:])
                    last.then_inc(turned, 1)

            conv(0, 0, False)
            conv(1, 1, False)
            turn(0, 0, False)
            with pe.Fori(1, S // 2) as i:
                conv(i * 2, 0)
                turn(i * 2 - 1, 1)
                conv(i * 2 + 1, 1)
                turn(i * 2, 0)
            turn(S - 1, 1)


def at_least(eng, sem, count):
    if not isinstance(count, int) or count > 0:
        eng.wait_ge(sem, count)


def split_stage(nc, tag, items):
    with ExitStack() as ctx:
        def sb(name, shape, dt=F32):
            return ctx.enter_context(nc.sbuf_tensor(f"{tag}_{name}", shape, dt))

        def sem(name):
            return ctx.enter_context(nc.semaphore(f"{tag}_{name}"))

        loaded = [sem(f"loaded{n}") for n in range(len(items))]
        hi_made, lo_made, stored = sem("hi_made"), sem("lo_made"), sem("stored")
        raw = [sb(f"raw{n}", [P, it[0].shape[1]]) for n, it in enumerate(items)]
        hi = [sb(f"hi{n}", [P, it[0].shape[1]], F32R) for n, it in enumerate(items)]
        lo = [sb(f"lo{n}", [P, it[0].shape[1]], F32R) for n, it in enumerate(items)]
        block = ctx.enter_context(nc.Block())

        @block.sync
        def _(sp):
            for n, (src, _h, _l) in enumerate(items):
                sp.dma_start(raw[n][:], src).then_inc(loaded[n], 16)
            for n, (_s, hi_out, lo_out) in enumerate(items):
                sp.wait_ge(hi_made, n + 1)
                sp.dma_start(hi_out, f32(hi[n][:])).then_inc(stored, 16)
                sp.wait_ge(lo_made, n + 1)
                sp.dma_start(lo_out, f32(lo[n][:])).then_inc(stored, 16)
            sp.wait_ge(stored, 32 * len(items))

        @block.scalar
        def _(act):
            for n in range(len(items)):
                act.wait_ge(loaded[n], 16)
                act.activation(hi[n][:], raw[n][:], ACT.Copy).then_inc(hi_made, 1)

        @block.vector
        def _(dve):
            for n in range(len(items)):
                dve.wait_ge(hi_made, n + 1)
                dve.tensor_tensor(lo[n][:], raw[n][:], f32(hi[n][:]), ALU.subtract).then_inc(lo_made, 1)


def norm_stage(nc, ident, x, ln_g, ln_b, x_hi_out, x_lo_out, nb=B):
    S = nb * NCH
    NT = CHUNK // TT
    with ExitStack() as ctx:
        def sb(name, shape, dt=F32):
            return ctx.enter_context(nc.sbuf_tensor(f"n_{name}", shape, dt))

        def psum(name, shape):
            return ctx.enter_context(nc.psum_tensor(f"n_{name}", shape, F32))

        def sem(name):
            return ctx.enter_context(nc.semaphore(f"n_{name}"))

        xc = sb("xc", [P, 2, CT, CHUNK])
        st = sb("st", [TT, NT, 6])
        mv = sb("mv", [TT, NT, 2])
        sd = sb("sd", [TT, NT])
        rs = sb("rs", [TT, NT])
        nrm = sb("nrm", [TT, 2, NT, C])
        full = sb("full", [P, 2, CT, CHUNK])
        hi = sb("hi", [P, 2, CT, CHUNK], F32R)
        lo = sb("lo", [P, 2, CT, CHUNK], F32R)
        gam = sb("gam", [P, CT])
        bet = sb("bet", [P, CT])
        eps = sb("eps", [P, 1])
        idle = sb("idle", [P, 1])
        ps_tok = psum("ps_tok", [P, NT, 512])
        ps_ch = psum("ps_ch", [P, CT, 512])
        x_in, par_in, eps_made = sem("x_in"), sem("par_in"), sem("eps_made")
        to_tok, to_ch, stats, sd_made, rs_made = sem("to_tok"), sem("to_ch"), sem("stats"), sem("sd_made"), sem("rs_made")
        normed, full_made, hi_made, lo_made, stored = (sem("normed"), sem("full_made"), sem("hi_made"), sem("lo_made"),
                                                       sem("stored"))
        xs = x.rearrange("b (t p) n -> b p t n", p=P)
        his = x_hi_out.rearrange("b (t p) n -> b p t n", p=P)
        los = x_lo_out.rearrange("b (t p) n -> b p t n", p=P)
        block = ctx.enter_context(nc.Block())

        @block.sync
        def _(sp):
            sp.dma_start(gam[:], ln_g.rearrange("(t p) -> p t", p=P), allow_slow_non_contiguous=True).then_inc(par_in, 16)
            sp.dma_start(bet[:], ln_b.rearrange("(t p) -> p t", p=P), allow_slow_non_contiguous=True).then_inc(par_in, 16)
            for a, z in segments(S + 3, [1, 2, 3, 4, S]):
                with sp.Fori(a, z) as it:
                    if a < S:
                        if a >= 1:
                            sp.wait_ge(x_in, it * 16)
                        if a >= 2:
                            sp.wait_ge(to_tok, (it - 1) * NT)
                        sp.dma_start(xc[:, it % 2], xs[it // NCH, :, :, bass.ds((it % NCH) * CHUNK, CHUNK)]).then_inc(x_in, 16)
                    if a >= 3:
                        s = it - 3
                        if a >= 4:
                            sp.wait_ge(stored, s * 32)
                        sp.wait_ge(lo_made, s * CT + CT)
                        for part, out in ((hi, his), (lo, los)):
                            sp.dma_start(out[s // NCH, :, :, bass.ds((s % NCH) * CHUNK, CHUNK)],
                                         f32(part[:, s % 2])).then_inc(stored, 16)
            sp.wait_ge(stored, S * 32)

        @block.vector
        def _(dve):
            dve.memset(eps[:], 1e-6).then_inc(eps_made, 1)
            for a, z in segments(S, [1, 2]):
                with dve.Fori(a, z) as it:
                    for t in range(NT):
                        dve.wait_ge(to_tok, it * NT + t + 1)
                        dve.bn_stats(st[:, t], ps_tok[0:TT, t, 0:C]).then_inc(stats, 1)
                    dve.wait_ge(stats, it * 2 * NT + NT)
                    dve.memset(idle[:], 0.0)
                    for t in range(NT):
                        dve.bn_aggr(mv[:, t], st[:, t]).then_inc(stats, 1)
                    dve.wait_ge(sd_made, it + 1)
                    dve.reciprocal(rs[:], sd[:]).then_inc(rs_made, 1)
                    if a >= 2:
                        dve.wait_ge(to_ch, (it - 1) * CT)
                    dve.wait_ge(rs_made, it + 1)
                    for t in range(NT):
                        dve.tensor_scalar(nrm[:, it % 2, t], ps_tok[0:TT, t, 0:C], mv[:, t, 0:1], rs[:, t:t + 1],
                                          ALU.subtract, ALU.mult).then_inc(normed, 1)

        @block.scalar
        def _(act):
            act.wait_ge(eps_made, 1)
            act.wait_ge(par_in, 32)
            for a, z in segments(S + 1, [1, 3, S]):
                with act.Fori(a, z) as it:
                    if a < S:
                        act.wait_ge(stats, it * 2 * NT + 2 * NT)
                        act.activation(sd[:], mv[:, :, 1], ACT.Sqrt, bias=eps[0:TT, 0:1]).then_inc(sd_made, 1)
                    if a >= 1:
                        s = it - 1
                        if a >= 3:
                            act.wait_ge(lo_made, (s - 1) * CT)
                            act.wait_ge(stored, (s - 1) * 32)
                        for t in range(CT):
                            act.wait_ge(to_ch, s * CT + t + 1)
                            act.activation(full[:, s % 2, t], ps_ch[:, t, 0:CHUNK], ACT.Identity,
                                           scale=gam[:, t:t + 1], bias=bet[:, t:t + 1]).then_inc(full_made, 1)
                        for t in range(CT):
                            act.wait_ge(full_made, s * CT + t + 1)
                            act.activation(hi[:, s % 2, t], full[:, s % 2, t], ACT.Copy).then_inc(hi_made, 1)

        @block.gpsimd
        def _(pool):
            for a, z in segments(S, [2]):
                with pool.Fori(a, z) as it:
                    if a >= 2:
                        pool.wait_ge(stored, (it - 1) * 32)
                    for t in range(CT):
                        pool.wait_ge(hi_made, it * CT + t + 1)
                        pool.tensor_tensor(lo[:, it % 2, t], full[:, it % 2, t], f32(hi[:, it % 2, t]),
                                           ALU.subtract).then_inc(lo_made, 1)

        @block.tensor
        def _(pe):
            def tokens(s, k):
                pe.wait_ge(x_in, (s + 1) * 16)
                at_least(pe, normed, s * NT)
                for t in range(NT):
                    for c in range(CT):
                        last = pe.transpose(ps_tok[0:TT, t, c * P:(c + 1) * P], xc[:, k, c, t * TT:(t + 1) * TT], ident[:])
                    last.then_inc(to_tok, 1)

            def channels(s, k):
                pe.wait_ge(normed, (s + 1) * NT)
                at_least(pe, full_made, s * CT)
                for c in range(CT):
                    for t in range(NT):
                        last = pe.transpose(ps_ch[:, c, t * TT:(t + 1) * TT], nrm[:, k, t, c * P:(c + 1) * P],
                                            ident[0:TT, 0:TT])
                    last.then_inc(to_ch, 1)

            tokens(0, 0)
            tokens(1, 1)
            channels(0, 0)
            with pe.Fori(1, S // 2) as i:
                tokens(i * 2, 0)
                channels(i * 2 - 1, 1)
                tokens(i * 2 + 1, 1)
                channels(i * 2, 0)
            channels(S - 1, 1)


def attend_stage(nc, ident, x_hi_in, x_lo_in, w_hi_in, w_lo_in, qb, kb, local, out, nb=B):
    NHEAD = nb * HEADS
    KT = N // P
    PAIRS = KT // 2
    STEPS = NCH * PAIRS
    LAG = 3
    QT = N // P
    PIECES = [(k * 512, min(512, N - k * 512)) for k in range((N + 511) // 512)]
    NMX = QT * len(PIECES)
    ROW = 2 * HD
    VT = 2 * CHUNK // P
    JOBS = [("k", c, c) for c in range(NCH)] + [("q", 0, 6), ("q", 1, 9), ("v", 0, 11), ("q", 2, 14), ("q", 3, 19),
                                               ("v", 1, 22), ("q", 4, 25), ("q", 5, 31), ("v", 2, 35)]
    NJ = len(JOBS)
    Q_JOB = {i: n for n, (kind, i, _s) in enumerate(JOBS) if kind == "q"}
    JOBS_AT = {s: n for n, (_k, _i, s) in enumerate(JOBS)}
    MAX_AT = {8 + (t * 40) // (QT - 1): t for t in range(QT)}
    FIN_AT = 49
    COMB_AT = {PAIRS * c + PAIRS - 1 + LAG + 2: c for c in range(NCH)}
    POOL_SUBS = [n for n in range(STEPS) if n >= 10 and n % 4 == 2]
    ON_POOL = {n: i for i, n in enumerate(POOL_SUBS)}
    DVE_SUBS = [n for n in range(STEPS) if n not in ON_POOL]
    ON_DVE = {n: i for i, n in enumerate(DVE_SUBS)}
    NP_, ND_ = len(POOL_SUBS), len(DVE_SUBS)

    with ExitStack() as ctx:
        def sb(name, shape, dt=F32):
            return ctx.enter_context(nc.sbuf_tensor(f"a_{name}", shape, dt))

        def psum(name, shape):
            return ctx.enter_context(nc.psum_tensor(f"a_{name}", shape, F32))

        def sem(name):
            return ctx.enter_context(nc.semaphore(f"a_{name}"))

        x_hi = sb("x_hi", [P, CT, N], F32R)
        x_lo = sb("x_lo", [P, CT, N], F32R)
        w = sb("w", [P, 2, 2, CT, 5 * HD], F32R)
        q = sb("q", [P, 2, N], F32R)
        k_hi = sb("k_hi", [P, 2, N], F32R)
        k_lo = sb("k_lo", [P, 2, N], F32R)
        v = sb("v", [P, 2, KT, ROW + 2], F32R)
        loc = sb("loc", [TT, 2, 4 * NCH, 2, HD])
        q_hi = sb("q_hi", [ROW, 2, CHUNK])
        e_full = sb("e_full", [P, 3, 2, CHUNK])
        e_hi = sb("e_hi", [P, 3, 2, CHUNK], F32R)
        e_lo = sb("e_lo", [P, 3, 2, CHUNK], F32R)
        o_t = sb("o_t", [ROW + 1, 2, CHUNK])
        r_sum = sb("r_sum", [P, 2, 3])
        o_tok = sb("o_tok", [P, 2, 3, HD])
        mx_part = sb("mx_part", [P, 2, QT, len(PIECES)])
        mx = sb("mx", [P, 2, QT])
        mx_row = sb("mx_row", [QT, P])
        low = sb("low", [ROW, 1])
        bias_all = sb("bias_all", [ROW, HEADS, 3])
        bias = sb("bias", [ROW, 2, 3])
        comb = sb("comb", [ROW + 1, HD + 1])

        ps_s = psum("ps_s", [P, 2, 2, 512])
        ps_o = psum("ps_o", [P, 512])
        ps_m = psum("ps_m", [P, 2, 512])
        ps_x = psum("ps_x", [P, 512])

        x_in = [sem(f"x_in{c}") for c in range(NCH)]
        head_in, bias_in, bias_taken = sem("head_in"), sem("bias_in"), sem("bias_taken")
        made_pool, made_dve, made_act = sem("made_pool"), sem("made_dve"), sem("made_act")
        proj_done, proj_hi, proj_lo = sem("proj_done"), sem("proj_hi"), sem("proj_lo")
        mx_done, mx_red, mx_fin = sem("mx_done"), sem("mx_red"), sem("mx_fin")
        row_turned, row_out, row_in = sem("row_turned"), sem("row_out"), sem("row_in")
        s_done, e_made, e_hi_made = sem("s_done"), sem("e_made"), sem("e_hi_made")
        lo_dve, lo_pool = sem("lo_dve"), sem("lo_pool")
        o_done, o_out, comb_done, r_made, o_made, stored = (sem("o_done"), sem("o_out"), sem("comb_done"),
                                                            sem("r_made"), sem("o_made"), sem("stored"))

        x_parts = [(x_hi, x_hi_in.rearrange("b (t p) n -> b p t n", p=P)),
                   (x_lo, x_lo_in.rearrange("b (t p) n -> b p t n", p=P))]
        loc_in = local.rearrange("b t p (h d) -> b h p t d", d=HD)
        out_v = out.rearrange("b (c t p) (h d) -> b h c p t d", p=P, t=3, d=HD)

        def wait_lo(eng, h, n, less=0):
            if n in ON_POOL:
                at_least(eng, lo_pool, h * NP_ + ON_POOL[n] + 1)
            else:
                at_least(eng, lo_dve, h * ND_ + ON_DVE[n] + 1)

        def back(h, n, d):
            return (h, n - d) if n >= d else (h - 1, n - d + STEPS)

        def bodies(body, eng):
            body(-1, 1, main=False, prev=False, nxt=True)
            body(0, 0, main=True, prev=False, nxt=True)
            if NHEAD > 2:
                with eng.Fori(0, (NHEAD - 2) // 2) as i:
                    body(i * 2 + 1, 1, main=True, prev=True, nxt=True)
                    body(i * 2 + 2, 0, main=True, prev=True, nxt=True)
            body(NHEAD - 1, 1, main=True, prev=True, nxt=False)
            body(NHEAD, 0, main=False, prev=True, nxt=False)

        block = ctx.enter_context(nc.Block())

        @block.sync
        def _(sp):
            def load_head(h):
                for part, src in ((0, w_hi_in), (1, w_lo_in)):
                    sp.dma_start(f32(w[:, h % 2, part]), src[h % HEADS]).then_inc(head_in, 16)
                for twice in range(2):
                    sp.dma_start(loc[:, h % 2, :, twice], loc_in[h // HEADS, h % HEADS]).then_inc(head_in, 16)

            def load_chunk(b, c):
                for part, src in x_parts:
                    sp.dma_start(f32(part[:, :, c * CHUNK:(c + 1) * CHUNK]),
                                 src[b, :, :, c * CHUNK:(c + 1) * CHUNK]).then_inc(x_in[c], 16)

            for col, src in ((0, qb), (2, kb)):
                for half in range(2):
                    sp.dma_start(bias_all[half * HD:(half + 1) * HD, :, col:col + 1],
                                 src.rearrange("(h d one) -> d h one", d=HD, one=1),
                                 allow_slow_non_contiguous=True).then_inc(bias_in, 16)
            load_head(0)
            for c in range(NCH):
                load_chunk(0, c)
            sp.wait_ge(head_in, 64)
            load_head(1)

            def next_head(h):
                sp.wait_ge(head_in, (h + 2) * 64)
                sp.wait_ge(proj_done, (h + 1) * NJ)
                load_head(h + 2)

            def next_image(b):
                last = (b + 1) * HEADS - 1
                for c in range(NCH):
                    used = max(n for n, (kind, i, _s) in enumerate(JOBS)
                               if i == (c // 2 if kind == "v" else c))
                    sp.wait_ge(proj_done, last * NJ + used + 1)
                    load_chunk(b + 1, c)

            if nb > 1:
                with sp.Fori(0, nb - 1) as b:
                    with sp.Fori(0, HEADS - 1) as h:
                        next_head(b * HEADS + h)
                    next_image(b)
                    next_head(b * HEADS + HEADS - 1)
            with sp.Fori((nb - 1) * HEADS, NHEAD - 2) as h:
                next_head(h)

        @block.gpsimd
        def _(pool):
            pool.memset(comb[:], 0.0).then_inc(made_pool, 1)
            pool.memset(low[:], 1.0).then_inc(made_pool, 1)
            pool.wait_ge(made_pool, 2)
            pool.affine_select(out=low[:], in_=low[:], compare_op=ALU.is_ge, fill=0.0, base=-HD, pattern=[[0, 1]],
                               channel_multiplier=1).then_inc(made_pool, 1)
            pool.affine_select(out=comb[:, 0:HD], in_=comb[:, 0:HD], compare_op=ALU.not_equal, fill=1.0, base=0,
                               pattern=[[-1, HD]], channel_multiplier=1).then_inc(made_pool, 1)
            pool.wait_ge(made_pool, 4)
            pool.affine_select(out=comb[:], in_=comb[:], compare_op=ALU.not_equal, fill=1.0, base=-HD,
                               pattern=[[-1, HD + 1]], channel_multiplier=1).then_inc(made_pool, 1)

            def body(h, par, main, prev, nxt):
                if not main:
                    return
                for n in POOL_SUBS:
                    pool.wait_ge(e_hi_made, h * STEPS + n + 1)
                    at_least(pool, o_done, h * STEPS + n - 2)
                    pool.tensor_tensor(e_lo[:, n % 3], e_full[:, n % 3], f32(e_hi[:, n % 3]),
                                       ALU.subtract).then_inc(lo_pool, 1)

            bodies(body, pool)

        @block.scalar
        def _(act):
            act.wait_ge(bias_in, 64)
            act.wait_ge(made_pool, 5)
            act.activation(bias_all[:, :, 1], bias_all[:, :, 0], ACT.Copy, scale=low[:, 0:1]).then_inc(made_act, 1)
            act.wait_ge(made_act, 1)
            act.wait_ge(made_dve, 4)

            def project(h, par, n):
                kind, i, _s = JOBS[n]
                cols = slice(i * CHUNK, (i + 1) * CHUNK)
                act.wait_ge(proj_done, h * NJ + n + 1)
                if n == 0:
                    act.wait_ge(bias_taken, h + 1)
                    at_least(act, s_done, (h - 1) * STEPS)
                if kind == "k":
                    act.activation(k_hi[0:ROW, par, cols], ps_x[0:ROW, 0:CHUNK], ACT.Identity,
                                   bias=bias[:, par, 2:3]).then_inc(proj_hi, 1)
                if kind == "q":
                    at_least(act, proj_lo, h * NJ + n - 1)
                    act.activation(q_hi[:, i % 2].bitcast(F32R), ps_x[0:ROW, 0:CHUNK], ACT.Identity,
                                   scale=low[:, 0:1], bias=bias[:, par, 1:2]).then_inc(proj_hi, 1)
                if kind == "v":
                    at_least(act, o_done, (h - 1) * STEPS)
                    act.activation(v[:, par, i * VT:(i + 1) * VT, 0:HD],
                                   ps_x[:, 0:VT * HD].rearrange("p (t d) -> p t d", d=HD), ACT.Copy).then_inc(proj_hi, 1)

            def hi_of(h, n):
                act.wait_ge(e_made, h * STEPS + n + 1)
                at_least(act, o_done, h * STEPS + n - 2)
                act.activation(e_hi[:, n % 3], e_full[:, n % 3], ACT.Copy).then_inc(e_hi_made, 1)

            def take_out(h, c):
                act.wait_ge(o_done, h * STEPS + PAIRS * (c + 1))
                at_least(act, comb_done, h * NCH + c - 1)
                act.activation(o_t[:, c % 2], ps_o[0:ROW + 1, 0:CHUNK], ACT.Copy).then_inc(o_out, 1)

            def store(h, c):
                act.wait_ge(o_made, h * NCH + c + 1)
                at_least(act, stored, (h * NCH + c) * 16)
                act.dma_start(out_v[h // HEADS, h % HEADS, c], o_tok[:, c % 2]).then_inc(stored, 16)

            def body(h, par, main, prev, nxt):
                for n in range(STEPS):
                    c, r = divmod(n - LAG - 1, PAIRS)
                    if main and n >= LAG + PAIRS and r == PAIRS - 1:
                        take_out(h, c)
                    if prev and n == LAG:
                        take_out(h - 1, NCH - 1)
                    if main:
                        act.wait_ge(s_done, h * STEPS + n + 1)
                        at_least(act, e_hi_made, h * STEPS + n - 2)
                        p_h, p_n = back(h, n, 3)
                        if prev or n >= 3:
                            wait_lo(act, p_h, p_n)
                        act.activation(e_full[:, n % 3], ps_s[:, n % 2, :, 0:CHUNK], ACT.Exp,
                                       scale=float(HD) ** -0.5).then_inc(e_made, 1)
                        if n >= 1:
                            hi_of(h, n - 1)
                    if n == 0 and prev:
                        hi_of(h - 1, STEPS - 1)
                    if nxt and n == 0:
                        act.activation(bias[:, 1 - par], bias_all[:, bass.ds((h + 1) % HEADS, 1), :].rearrange("p o c -> p (o c)"),
                                       ACT.Copy).then_inc(bias_taken, 1)
                    if nxt and n in JOBS_AT:
                        project(h + 1, 1 - par, JOBS_AT[n])
                    if nxt and n == FIN_AT:
                        act.wait_ge(row_turned, h + 2)
                        at_least(act, row_in, (h + 1) * 16)
                        act.activation(mx_row[:].bitcast(F32R), ps_x[0:QT, 0:P], ACT.Copy, scale=-1.0).then_inc(row_out, 1)
                        act.wait_ge(row_out, h + 2)
                        act.dma_start(f32(q[ROW:ROW + 1, 1 - par, :]).rearrange("o (t p) -> o t p", p=P),
                                      mx_row[:]).then_inc(row_in, 16)
                    if main and n - 4 in COMB_AT:
                        store(h, COMB_AT[n - 4])
                    if prev and n - 4 + STEPS in COMB_AT:
                        store(h - 1, COMB_AT[n - 4 + STEPS])

            bodies(body, act)
            act.wait_ge(stored, NHEAD * NCH * 16)

        @block.vector
        def _(dve):
            dve.memset(f32(k_hi[ROW:ROW + 1]), 1.0).then_inc(made_dve, 1)
            dve.memset(f32(k_lo[ROW:ROW + 1]), 0.0).then_inc(made_dve, 1)
            dve.memset(f32(v[:, :, :, ROW:ROW + 1]), 1.0).then_inc(made_dve, 1)
            dve.memset(f32(q[ROW:ROW + 1]), 0.0).then_inc(made_dve, 1)
            dve.wait_ge(bias_in, 64)

            def project(h, par, n):
                kind, i, _s = JOBS[n]
                cols = slice(i * CHUNK, (i + 1) * CHUNK)
                dve.wait_ge(proj_hi, h * NJ + n + 1)
                if n == 0:
                    dve.wait_ge(bias_taken, h + 1)
                if kind == "k":
                    dve.scalar_tensor_tensor(out=k_lo[0:ROW, par, cols], in0=ps_x[0:ROW, 0:CHUNK],
                                             scalar=bias[:, par, 2:3],
                                             in1=f32(k_hi[0:ROW, par, cols]), op0=ALU.add,
                                             op1=ALU.subtract).then_inc(proj_lo, 1)
                if kind == "q":
                    dve.scalar_tensor_tensor(out=q[0:ROW, par, cols], in0=ps_x[0:ROW, 0:CHUNK],
                                             scalar=bias[:, par, 0:1], in1=q_hi[:, i % 2],
                                             op0=ALU.add, op1=ALU.subtract).then_inc(proj_lo, 1)
                if kind == "v":
                    tiles = slice(i * VT, (i + 1) * VT)
                    dve.tensor_tensor(v[:, par, tiles, HD:ROW], ps_x[:, 0:VT * HD].rearrange("p (t d) -> p t d", d=HD),
                                      f32(v[:, par, tiles, 0:HD]), ALU.subtract).then_inc(proj_lo, 1)

            def lo_of(h, n):
                dve.wait_ge(e_hi_made, h * STEPS + n + 1)
                at_least(dve, o_done, h * STEPS + n - 2)
                dve.tensor_tensor(e_lo[:, n % 3], e_full[:, n % 3], f32(e_hi[:, n % 3]), ALU.subtract).then_inc(lo_dve, 1)

            def maxima(h, par, t):
                if t == 0:
                    at_least(dve, mx_fin, h - 1)
                for k in range(len(PIECES)):
                    m = t * len(PIECES) + k
                    dve.wait_ge(mx_done, h * NMX + m + 1)
                    dve.tensor_reduce(mx_part[:, par, t, k:k + 1], ps_m[:, m % 2, 0:PIECES[k][1]], AX.X,
                                      ALU.max).then_inc(mx_red, 1)

            def normalise(h, c):
                dve.wait_ge(comb_done, h * NCH + c + 1)
                at_least(dve, o_made, h * NCH + c - 1)
                sums = ps_x[:, 0:3 * (HD + 1)].rearrange("p (t d) -> p t d", d=HD + 1)
                dve.reciprocal(r_sum[:, c % 2, :].unsqueeze(2), sums[:, :, HD:HD + 1]).then_inc(r_made, 1)
                dve.wait_ge(r_made, h * NCH + c + 1)
                at_least(dve, stored, (h * NCH + c - 1) * 16)
                dve.tensor_tensor(o_tok[:, c % 2], sums[:, :, 0:HD],
                                  r_sum[:, c % 2, :].unsqueeze(2).to_broadcast([P, 3, HD]), ALU.mult).then_inc(o_made, 1)

            def body(h, par, main, prev, nxt):
                for n in range(STEPS):
                    if prev and n < 2:
                        l_n = n - 2 + STEPS
                        if l_n in ON_DVE:
                            lo_of(h - 1, l_n)
                    if main and n >= 2 and n - 2 in ON_DVE:
                        lo_of(h, n - 2)
                    if nxt and n in JOBS_AT:
                        project(h + 1, 1 - par, JOBS_AT[n])
                    if main and n in COMB_AT:
                        normalise(h, COMB_AT[n])
                    if prev and n + STEPS in COMB_AT:
                        normalise(h - 1, COMB_AT[n + STEPS])
                    if nxt and n in MAX_AT:
                        maxima(h + 1, 1 - par, MAX_AT[n])
                    if nxt and n == FIN_AT:
                        dve.wait_ge(mx_red, (h + 2) * NMX)
                        at_least(dve, row_turned, h)
                        dve.tensor_reduce(mx[:, 1 - par], mx_part[:, 1 - par], AX.X, ALU.max).then_inc(mx_fin, 1)

            bodies(body, dve)

        @block.tensor
        def _(pe):
            pe.wait_ge(made_pool, 5)
            pe.wait_ge(made_dve, 4)
            free = [None]

            def take_ps_x(sem_, count):
                if free[0] is not None:
                    at_least(pe, *free[0])
                free[0] = (sem_, count)

            def project(h, par, n):
                kind, i, _s = JOBS[n]
                take_ps_x(proj_lo, h * NJ + n + 1)
                if n == 0:
                    pe.wait_ge(head_in, (h + 1) * 64)
                for c in ([i] if kind != "v" else [2 * i, 2 * i + 1]):
                    pe.wait_ge(x_in[c], (h // HEADS + 1) * 32)
                parts = ((0, x_hi), (0, x_lo), (1, x_hi))
                if kind == "v":
                    for t in range(VT):
                        tok = slice((i * VT + t) * P, (i * VT + t + 1) * P)
                        for j, (wp, xp) in enumerate(parts):
                            for c in range(CT):
                                last = pe.matmul(ps_x[:, t * HD:(t + 1) * HD], xp[:, c, tok], w[:, par, wp, c, 4 * HD:],
                                                 start=j == 0 and c == 0, stop=j == 2 and c == CT - 1)
                else:
                    off = 0 if kind == "q" else ROW
                    cols = slice(i * CHUNK, (i + 1) * CHUNK)
                    for j, (wp, xp) in enumerate(parts):
                        for c in range(CT):
                            last = pe.matmul(ps_x[0:ROW, 0:CHUNK], w[:, par, wp, c, off:off + ROW], xp[:, c, cols], start=j == 0 and c == 0,
                                             stop=kind == "k" and j == 2 and c == CT - 1)
                    if kind == "q":
                        for t in range(4):
                            dst = ps_x[0:ROW, 0:CHUNK].rearrange("p (two r w) -> p r two w", two=2, w=W)[:, t]
                            last = pe.matmul(dst, loc[:, par, i * 4 + t].rearrange("p two d -> p (two d)"),
                                             ident[0:TT, 0:TT].rearrange("p (two w) -> p two w", w=W),
                                             start=False, stop=t == 3)
                last.then_inc(proj_done, 1)

            def maxima(h, par, t):
                for k, (k0, kn) in enumerate(PIECES):
                    m = t * len(PIECES) + k
                    if k == 0:
                        pe.wait_ge(proj_lo, h * NJ + Q_JOB[t // 3] + 1)
                    at_least(pe, mx_red, h * NMX + m - 1)
                    pe.matmul(ps_m[:, m % 2, 0:kn], q[0:ROW, par, t * P:(t + 1) * P], k_hi[0:ROW, par, k0:k0 + kn],
                              start=True, stop=True).then_inc(mx_done, 1)

            def scores(h, par, n):
                c, r = divmod(n, PAIRS)
                if n == 0:
                    pe.wait_ge(proj_lo, (h + 1) * NJ)
                    pe.wait_ge(row_in, (h + 1) * 16)
                at_least(pe, e_made, h * STEPS + n - 1)
                for t in range(2):
                    for part in (k_hi, k_lo):
                        last = pe.matmul(ps_s[:, n % 2, t, 0:CHUNK],
                                         part[0:ROW + 1, par, (2 * r + t) * P:(2 * r + t + 1) * P],
                                         q[0:ROW + 1, par, c * CHUNK:(c + 1) * CHUNK],
                                         start=part is k_hi, stop=part is k_lo)
                last.then_inc(s_done, 1)

            def products(h, par, n):
                c, r = divmod(n, PAIRS)
                if r == 0:
                    at_least(pe, o_out, h * NCH + c)
                pe.wait_ge(e_hi_made, h * STEPS + n + 1)
                wait_lo(pe, h, n)
                for j, part in enumerate((e_hi, e_lo)):
                    for t in range(2):
                        last = pe.matmul(ps_o[0:ROW + 1, 0:CHUNK], v[:, par, 2 * r + t, 0:ROW + 1], part[:, n % 3, t],
                                         start=r == 0 and j == 0 and t == 0, stop=r == PAIRS - 1 and j == 1 and t == 1)
                last.then_inc(o_done, 1)

            def combine(h, c):
                take_ps_x(o_made, h * NCH + c + 1)
                pe.wait_ge(o_out, h * NCH + c + 1)
                for t in range(3):
                    last = pe.matmul(ps_x[:, t * (HD + 1):(t + 1) * (HD + 1)], o_t[:, c % 2, t * P:(t + 1) * P],
                                     comb[:], start=True, stop=True)
                last.then_inc(comb_done, 1)

            def body(h, par, main, prev, nxt):
                for n in range(STEPS):
                    if main:
                        scores(h, par, n)
                    if nxt and n in JOBS_AT:
                        project(h + 1, 1 - par, JOBS_AT[n])
                    if main and n in COMB_AT:
                        combine(h, COMB_AT[n])
                    if prev and n + STEPS in COMB_AT:
                        combine(h - 1, COMB_AT[n + STEPS])
                    if nxt and n in MAX_AT:
                        maxima(h + 1, 1 - par, MAX_AT[n])
                    if nxt and n == FIN_AT:
                        take_ps_x(row_out, h + 2)
                        pe.wait_ge(mx_fin, h + 2)
                        pe.transpose(ps_x[0:QT, 0:P], mx[:, 1 - par], ident[:]).then_inc(row_turned, 1)
                    if prev and n < LAG:
                        products(h - 1, 1 - par, n - LAG + STEPS)
                    if main and n >= LAG:
                        products(h, par, n - LAG)

            bodies(body, pe)


def project_stage(nc, ident, o, w_hi_in, w_lo_in, v_bias, p_bias, x, y, nb=B):
    S = nb * NCH
    T3 = CHUNK // P
    with ExitStack() as ctx:
        def sb(name, shape, dt=F32):
            return ctx.enter_context(nc.sbuf_tensor(f"p_{name}", shape, dt))

        def psum(name, shape):
            return ctx.enter_context(nc.psum_tensor(f"p_{name}", shape, F32))

        def sem(name):
            return ctx.enter_context(nc.semaphore(f"p_{name}"))

        w_hi = sb("w_hi", [P, CT, C], F32R)
        w_lo = sb("w_lo", [P, CT, C], F32R)
        vb = sb("vb", [P, CT])
        pb = sb("pb", [P, CT])
        o_tok = sb("o_tok", [P, 2, T3, C])
        res = sb("res", [P, 2, CT, CHUNK])
        o_hi = sb("o_hi", [P, 2, CT, CHUNK], F32R)
        o_lo = sb("o_lo", [P, 2, CT, CHUNK], F32R)
        yt = sb("yt", [P, 2, CT, CHUNK])
        ps_t = psum("ps_t", [P, CT, 512])
        ps_y = psum("ps_y", [P, CT, 512])
        par_in, in_, turned = sem("par_in"), sem("in"), sem("turned")
        hi_made, lo_made, y_done, y_made, stored = (sem("hi_made"), sem("lo_made"), sem("y_done"), sem("y_made"),
                                                    sem("stored"))
        o_v = o.rearrange("b (s t p) c -> (b s) p t c", t=T3, p=P)
        x_v = x.rearrange("b (t p) n -> b p t n", p=P)
        y_v = y.rearrange("b (t p) n -> b p t n", p=P)
        block = ctx.enter_context(nc.Block())

        @block.sync
        def _(sp):
            sp.dma_start(f32(w_hi[:]).rearrange("p t n -> p (t n)"), w_hi_in).then_inc(par_in, 16)
            sp.dma_start(f32(w_lo[:]).rearrange("p t n -> p (t n)"), w_lo_in).then_inc(par_in, 16)
            sp.dma_start(vb[:], v_bias.rearrange("(t p) -> p t", p=P), allow_slow_non_contiguous=True).then_inc(par_in, 16)
            sp.dma_start(pb[:], p_bias.rearrange("(t p) -> p t", p=P), allow_slow_non_contiguous=True).then_inc(par_in, 16)
            for a, z in segments(S + 2, [1, 2, 3, S]):
                with sp.Fori(a, z) as it:
                    if a < S:
                        if a >= 1:
                            sp.wait_ge(in_, it * 32)
                        if a >= 2:
                            sp.wait_ge(y_made, (it - 1) * CT)
                        sp.dma_start(o_tok[:, it % 2], o_v[it]).then_inc(in_, 16)
                        sp.dma_start(res[:, it % 2], x_v[it // NCH, :, :, bass.ds((it % NCH) * CHUNK, CHUNK)]).then_inc(in_, 16)
                    if a >= 2:
                        s = it - 2
                        if a >= 3:
                            sp.wait_ge(stored, s * 16)
                        sp.wait_ge(y_made, s * CT + CT)
                        sp.dma_start(y_v[s // NCH, :, :, bass.ds((s % NCH) * CHUNK, CHUNK)], yt[:, s % 2]).then_inc(stored, 16)
            sp.wait_ge(stored, S * 16)

        @block.scalar
        def _(act):
            act.wait_ge(par_in, 64)
            for a, z in segments(S, [2]):
                with act.Fori(a, z) as it:
                    if a >= 2:
                        act.wait_ge(y_done, (it - 1) * CT)
                    for t in range(CT):
                        act.wait_ge(turned, it * CT + t + 1)
                        act.activation(o_hi[:, it % 2, t], ps_t[:, t, 0:CHUNK], ACT.Identity,
                                       bias=vb[:, t:t + 1]).then_inc(hi_made, 1)

        @block.vector
        def _(dve):
            dve.wait_ge(par_in, 64)
            for a, z in segments(S + 1, [1, 2, 3, S]):
                with dve.Fori(a, z) as it:
                    if a < S:
                        for t in range(CT):
                            dve.wait_ge(hi_made, it * CT + t + 1)
                            dve.scalar_tensor_tensor(out=o_lo[:, it % 2, t], in0=ps_t[:, t, 0:CHUNK], scalar=vb[:, t:t + 1],
                                                     in1=f32(o_hi[:, it % 2, t]), op0=ALU.add,
                                                     op1=ALU.subtract).then_inc(lo_made, 1)
                    if a >= 1:
                        s = it - 1
                        if a >= 3:
                            dve.wait_ge(stored, (s - 1) * 16)
                        for t in range(CT):
                            dve.wait_ge(y_done, s * CT + t + 1)
                            dve.scalar_tensor_tensor(out=yt[:, s % 2, t], in0=ps_y[:, t, 0:CHUNK], scalar=pb[:, t:t + 1],
                                                     in1=res[:, s % 2, t], op0=ALU.add, op1=ALU.add).then_inc(y_made, 1)

        @block.tensor
        def _(pe):
            pe.wait_ge(par_in, 64)

            def turn(s, k):
                pe.wait_ge(in_, (s + 1) * 32)
                at_least(pe, lo_made, s * CT)
                for c in range(CT):
                    for t in range(T3):
                        last = pe.transpose(ps_t[:, c, t * P:(t + 1) * P], o_tok[:, k, t, c * P:(c + 1) * P], ident[:])
                    last.then_inc(turned, 1)

            def mul(s, k):
                pe.wait_ge(lo_made, (s + 1) * CT)
                for m in range(CT):
                    at_least(pe, y_made, (s - 1) * CT + m + 1)
                    for j, (wp, op) in enumerate(((w_hi, o_hi), (w_hi, o_lo), (w_lo, o_hi))):
                        for c in range(CT):
                            last = pe.matmul(ps_y[:, m, 0:CHUNK], wp[:, c, m * P:(m + 1) * P], op[:, k, c],
                                             start=j == 0 and c == 0, stop=j == 2 and c == CT - 1)
                    last.then_inc(y_done, 1)

            turn(0, 0)
            turn(1, 1)
            mul(0, 0)
            with pe.Fori(1, S // 2) as i:
                turn(i * 2, 0)
                mul(i * 2 - 1, 1)
                turn(i * 2 + 1, 1)
                mul(i * 2, 0)
            mul(S - 1, 1)


def mlp_stage(nc, ident, ones, n1, w1_hi_in, w1_lo_in, w2_hi_in, w2_lo_in, b1, grn_g, grn_b, b2, y, out, nb=B):
    with ExitStack() as ctx:
        def sb(name, shape, dt=F32):
            return ctx.enter_context(nc.sbuf_tensor(f"m_{name}", shape, dt))

        def psum(name, shape):
            return ctx.enter_context(nc.psum_tensor(f"m_{name}", shape, F32))

        def sem(name):
            return ctx.enter_context(nc.semaphore(f"m_{name}"))

        NF = NCH * FT
        NC3 = NCH * CT
        w1_hi, w1_lo = sb("w1_hi", [P, CT, FH], F32R), sb("w1_lo", [P, CT, FH], F32R)
        w2_hi, w2_lo = sb("w2_hi", [P, FT, C], F32R), sb("w2_lo", [P, FT, C], F32R)
        hid = sb("hid", [P, FT, N])
        io = sb("io", [P, 4 * C])
        x_hi, x_lo = sb("x_hi", [P, CT, CHUNK], F32R), sb("x_lo", [P, CT, CHUNK], F32R)
        h_hi, h_lo = sb("h_hi", [P, 2, CHUNK], F32R), sb("h_lo", [P, 2, CHUNK], F32R)
        junk = sb("junk", [P, CHUNK])
        par = sb("par", [P, 3, FT])
        bias2 = sb("bias2", [P, CT])
        sq = sb("sq", [P, FT, NCH])
        tot, gx, nx, gn, scale = (sb(n, [P, FT]) for n in ("tot", "gx", "nx", "gn", "scale"))
        mean = sb("mean", [P, 3])
        ps_t, ps_h, ps_y = psum("ps_t", [P, CT, 512]), psum("ps_h", [P, 2, 512]), psum("ps_y", [P, CT, 512])
        par_in, tok_in, res_in = sem("par_in"), sem("tok_in"), sem("res_in")
        turned, x_hi_made, x_lo_made = sem("turned"), sem("x_hi_made"), sem("x_lo_made")
        h_done, h_made, sq_made = sem("h_done"), sem("h_made"), sem("sq_made")
        tot_made, gx_made, gsum_done, grn_step = sem("tot_made"), sem("gx_made"), sem("gsum_done"), sem("grn_step")
        scaled, h_hi_made, h_lo_made = sem("scaled"), sem("h_hi_made"), sem("h_lo_made")
        h_used, y_done, y_made, stored = sem("h_used"), sem("y_done"), sem("y_made"), sem("stored")
        USES = FT - 1

        def slot_used(eng, b, n):
            c, f = divmod(n - 2, FT)
            if n < 2:
                at_least(eng, y_done, b * NC3)
            elif f == FT - 1:
                eng.wait_ge(y_done, (b * NCH + c + 1) * CT)
            else:
                eng.wait_ge(h_used, (b * NCH + c) * USES + f + 1)

        GRN = 6

        tok = io[0:TT].rearrange("p (t c) -> p t c", t=4)
        res = io[:, 0:CT * CHUNK].rearrange("p (t n) -> p t n", t=CT)
        tok_v = n1.rearrange("b (s t) p c -> b s p t c", t=4)
        y_v = y.rearrange("b (t p) (s n) -> b s p t n", p=P, n=CHUNK)
        out_v = out.rearrange("b (t p) (s n) -> b s p t n", p=P, n=CHUNK)

        def images(eng, *parts):
            for part in parts:
                part(0)
            if nb > 1:
                with eng.Fori(1, nb) as b:
                    for part in parts:
                        with eng.Fori(b, b + 1) as own:
                            part(own)

        block = ctx.enter_context(nc.Block())

        @block.sync
        def _(sp):
            for dst, src in ((w1_hi, w1_hi_in), (w1_lo, w1_lo_in), (w2_hi, w2_hi_in), (w2_lo, w2_lo_in)):
                sp.dma_start(f32(dst[:]).rearrange("p t n -> p (t n)"), src).then_inc(par_in, 16)
            for i, src in enumerate((b1, grn_g, grn_b)):
                sp.dma_start(par[:, i], src.rearrange("(t p) -> p t", p=P), allow_slow_non_contiguous=True).then_inc(par_in, 16)
            sp.dma_start(bias2[:], b2.rearrange("(t p) -> p t", p=P), allow_slow_non_contiguous=True).then_inc(par_in, 16)

            def tokens(b):
                for c in range(NCH):
                    if c == 0:
                        at_least(sp, stored, b * NCH * 16)
                    else:
                        sp.wait_ge(turned, (b * NCH + c) * CT)
                    sp.dma_start(tok, tok_v[b, c]).then_inc(tok_in, 16)

            def results(b):
                for c in range(NCH):
                    if c == 0:
                        sp.wait_ge(turned, (b + 1) * NC3)
                    at_least(sp, stored, (b * NCH + c) * 16)
                    sp.dma_start(res, y_v[b, c]).then_inc(res_in, 16)
                    sp.wait_ge(y_made, b * NC3 + (c + 1) * CT)
                    sp.dma_start(out_v[b, c], res).then_inc(stored, 16)

            images(sp, tokens, results)
            sp.wait_ge(stored, nb * NCH * 16)

        @block.scalar
        def _(act):
            act.wait_ge(par_in, 128)

            def up(b):
                for c in range(NCH):
                    at_least(act, h_done, (b * NCH + c) * FT)
                    for t in range(CT):
                        act.wait_ge(turned, (b * NCH + c) * CT + t + 1)
                        act.activation(x_hi[:, t], ps_t[:, t, 0:CHUNK], ACT.Copy).then_inc(x_hi_made, 1)
                    if c == 0:
                        at_least(act, h_lo_made, b * NF)
                        at_least(act, h_hi_made, b * NF)
                    for f in range(FT):
                        n = c * FT + f
                        act.wait_ge(h_done, b * NF + n + 1)
                        act.activation(hid[:, f, c * CHUNK:(c + 1) * CHUNK], ps_h[:, f % 2, 0:CHUNK], ACT.Gelu,
                                       bias=par[:, 0, f:f + 1]).then_inc(h_made, 1)

            def down(b):
                act.wait_ge(tot_made, b + 1)
                act.activation(gx[:], tot[:], ACT.Sqrt).then_inc(gx_made, 1)
                for n in range(NF):
                    c, f = divmod(n, FT)
                    act.wait_ge(scaled, b * NF + n + 1)
                    slot_used(act, b, n)
                    act.activation(h_hi[:, n % 2], hid[:, f, c * CHUNK:(c + 1) * CHUNK], ACT.Copy).then_inc(h_hi_made, 1)

            images(act, up, down)

        @block.vector
        def _(dve):
            dve.wait_ge(par_in, 128)

            def grn(b):
                dve.wait_ge(sq_made, (b + 1) * NF)
                dve.tensor_reduce(tot[:], sq[:], AX.X, ALU.add).then_inc(tot_made, 1)
                dve.wait_ge(gsum_done, b + 1)
                dve.tensor_reduce(mean[:, 0:1], ps_t[:, 0, 0:FT], AX.X, ALU.add).then_inc(grn_step, 1)
                at = b * GRN
                dve.wait_ge(grn_step, at + 1)
                dve.tensor_scalar(mean[:, 1:2], mean[:, 0:1], 1.0 / FH, 1e-6, ALU.mult, ALU.add).then_inc(grn_step, 1)
                dve.wait_ge(grn_step, at + 2)
                dve.reciprocal(mean[:, 2:3], mean[:, 1:2]).then_inc(grn_step, 1)
                dve.wait_ge(grn_step, at + 3)
                dve.tensor_scalar(nx[:], gx[:], mean[:, 2:3], None, ALU.mult).then_inc(grn_step, 1)
                dve.wait_ge(grn_step, at + 4)
                dve.tensor_tensor(gn[:], nx[:], par[:, 1], ALU.mult).then_inc(grn_step, 1)
                dve.wait_ge(grn_step, at + 5)
                dve.tensor_scalar(scale[:], gn[:], 1.0, None, ALU.add).then_inc(grn_step, 1)

            def up(b):
                for c in range(NCH):
                    for t in range(CT):
                        dve.wait_ge(x_hi_made, (b * NCH + c) * CT + t + 1)
                        dve.tensor_tensor(x_lo[:, t], ps_t[:, t, 0:CHUNK], f32(x_hi[:, t]), ALU.subtract).then_inc(x_lo_made, 1)
                    for f in range(FT):
                        n = c * FT + f
                        dve.wait_ge(h_made, b * NF + n + 1)
                        at_least(dve, sq_made, b * NF + n)
                        part = hid[:, f, c * CHUNK:(c + 1) * CHUNK]
                        dve.tensor_tensor_reduce(junk[:], part, part, 1.0, 0.0, ALU.mult, ALU.add,
                                                 sq[:, f, c:c + 1]).then_inc(sq_made, 1)

            def affine(b, n):
                c, f = divmod(n, FT)
                part = hid[:, f, c * CHUNK:(c + 1) * CHUNK]
                dve.tensor_scalar(part, part, scale[:, f:f + 1], par[:, 2, f:f + 1], ALU.mult, ALU.add).then_inc(scaled, 1)

            def down(b):
                grn(b)
                dve.wait_ge(grn_step, (b + 1) * GRN)
                affine(b, 0)
                for c in range(NCH):
                    for f in range(FT):
                        n = c * FT + f
                        if n + 1 < NF:
                            affine(b, n + 1)
                        dve.wait_ge(h_hi_made, b * NF + n + 1)
                        slot_used(dve, b, n)
                        dve.tensor_tensor(h_lo[:, n % 2], hid[:, f, c * CHUNK:(c + 1) * CHUNK], f32(h_hi[:, n % 2]),
                                          ALU.subtract).then_inc(h_lo_made, 1)
                    dve.wait_ge(res_in, (b * NCH + c + 1) * 16)
                    for t in range(CT):
                        dve.wait_ge(y_done, (b * NCH + c) * CT + t + 1)
                        dve.scalar_tensor_tensor(out=res[:, t], in0=ps_y[:, t, 0:CHUNK], scalar=bias2[:, t:t + 1],
                                                 in1=res[:, t], op0=ALU.add, op1=ALU.add).then_inc(y_made, 1)

            images(dve, up, down)

        @block.tensor
        def _(pe):
            pe.wait_ge(par_in, 128)

            def turn(b, c):
                pe.wait_ge(tok_in, (b * NCH + c + 1) * 16)
                at_least(pe, x_lo_made, (b * NCH + c) * CT)
                if c == 0:
                    at_least(pe, grn_step, b * GRN)
                for t in range(CT):
                    dst = ps_t[:, t, 0:CHUNK].rearrange("p (two r w) -> p r two w", two=2, w=W)
                    for r in range(4):
                        last = pe.transpose(dst[:, r], tok[:, r, t * P:(t + 1) * P],
                                            ident[0:TT, 0:TT].rearrange("p (two w) -> p two w", w=W))
                    last.then_inc(turned, 1)

            def up(b, c):
                for f in range(FT):
                    n = c * FT + f
                    if f == 0:
                        pe.wait_ge(x_lo_made, (b * NCH + c + 1) * CT)
                    at_least(pe, h_made, b * NF + n - 1)
                    for j, (wp, xp) in enumerate(((w1_hi, x_hi), (w1_hi, x_lo), (w1_lo, x_hi))):
                        for t in range(CT):
                            last = pe.matmul(ps_h[:, f % 2, 0:CHUNK], wp[:, t, f * P:(f + 1) * P], xp[:, t],
                                             start=j == 0 and t == 0, stop=j == 2 and t == CT - 1)
                    last.then_inc(h_done, 1)

            def down(b, c):
                for f in range(FT):
                    n = c * FT + f
                    pe.wait_ge(h_hi_made, b * NF + n + 1)
                    pe.wait_ge(h_lo_made, b * NF + n + 1)
                    for m in range(CT):
                        if f == 0:
                            at_least(pe, y_made, (b * NCH + c - 1) * CT + m + 1)
                        for j, (wp, hp) in enumerate(((w2_hi, h_hi), (w2_hi, h_lo), (w2_lo, h_hi))):
                            last = pe.matmul(ps_y[:, m, 0:CHUNK], wp[:, f, m * P:(m + 1) * P], hp[:, n % 2],
                                             start=f == 0 and j == 0, stop=f == FT - 1 and j == 2)
                        if f == FT - 1:
                            last.then_inc(y_done, 1)
                    if f < FT - 1:
                        last.then_inc(h_used, 1)

            def all_up(b):
                for c in range(NCH):
                    turn(b, c)
                    up(b, c)

            def all_down(b):
                pe.wait_ge(gx_made, b + 1)
                pe.matmul(ps_t[:, 0, 0:FT], ones[:], gx[:], start=True, stop=True).then_inc(gsum_done, 1)
                for c in range(NCH):
                    down(b, c)

            images(pe, all_up, all_down)


def build(nc, a, out):
    def scratch(name, shape):
        return nc.dram_tensor(name, shape, F32, kind="Internal").ap()

    tok = (B, 4 * NCH, TT, C)
    x_hi, x_lo = scratch("x_hi", (B, C, N)), scratch("x_lo", (B, C, N))
    local, normed1 = scratch("local", tok), scratch("normed1", tok)
    o, y = scratch("o", (B, N, C)), scratch("y", (B, C, N))
    pairs = {}
    for name in ("w_qkv", "w_proj", "w_up", "w_down"):
        pairs[name] = scratch(name + "_hi", a[name].shape), scratch(name + "_lo", a[name].shape)
    flat = a["x"].rearrange("b c h w -> b c (h w)")
    with ExitStack() as ctx:
        ident, cmask, ones = shared_consts(nc, ctx)
        split_stage(nc, "s", [(a["w_qkv"][h], pairs["w_qkv"][0][h], pairs["w_qkv"][1][h]) for h in range(HEADS)]
                    + [(a[n], *pairs[n]) for n in ("w_proj", "w_up", "w_down")])
        conv_stage(nc, "c0", ident, cmask, a["x"], a["taps0"],
                   [a["bn_gamma"], a["bn_beta"], a["bn_mean"], a["bn_var"]], a["ln0_g"], a["ln0_b"], local)
        norm_stage(nc, ident, flat, a["ln0_g"], a["ln0_b"], x_hi, x_lo)
        attend_stage(nc, ident, x_hi, x_lo, *(p.rearrange("h p n -> h p n") for p in pairs["w_qkv"]),
                     a["qkv_b"][0:C], a["qkv_b"][C:2 * C], local, o)
        project_stage(nc, ident, o, *pairs["w_proj"], a["qkv_b"][2 * C:3 * C], a["proj_b"], flat, y)
        conv_stage(nc, "c1", ident, cmask, y.rearrange("b c (h w) -> b c h w", w=W), a["taps1"], [a["dw_b"]],
                   a["ln1_g"], a["ln1_b"], normed1)
        mlp_stage(nc, ident, ones, normed1, *pairs["w_up"], *pairs["w_down"], a["b1"], a["grn_g"], a["grn_b"],
                  a["b2"], y, out.rearrange("b c h w -> b c (h w)"))


def kernel(**inputs):
    import concourse.bacc as bacc
    from concourse.bass_utils import run_bass_kernel_spmd as run

    def tiles(w):
        t = w.shape[0] // P
        return np.ascontiguousarray(w.reshape(t, P, -1).transpose(1, 0, 2).reshape(P, -1))

    i = {k: np.asarray(v) for k, v in inputs.items()}
    qkv = i["L0_conv_qkv_w"].reshape(3, HEADS, HD, C)
    qkv = np.stack([qkv[0], qkv[0], qkv[1], qkv[1], qkv[2]]).transpose(1, 3, 0, 2).reshape(HEADS, C, 5 * HD)
    arrays = {
        "x": i["x"],
        "w_qkv": np.stack([tiles(w) for w in qkv]),
        "w_proj": tiles(i["L0_conv_proj_w"].T),
        "w_up": tiles(i["L1_conv_w1"]),
        "w_down": tiles(i["L1_conv_w2"]),
        "taps0": i["L0_conv_conv_w"][:, :, ::-1],
        "taps1": i["L1_conv_dw_w"][:, :, ::-1],
        "bn_gamma": i["L0_conv_bn_gamma"], "bn_beta": i["L0_conv_bn_beta"],
        "bn_mean": i["L0_conv_bn_mean"], "bn_var": i["L0_conv_bn_var"],
        "ln0_g": i["L0_conv_ln_gamma"], "ln0_b": i["L0_conv_ln_beta"],
        "qkv_b": i["L0_conv_qkv_b"], "proj_b": i["L0_conv_proj_b"],
        "dw_b": i["L1_conv_dw_b"], "ln1_g": i["L1_conv_ln_g"], "ln1_b": i["L1_conv_ln_b"],
        "b1": i["L1_conv_b1"], "grn_g": i["L1_conv_grn_g"], "grn_b": i["L1_conv_grn_b"], "b2": i["L1_conv_b2"],
    }
    arrays = {k: np.ascontiguousarray(v) for k, v in arrays.items()}
    nc = bacc.Bacc("TRN2", target_bir_lowering=False, num_devices=1)
    aps = {k: nc.dram_tensor("in_" + k, v.shape, F32, kind="ExternalInput").ap() for k, v in arrays.items()}
    out = nc.dram_tensor("out", (B, C, H, W), F32, kind="ExternalOutput").ap()
    build(nc, aps, out)
    r = run(nc, [{"in_" + k: v for k, v in arrays.items()}], core_ids=[0])
    return r.results[0]["out"]
```

```python
from contextlib import ExitStack

import numpy as np

import concourse.bass as bass
from concourse import mybir
from concourse.alu_op_type import AluOpType as ALU

F32 = mybir.dt.float32
F32R = mybir.dt.float32r
ACT = mybir.ActivationFunctionType
AX = mybir.AxisListType

B, C, H, W = 4, 384, 48, 48
N = H * W
P = 128
CT = C // P
HEADS, HD = 8, 48
CHUNK = 384
NCH = N // CHUNK
TT = 96
FH = 4 * C
FT = FH // P
QR = 4
GC = P // QR
NG = C // GC
HB = H // QR
KS = 7
NU = KS + 2 * QR - 3


def f32(ap):
    return ap.bitcast(F32)


def f32r(ap):
    return ap.bitcast(F32R)


def shared_consts(nc, ctx):
    ident = ctx.enter_context(nc.sbuf_tensor("ident", [P, P], F32))
    cmask = ctx.enter_context(nc.sbuf_tensor("cmask", [P, GC], F32))
    ones = ctx.enter_context(nc.sbuf_tensor("ones", [P, P], F32))
    made = ctx.enter_context(nc.semaphore("consts_made"))
    with nc.Block() as block:
        @block.gpsimd
        def _(pool):
            pool.memset(ident[:], 0.0).then_inc(made, 1)
            pool.memset(ones[:], 1.0).then_inc(made, 1)
            pool.wait_ge(made, 2)
            pool.affine_select(out=ident[:], in_=ident[:], compare_op=ALU.not_equal, fill=1.0, base=0,
                               pattern=[[-1, P]], channel_multiplier=1).then_inc(made, 1)
            pool.wait_ge(made, 3)
            pool.tensor_tensor(cmask[:], ident[:, 0:GC], ident[:, GC:2 * GC], ALU.add).then_inc(made, 1)
            for r in range(2, QR):
                pool.wait_ge(made, 2 + r)
                pool.tensor_tensor(cmask[:], cmask[:], ident[:, r * GC:(r + 1) * GC], ALU.add).then_inc(made, 1)
    return ident, cmask, ones


def segments(total, edges):
    cuts = sorted({0, total, *[e for e in edges if 0 < e < total]})
    return list(zip(cuts[:-1], cuts[1:]))


def at_least(eng, sem, count):
    if not isinstance(count, int) or count > 0:
        eng.wait_ge(sem, count)


def conv_stage(nc, tag, ident, cmask, src, taps, affine, ln_g, ln_b, dst, nb=B):
    S = nb * NG
    LE = 2
    LN = NG + 2
    LC = LN + 2
    with ExitStack() as ctx:
        def sb(name, shape, dt=F32):
            return ctx.enter_context(nc.sbuf_tensor(f"{tag}_{name}", shape, dt))

        def psum(name, shape):
            return ctx.enter_context(nc.psum_tensor(f"{tag}_{name}", shape, F32))

        def sem(name):
            return ctx.enter_context(nc.semaphore(f"{tag}_{name}"))

        tap_raw = sb("tap_raw", [P, NG, NU, KS])
        tap_hi = sb("tap_hi", [P, NG, NU, KS], F32R)
        tap_lo = sb("tap_lo", [P, NG, NU, KS], F32R)
        band_hi = sb("band_hi", [P, 2, 3, KS, P], F32R)
        band_lo = sb("band_lo", [P, 2, 3, KS, P], F32R)
        x_raw = sb("x_raw", [P, 2, HB, W])
        x_hi = sb("x_hi", [P, 2, HB + 2, W + 6], F32R)
        x_lo = sb("x_lo", [P, 2, HB + 2, W + 6], F32R)
        par = sb("par", [P, 4, NG])
        scale = sb("scale", [P, NG])
        shift = sb("shift", [P, NG])
        tmp = sb("tmp", [P, 3, NG])
        local = sb("local", [P, 2, HB * W])
        tok = sb("tok", [TT, 2, 4 * NCH, C])
        gam = sb("gam", [TT, C])
        bet = sb("bet", [TT, C])
        st = sb("st", [TT, 2, 6])
        mv = sb("mv", [TT, 2, 2])
        sd = sb("sd", [TT, 2])
        rs = sb("rs", [TT, 2])
        idle = sb("idle", [TT, 1])
        eps = sb("eps", [P, 1])
        eps_bn = sb("eps_bn", [P, 1])
        cen = sb("cen", [TT, 2, C])
        nrm = sb("nrm", [TT, 2, 2, C])
        chan = sb("chan", [P, 2, CT, 2, 2, W])
        acc = psum("acc", [P, 4, 512])
        tps = psum("tps", [P, 2, 512])
        cps = psum("cps", [P, 2, 512])

        taps_in, par_in = sem("taps_in"), sem("par_in")
        zeroed, taps_hi, taps_lo = sem("zeroed"), sem("taps_hi"), sem("taps_lo")
        bn_sd, bn_dve = sem("bn_sd"), sem("bn_dve")
        x_in = sem("x_in")
        hi_made, lo_made, bands_made = sem("hi_made"), sem("lo_made"), sem("bands_made")
        conv_done, local_made, turned, tok_made = sem("conv_done"), sem("local_made"), sem("turned"), sem("tok_made")
        sd_made, dve_ln, nrm_made = sem("sd_made"), sem("dve_ln"), sem("nrm_made")
        back, chan_made, stored = sem("back"), sem("chan_made"), sem("stored")

        groups = src.rearrange("b (g c) (hb hi) w -> (b g) hi c hb w", c=GC, hi=QR)
        tap_src = taps.rearrange("(g c) one kh kw -> c g (one kh kw)", c=GC)
        rows_out = dst.rearrange("b (t p) (k two j w) -> b k j t p two w", p=P, two=2, j=2, w=2 * W)
        batch_norm = len(affine) == 4
        HALF = HB // 2 * W

        block = ctx.enter_context(nc.Block())

        @block.sync
        def _(sp):
            sp.wait_ge(zeroed, 1)
            for hi in range(QR):
                sp.dma_start(tap_raw[hi * GC:(hi + 1) * GC, :, hi + 1:hi + 1 + KS, :].rearrange("c g u d -> c g (u d)"),
                             tap_src).then_inc(taps_in, 16)
            for hi in range(QR):
                for k, v in enumerate(affine):
                    sp.dma_start(par[hi * GC:(hi + 1) * GC, k, :], v.rearrange("(g c) -> c g", c=GC),
                                 allow_slow_non_contiguous=True).then_inc(par_in, 16)
            sp.dma_start(gam[:], ln_g.partition_broadcast(TT)).then_inc(par_in, 16)
            sp.dma_start(bet[:], ln_b.partition_broadcast(TT)).then_inc(par_in, 16)
            for a, z in segments(S + LC + 1, [1, 2, S, LC + 1, LC + 2]):
                with sp.Fori(a, z) as it:
                    if a < S:
                        if a >= 2:
                            sp.wait_ge(lo_made, it - 1)
                        if a >= 1:
                            sp.wait_ge(x_in, it * 16 * QR)
                        for hi in range(QR):
                            sp.dma_start(x_raw[hi * GC:(hi + 1) * GC, it % 2, :, :],
                                         groups[it, hi]).then_inc(x_in, 16)
                    if a >= LC + 1:
                        s = it - (LC + 1)
                        if a >= LC + 2:
                            sp.wait_ge(stored, s * 16 * CT)
                        sp.wait_ge(chan_made, s * 2 + 2)
                        for c in range(CT):
                            sp.dma_start(rows_out[s // NG, (s % NG) // 2, s % 2, c],
                                         chan[:, s % 2, c].rearrange("p two t w -> p two (t w)")).then_inc(stored, 16)
            sp.wait_ge(stored, S * 16 * CT)

        @block.scalar
        def _(act):
            act.wait_ge(taps_in, 16 * QR)
            act.activation(tap_hi[:], tap_raw[:], ACT.Copy).then_inc(taps_hi, 1)
            act.wait_ge(zeroed, 4)
            act.wait_ge(par_in, 16 * (QR * len(affine) + 2))
            if batch_norm:
                act.activation(tmp[:, 0], par[:, 3], ACT.Sqrt, bias=eps_bn[:, 0:1]).then_inc(bn_sd, 1)
            act.wait_ge(bn_dve, 4 if batch_norm else 2)
            for a, z in segments(S + LC, [1, 2, 3, S, S + 1, LN, S + LN, LC, LC + 2]):
                with act.Fori(a, z) as it:
                    if a < S:
                        act.wait_ge(x_in, (it + 1) * 16 * QR)
                        if a >= 2:
                            act.wait_ge(conv_done, it - 1)
                        act.activation(x_hi[:, it % 2, 1:HB + 1, 3:3 + W], x_raw[:, it % 2], ACT.Copy).then_inc(hi_made, 1)
                    if 1 <= a < S + 1:
                        s = it - 1
                        act.wait_ge(conv_done, it)
                        if a >= 3:
                            act.wait_ge(turned, (it - 2) * 2)
                        for h in range(2):
                            act.activation(local[:, s % 2, h * HALF:(h + 1) * HALF],
                                           acc[:, bass.ds((s % 2) * 2 + h, 1), 0:HALF], ACT.Identity,
                                           scale=scale[:, bass.ds(s % NG, 1)],
                                           bias=shift[:, bass.ds(s % NG, 1)]).then_inc(local_made, 1)
                    if a >= LC:
                        s = it - LC
                        if a >= LC + 2:
                            act.wait_ge(stored, (s - 1) * 16 * CT)
                        for t in range(2):
                            act.wait_ge(back, s * 2 + t + 1)
                            act.activation(chan[:, s % 2, :, :, t, :],
                                           cps[:, t, 0:CT * TT].rearrange("p (c two w) -> p c two w", c=CT, two=2),
                                           ACT.Copy).then_inc(chan_made, 1)
                    if LN <= a < S + LN:
                        s = it - LN
                        act.wait_ge(dve_ln, s * 7 + 4)
                        act.activation(sd[:], mv[:, :, 1], ACT.Sqrt, bias=eps[0:TT, 0:1]).then_inc(sd_made, 1)

        @block.vector
        def _(dve):
            dve.memset(tap_raw[:], 0.0).then_inc(zeroed, 1)
            dve.memset(eps[:], 1e-6).then_inc(zeroed, 1)
            dve.memset(eps_bn[:], 1e-5).then_inc(zeroed, 1)
            dve.memset(f32(x_hi[:]), 0.0)
            dve.memset(f32(x_lo[:]), 0.0).then_inc(zeroed, 1)
            dve.wait_ge(taps_hi, 1)
            dve.tensor_tensor(tap_lo[:], tap_raw[:], f32(tap_hi[:]), ALU.subtract).then_inc(taps_lo, 1)
            dve.wait_ge(par_in, 16 * (QR * len(affine) + 2))
            if batch_norm:
                dve.wait_ge(bn_sd, 1)
                dve.reciprocal(tmp[:, 1], tmp[:, 0]).then_inc(bn_dve, 1)
                dve.wait_ge(bn_dve, 1)
                dve.tensor_tensor(scale[:], par[:, 0], tmp[:, 1], ALU.mult).then_inc(bn_dve, 1)
                dve.wait_ge(bn_dve, 2)
                dve.tensor_tensor(tmp[:, 2], par[:, 2], scale[:], ALU.mult).then_inc(bn_dve, 1)
                dve.wait_ge(bn_dve, 3)
                dve.tensor_tensor(shift[:], par[:, 1], tmp[:, 2], ALU.subtract).then_inc(bn_dve, 1)
            else:
                dve.memset(scale[:], 1.0).then_inc(bn_dve, 1)
                dve.tensor_copy(shift[:], par[:, 0]).then_inc(bn_dve, 1)
            for a, z in segments(S + LN, [2, S, S + LE, LN, LN + 1, LN + 2]):
                with dve.Fori(a, z) as it:
                    if a < S:
                        dve.wait_ge(hi_made, it + 1)
                        if a >= 2:
                            dve.wait_ge(conv_done, it - 1)
                        dve.tensor_tensor(x_lo[:, it % 2, 1:HB + 1, 3:3 + W], x_raw[:, it % 2],
                                          f32(x_hi[:, it % 2, 1:HB + 1, 3:3 + W]), ALU.subtract).then_inc(lo_made, 1)
                    if a >= LN + 1:
                        dve.wait_ge(nrm_made, (it - LN) * 2)
                    if LE <= a < S + LE:
                        s = it - LE
                        for h in range(2):
                            dve.wait_ge(turned, s * 2 + h + 1)
                            dve.tensor_copy(
                                tok[:, (s // NG) % 2, 12 * h:12 * h + 12, bass.ds((s % NG) * GC, GC)],
                                tps[0:TT, h, 0:CHUNK].rearrange("p (t c) -> p t c", c=GC)).then_inc(tok_made, 1)
                    if a >= LN:
                        s = it - LN
                        slot = (s // NG) % 2
                        dve.wait_ge(tok_made, min(S, a - 1) * 2 if z - a == 1 or a >= S else (it - 1) * 2)
                        for t in range(2):
                            dve.bn_stats(st[:, t], tok[:, slot, bass.ds((s % NG) * 2 + t, 1), :]).then_inc(dve_ln, 1)
                        dve.wait_ge(dve_ln, s * 7 + 2)
                        dve.memset(idle[:], 0.0)
                        for t in range(2):
                            dve.bn_aggr(mv[:, t], st[:, t]).then_inc(dve_ln, 1)
                        dve.wait_ge(sd_made, s + 1)
                        dve.reciprocal(rs[:], sd[:]).then_inc(dve_ln, 1)
                        for t in range(2):
                            dve.scalar_tensor_tensor(out=cen[:, t], in0=tok[:, slot, bass.ds((s % NG) * 2 + t, 1), :],
                                                     scalar=mv[:, t, 0:1], in1=gam[:], op0=ALU.subtract,
                                                     op1=ALU.mult).then_inc(dve_ln, 1)
                        if a >= LN + 2:
                            dve.wait_ge(back, (s - 1) * 2)
                        for t in range(2):
                            dve.wait_ge(dve_ln, s * 7 + 6 + t)
                            dve.scalar_tensor_tensor(out=nrm[:, s % 2, t], in0=cen[:, t], scalar=rs[:, t:t + 1],
                                                     in1=bet[:], op0=ALU.mult, op1=ALU.add).then_inc(nrm_made, 1)

        @block.gpsimd
        def _(pool):
            pool.wait_ge(taps_lo, 1)
            for a, z in segments(S, [2]):
                with pool.Fori(a, z) as it:
                    if a >= 2:
                        pool.wait_ge(conv_done, it - 1)
                    for band, tap in ((band_hi, tap_hi), (band_lo, tap_lo)):
                        for o in range(3):
                            u0 = 2 * QR - QR * o
                            taps_of = f32(tap[:, bass.ds(it % NG, 1), u0:u0 + QR, :]).rearrange("p one u d -> p (one d) u")
                            last = pool.tensor_tensor(
                                band[:, it % 2, o].rearrange("p d (u c) -> p d u c", c=GC),
                                taps_of.unsqueeze(3).to_broadcast([P, KS, QR, GC]),
                                cmask[:].unsqueeze(1).unsqueeze(1).to_broadcast([P, KS, QR, GC]), ALU.mult)
                    last.then_inc(bands_made, 1)

        @block.tensor
        def _(pe):
            def conv(s, k, wait_acc=True):
                pe.wait_ge(bands_made, s + 1)
                pe.wait_ge(lo_made, s + 1)
                if wait_acc:
                    pe.wait_ge(local_made, (s - 1) * 2)
                for o in range(3):
                    for d in range(KS):
                        first, end = o == 0 and d == 0, o == 2 and d == KS - 1
                        for band, xs in ((band_hi, (x_hi, x_lo)), (band_lo, (x_hi,))):
                            for h in range(2):
                                for x in xs:
                                    r0 = h * HB // 2 + o
                                    last = pe.matmul(acc[:, 2 * k + h, 0:HALF], band[:, k, o, d, :],
                                                     x[:, k, r0:r0 + HB // 2, d:d + W],
                                                     start=first and band is band_hi and x is x_hi,
                                                     stop=end and band is band_lo)
                last.then_inc(conv_done, 1)

            def turn(s, k, wait_tok=True):
                for h in range(2):
                    pe.wait_ge(local_made, s * 2 + h + 1)
                    if wait_tok:
                        pe.wait_ge(tok_made, s * 2 - 1 + h)
                    for t in range(3):
                        last = pe.transpose(tps[0:TT, h, t * P:(t + 1) * P],
                                            local[:, k, h * HALF + t * TT:h * HALF + (t + 1) * TT], ident[:])
                    last.then_inc(turned, 1)

            def to_channels(s, k):
                pe.wait_ge(nrm_made, s * 2 + 2)
                at_least(pe, chan_made, s * 2)
                for t in range(2):
                    for c in range(CT):
                        last = pe.transpose(cps[:, t, c * TT:(c + 1) * TT], nrm[:, k, t, c * P:(c + 1) * P],
                                            ident[0:TT, 0:TT])
                    last.then_inc(back, 1)

            conv(0, 0, False)
            conv(1, 1, False)
            turn(0, 0, False)
            with pe.Fori(1, LC // 2) as i:
                conv(i * 2, 0)
                turn(i * 2 - 1, 1)
                conv(i * 2 + 1, 1)
                turn(i * 2, 0)
            for it in range(LC, LC + 2):
                if it < S:
                    to_channels(it - LC, it % 2)
                    conv(it, it % 2)
                    turn(it - 1, 1 - it % 2)
            with pe.Fori(LC // 2 + 1, S // 2) as i:
                to_channels(i * 2 - LC, 0)
                conv(i * 2, 0)
                turn(i * 2 - 1, 1)
                to_channels(i * 2 + 1 - LC, 1)
                conv(i * 2 + 1, 1)
                turn(i * 2, 0)
            turn(S - 1, 1)
            with pe.Fori(S // 2, (S + LC) // 2) as i:
                to_channels(i * 2 - LC, 0)
                to_channels(i * 2 + 1 - LC, 1)


def split_stage(nc, tag, items):
    with ExitStack() as ctx:
        def sb(name, shape, dt=F32):
            return ctx.enter_context(nc.sbuf_tensor(f"{tag}_{name}", shape, dt))

        def sem(name):
            return ctx.enter_context(nc.semaphore(f"{tag}_{name}"))

        loaded = [sem(f"loaded{n}") for n in range(len(items))]
        hi_made, lo_made, stored = sem("hi_made"), sem("lo_made"), sem("stored")
        raw = [sb(f"raw{n}", [P, it[0].shape[1]]) for n, it in enumerate(items)]
        hi = [sb(f"hi{n}", [P, it[0].shape[1]], F32R) for n, it in enumerate(items)]
        lo = [sb(f"lo{n}", [P, it[0].shape[1]], F32R) for n, it in enumerate(items)]
        block = ctx.enter_context(nc.Block())

        @block.sync
        def _(sp):
            for n, (src, _h, _l) in enumerate(items):
                sp.dma_start(raw[n][:], src).then_inc(loaded[n], 16)
            for n, (_s, hi_out, lo_out) in enumerate(items):
                sp.wait_ge(hi_made, n + 1)
                sp.dma_start(hi_out, f32(hi[n][:])).then_inc(stored, 16)
                sp.wait_ge(lo_made, n + 1)
                sp.dma_start(lo_out, f32(lo[n][:])).then_inc(stored, 16)
            sp.wait_ge(stored, 32 * len(items))

        @block.scalar
        def _(act):
            for n in range(len(items)):
                act.wait_ge(loaded[n], 16)
                act.activation(hi[n][:], raw[n][:], ACT.Copy).then_inc(hi_made, 1)

        @block.vector
        def _(dve):
            for n in range(len(items)):
                dve.wait_ge(hi_made, n + 1)
                dve.tensor_tensor(lo[n][:], raw[n][:], f32(hi[n][:]), ALU.subtract).then_inc(lo_made, 1)


def norm_stage(nc, ident, x, ln_g, ln_b, w_hi_in, w_lo_in, x_hi_out, x_lo_out, v_out, nb=B):
    S = nb * NCH
    NT = CHUNK // P
    with ExitStack() as ctx:
        def sb(name, shape, dt=F32):
            return ctx.enter_context(nc.sbuf_tensor(f"n_{name}", shape, dt))

        def psum(name, shape):
            return ctx.enter_context(nc.psum_tensor(f"n_{name}", shape, F32))

        def sem(name):
            return ctx.enter_context(nc.semaphore(f"n_{name}"))

        xc = sb("xc", [P, 2, CT, CHUNK])
        st = sb("st", [P, NT, 6])
        mv = sb("mv", [P, NT, 2])
        sd = sb("sd", [P, NT])
        rs = sb("rs", [P, NT])
        nrm = sb("nrm", [P, 2, NT, C])
        w_hi, w_lo = sb("w_hi", [P, CT, C], F32R), sb("w_lo", [P, CT, C], F32R)
        v = sb("v", [P, 2, NT, HEADS, 2, HD])
        full = sb("full", [P, 2, CT, CHUNK])
        hi = sb("hi", [P, 2, CT, CHUNK], F32R)
        lo = sb("lo", [P, 2, CT, CHUNK], F32R)
        gam = sb("gam", [P, CT])
        bet = sb("bet", [P, CT])
        eps = sb("eps", [P, 1])
        idle = sb("idle", [P, 1])
        ps_tok = psum("ps_tok", [P, NT, 512])
        ps_ch = psum("ps_ch", [P, CT, 512])
        ps_v = psum("ps_v", [P, 2, 512])
        v_done, v_hi_made, v_made, v_stored = sem("v_done"), sem("v_hi_made"), sem("v_made"), sem("v_stored")
        x_in, par_in, eps_made = sem("x_in"), sem("par_in"), sem("eps_made")
        to_tok, to_ch, stats, sd_made, rs_made = sem("to_tok"), sem("to_ch"), sem("stats"), sem("sd_made"), sem("rs_made")
        normed, full_made, hi_made, lo_made, stored = (sem("normed"), sem("full_made"), sem("hi_made"), sem("lo_made"),
                                                       sem("stored"))
        xs = x.rearrange("b (t p) n -> b p t n", p=P)
        his = x_hi_out.rearrange("b (t p) n -> b p t n", p=P)
        los = x_lo_out.rearrange("b (t p) n -> b p t n", p=P)
        v_v = v_out.rearrange("b h (s t p) n -> b s t p h n", t=NT, p=P)
        block = ctx.enter_context(nc.Block())

        @block.sync
        def _(sp):
            sp.dma_start(gam[:], ln_g.rearrange("(t p) -> p t", p=P), allow_slow_non_contiguous=True).then_inc(par_in, 16)
            sp.dma_start(bet[:], ln_b.rearrange("(t p) -> p t", p=P), allow_slow_non_contiguous=True).then_inc(par_in, 16)
            for part, src in ((w_hi, w_hi_in), (w_lo, w_lo_in)):
                sp.dma_start(f32(part[:]).rearrange("p t n -> p (t n)"), src).then_inc(par_in, 16)
            for a, z in segments(S + 4, [1, 2, 3, 4, 5, S, S + 3]):
                with sp.Fori(a, z) as it:
                    if a < S:
                        if a >= 1:
                            sp.wait_ge(x_in, it * 16)
                        if a >= 2:
                            sp.wait_ge(to_tok, (it - 1) * NT)
                        sp.dma_start(xc[:, it % 2], xs[it // NCH, :, :, bass.ds((it % NCH) * CHUNK, CHUNK)]).then_inc(x_in, 16)
                    if 3 <= a < S + 3:
                        s = it - 3
                        if a >= 4:
                            sp.wait_ge(stored, s * 32)
                        sp.wait_ge(lo_made, s * CT + CT)
                        for part, out in ((hi, his), (lo, los)):
                            sp.dma_start(out[s // NCH, :, :, bass.ds((s % NCH) * CHUNK, CHUNK)],
                                         f32(part[:, s % 2])).then_inc(stored, 16)
                    if a >= 4:
                        s = it - 4
                        if a >= 5:
                            sp.wait_ge(v_stored, s * 16 * NT)
                        sp.wait_ge(v_made, s * NT + NT)
                        for t in range(NT):
                            sp.dma_start(v_v[s // NCH, s % NCH, t],
                                         v[:, s % 2, t].rearrange("p h two d -> p h (two d)")).then_inc(v_stored, 16)
            sp.wait_ge(stored, S * 32)
            sp.wait_ge(v_stored, S * 16 * NT)

        @block.vector
        def _(dve):
            dve.memset(eps[:], 1e-6).then_inc(eps_made, 1)
            def values(s):
                for t in range(NT):
                    dve.wait_ge(v_hi_made, s * NT + t + 1)
                    dve.tensor_tensor(f32r(v[:, s % 2, t, :, 1, :]),
                                      ps_v[:, bass.ds((s * NT + t) % 2, 1), 0:C].rearrange("p one (h d) -> p (one h) d", d=HD),
                                      v[:, s % 2, t, :, 0, :], ALU.subtract).then_inc(v_made, 1)

            for a, z in segments(S + 2, [1, 2, S]):
                with dve.Fori(a, z) as it:
                    if a >= S:
                        values(it - 2)
                        continue
                    for t in range(NT):
                        dve.wait_ge(to_tok, it * NT + t + 1)
                        dve.bn_stats(st[:, t], ps_tok[:, t, 0:C]).then_inc(stats, 1)
                    dve.wait_ge(stats, it * 2 * NT + NT)
                    dve.memset(idle[:], 0.0)
                    for t in range(NT):
                        dve.bn_aggr(mv[:, t], st[:, t]).then_inc(stats, 1)
                    dve.wait_ge(sd_made, it + 1)
                    dve.reciprocal(rs[:], sd[:]).then_inc(rs_made, 1)
                    if a >= 2:
                        dve.wait_ge(to_ch, (it - 1) * CT)
                    dve.wait_ge(rs_made, it + 1)
                    for t in range(NT):
                        dve.tensor_scalar(nrm[:, it % 2, t], ps_tok[:, t, 0:C], mv[:, t, 0:1], rs[:, t:t + 1],
                                          ALU.subtract, ALU.mult).then_inc(normed, 1)
                    if a >= 2:
                        values(it - 2)

        @block.scalar
        def _(act):
            act.wait_ge(eps_made, 1)
            act.wait_ge(par_in, 64)
            for a, z in segments(S + 2, [1, 2, 3, 4, S, S + 1]):
                with act.Fori(a, z) as it:
                    if a < S:
                        act.wait_ge(stats, it * 2 * NT + 2 * NT)
                        act.activation(sd[:], mv[:, :, 1], ACT.Sqrt, bias=eps[:, 0:1]).then_inc(sd_made, 1)
                    if 1 <= a < S + 1:
                        s = it - 1
                        if a >= 3:
                            act.wait_ge(lo_made, (s - 1) * CT)
                            act.wait_ge(stored, (s - 1) * 32)
                        for t in range(CT):
                            act.wait_ge(to_ch, s * CT + t + 1)
                            act.activation(full[:, s % 2, t], ps_ch[:, t, 0:CHUNK], ACT.Identity,
                                           scale=gam[:, t:t + 1], bias=bet[:, t:t + 1]).then_inc(full_made, 1)
                        for t in range(CT):
                            act.wait_ge(full_made, s * CT + t + 1)
                            if a >= 3:
                                act.wait_ge(v_done, (s - 1) * NT)
                            act.activation(hi[:, s % 2, t], full[:, s % 2, t], ACT.Copy).then_inc(hi_made, 1)
                    if a >= 2:
                        s = it - 2
                        if a >= 4:
                            act.wait_ge(v_stored, (s - 1) * 16 * NT)
                        for t in range(NT):
                            act.wait_ge(v_done, s * NT + t + 1)
                            act.activation(f32r(v[:, s % 2, t, :, 0, :]),
                                           ps_v[:, bass.ds((s * NT + t) % 2, 1), 0:C].rearrange("p one (h d) -> p (one h) d", d=HD),
                                           ACT.Copy).then_inc(v_hi_made, 1)

        @block.gpsimd
        def _(pool):
            for a, z in segments(S, [2]):
                with pool.Fori(a, z) as it:
                    if a >= 2:
                        pool.wait_ge(stored, (it - 1) * 32)
                        pool.wait_ge(v_done, (it - 1) * NT)
                    for t in range(CT):
                        pool.wait_ge(hi_made, it * CT + t + 1)
                        pool.tensor_tensor(lo[:, it % 2, t], full[:, it % 2, t], f32(hi[:, it % 2, t]),
                                           ALU.subtract).then_inc(lo_made, 1)

        @block.tensor
        def _(pe):
            def tokens(s, k):
                pe.wait_ge(x_in, (s + 1) * 16)
                at_least(pe, normed, s * NT)
                for t in range(NT):
                    for c in range(CT):
                        last = pe.transpose(ps_tok[:, t, c * P:(c + 1) * P], xc[:, k, c, t * P:(t + 1) * P], ident[:])
                    last.then_inc(to_tok, 1)

            def channels(s, k):
                pe.wait_ge(normed, (s + 1) * NT)
                at_least(pe, full_made, s * CT)
                for c in range(CT):
                    for t in range(NT):
                        last = pe.transpose(ps_ch[:, c, t * P:(t + 1) * P], nrm[:, k, t, c * P:(c + 1) * P], ident[:])
                    last.then_inc(to_ch, 1)

            def values(s, k):
                pe.wait_ge(hi_made, (s + 1) * CT)
                pe.wait_ge(lo_made, (s + 1) * CT)
                for t in range(NT):
                    at_least(pe, v_made, s * NT + t - 1)
                    tok = slice(t * P, (t + 1) * P)
                    for j, (xp, wp) in enumerate(((hi, w_hi), (lo, w_hi), (hi, w_lo))):
                        for c in range(CT):
                            last = pe.matmul(ps_v[:, (k * NT + t) % 2, 0:C], xp[:, k, c, tok], wp[:, c, :],
                                             start=j == 0 and c == 0, stop=j == 2 and c == CT - 1)
                    last.then_inc(v_done, 1)

            pe.wait_ge(par_in, 64)
            tokens(0, 0)
            tokens(1, 1)
            channels(0, 0)
            tokens(2, 0)
            channels(1, 1)
            values(0, 0)
            tokens(3, 1)
            channels(2, 0)
            values(1, 1)
            with pe.Fori(2, S // 2) as i:
                tokens(i * 2, 0)
                channels(i * 2 - 1, 1)
                values(i * 2 - 2, 0)
                tokens(i * 2 + 1, 1)
                channels(i * 2, 0)
                values(i * 2 - 1, 1)
            channels(S - 1, 1)
            values(S - 2, 0)
            values(S - 1, 1)


def attend_stage(nc, ident, x_hi_in, x_lo_in, v_in, w_hi_in, w_lo_in, qb, kb, local, out, nb=B):
    NHEAD = nb * HEADS
    KT = N // P
    PAIRS = KT // 2
    STEPS = NCH * PAIRS
    LAG = 3
    QT = N // P
    PIECES = [(k * 512, min(512, N - k * 512)) for k in range((N + 511) // 512)]
    NMX = QT * len(PIECES)
    ROW = 2 * HD
    JOBS = [("k", 0, 0), ("k", 1, 1), ("q", 0, 2), ("k", 2, 3), ("k", 3, 4), ("k", 4, 5), ("k", 5, 6),
            ("q", 1, 10), ("q", 2, 17), ("q", 3, 24), ("q", 4, 32), ("q", 5, 39)]
    NJ = len(JOBS)
    JOB_OF = {(kind, i): n for n, (kind, i, _s) in enumerate(JOBS)}
    JOBS_AT = {s: n for n, (_k, _i, s) in enumerate(JOBS)}
    MAX_AT = {7 + m // 2: (m, m + 1) for m in range(0, NMX, 2)}
    ROWS_AT = {32: 0, 53: 1}
    HQ = QT // 2
    COMB_AT = {PAIRS * c + PAIRS - 1 + LAG + 2: c for c in range(NCH)}
    POOL_SUBS = [n for n in range(STEPS) if n >= 10 and n % 4 == 2]
    ON_POOL = {n: i for i, n in enumerate(POOL_SUBS)}
    DVE_SUBS = [n for n in range(STEPS) if n not in ON_POOL]
    ON_DVE = {n: i for i, n in enumerate(DVE_SUBS)}
    NP_, ND_ = len(POOL_SUBS), len(DVE_SUBS)

    with ExitStack() as ctx:
        def sb(name, shape, dt=F32):
            return ctx.enter_context(nc.sbuf_tensor(f"a_{name}", shape, dt))

        def psum(name, shape):
            return ctx.enter_context(nc.psum_tensor(f"a_{name}", shape, F32))

        def sem(name):
            return ctx.enter_context(nc.semaphore(f"a_{name}"))

        x_hi = sb("x_hi", [P, CT, N], F32R)
        x_lo = sb("x_lo", [P, CT, N], F32R)
        w = sb("w", [P, 2, 2, CT, 4 * HD], F32R)
        q = sb("q", [P, 2, N], F32R)
        k_hi = sb("k_hi", [P, 2, N], F32R)
        k_lo = sb("k_lo", [P, 2, N], F32R)
        v = sb("v", [P, 2, KT, ROW + 2], F32R)
        loc = sb("loc", [ROW, 2, N])
        q_full = sb("q_full", [ROW, 2, CHUNK])
        q_hi = sb("q_hi", [ROW, 2, CHUNK])
        e_full = sb("e_full", [P, 3, 2, CHUNK])
        e_hi = sb("e_hi", [P, 3, 2, CHUNK], F32R)
        e_lo = sb("e_lo", [P, 3, 2, CHUNK], F32R)
        o_t = sb("o_t", [ROW + 1, 2, CHUNK])
        r_sum = sb("r_sum", [P, 2, 3])
        o_tok = sb("o_tok", [P, 2, 3, HD])
        mx_part = sb("mx_part", [P, 2, QT, len(PIECES)])
        mx = sb("mx", [P, 2, QT])
        mx_row = sb("mx_row", [HQ, 2, P])
        low = sb("low", [ROW, 1])
        bias_all = sb("bias_all", [ROW, HEADS, 2])
        bias = sb("bias", [ROW, 2, 2])
        comb = sb("comb", [ROW + 1, HD + 1])

        ps_s = psum("ps_s", [P, 2, 2, 512])
        ps_o = psum("ps_o", [P, 512])
        ps_m = psum("ps_m", [P, 2, 512])
        ps_x = psum("ps_x", [P, 512])

        x_in = [sem(f"x_in{c}") for c in range(NCH)]
        head_in, v_arrived, bias_in, bias_taken = sem("head_in"), sem("v_arrived"), sem("bias_in"), sem("bias_taken")
        made_pool, made_dve = sem("made_pool"), sem("made_dve")
        q_full_made, k_hi_made, q_hi_made = sem("q_full_made"), sem("k_hi_made"), sem("q_hi_made")
        proj_done, k_made, q_made = sem("proj_done"), sem("k_made"), sem("q_made")
        mx_done, mx_red, mx_fin = sem("mx_done"), sem("mx_red"), sem("mx_fin")
        row_turned, row_out, row_in = sem("row_turned"), sem("row_out"), [sem("row_in0"), sem("row_in1")]
        s_done, e_made, e_hi_made = sem("s_done"), sem("e_made"), sem("e_hi_made")
        lo_dve, lo_pool = sem("lo_dve"), sem("lo_pool")
        o_done, o_out, comb_done, r_made, o_made, stored = (sem("o_done"), sem("o_out"), sem("comb_done"),
                                                            sem("r_made"), sem("o_made"), sem("stored"))

        x_parts = [(x_hi, x_hi_in.rearrange("b (t p) n -> b p t n", p=P)),
                   (x_lo, x_lo_in.rearrange("b (t p) n -> b p t n", p=P))]
        loc_in = local.rearrange("b (h d) n -> b h d n", d=HD)
        v_v = v_in.rearrange("b h (t p) n -> b h p t n", p=P)
        out_v = out.rearrange("b (c t p) (h d) -> b h c p t d", p=P, t=3, d=HD)

        def wait_lo(eng, h, n, less=0):
            if n in ON_POOL:
                at_least(eng, lo_pool, h * NP_ + ON_POOL[n] + 1)
            else:
                at_least(eng, lo_dve, h * ND_ + ON_DVE[n] + 1)

        def back(h, n, d):
            return (h, n - d) if n >= d else (h - 1, n - d + STEPS)

        def bodies(body, eng):
            body(-1, 1, main=False, prev=False, nxt=True)
            body(0, 0, main=True, prev=False, nxt=True)
            if NHEAD > 2:
                with eng.Fori(0, (NHEAD - 2) // 2) as i:
                    body(i * 2 + 1, 1, main=True, prev=True, nxt=True)
                    body(i * 2 + 2, 0, main=True, prev=True, nxt=True)
            body(NHEAD - 1, 1, main=True, prev=True, nxt=False)
            body(NHEAD, 0, main=False, prev=True, nxt=False)

        block = ctx.enter_context(nc.Block())

        @block.sync
        def _(sp):
            def load_head(h):
                for part, src in ((0, w_hi_in), (1, w_lo_in)):
                    sp.dma_start(f32(w[:, h % 2, part]), src[h % HEADS]).then_inc(head_in, 16)
                for twice in range(2):
                    sp.dma_start(loc[twice * HD:(twice + 1) * HD, h % 2], loc_in[h // HEADS, h % HEADS]).then_inc(head_in, 16)

            def load_chunk(b, c):
                for part, src in x_parts:
                    sp.dma_start(f32(part[:, :, c * CHUNK:(c + 1) * CHUNK]),
                                 src[b, :, :, c * CHUNK:(c + 1) * CHUNK]).then_inc(x_in[c], 16)

            for col, src in ((0, qb), (1, kb)):
                for half in range(2):
                    sp.dma_start(bias_all[half * HD:(half + 1) * HD, :, col:col + 1],
                                 src.rearrange("(h d one) -> d h one", d=HD, one=1),
                                 allow_slow_non_contiguous=True).then_inc(bias_in, 16)
            load_head(0)
            for c in range(NCH):
                load_chunk(0, c)

            def step(g, more=True, first=False):
                if more:
                    if not first:
                        sp.wait_ge(q_full_made, g * NCH)
                    sp.wait_ge(head_in, (g + 1) * 64)
                    load_head(g + 1)
                if not first:
                    sp.wait_ge(v_arrived, g * 16)
                    at_least(sp, o_done, (g - 1) * STEPS)
                sp.dma_start(f32(v[:, g % 2, :, 0:ROW]), v_v[g // HEADS, g % HEADS]).then_inc(v_arrived, 16)

            def next_image(b):
                last = (b + 1) * HEADS - 1
                for c in range(NCH):
                    sp.wait_ge(proj_done, last * NJ + max(JOB_OF["q", c], JOB_OF["k", c]) + 1)
                    load_chunk(b + 1, c)

            step(0, first=True)
            step(1)
            with sp.Fori(2, HEADS - 1) as g:
                step(g)
            step(HEADS - 1, more=nb > 1)
            if nb > 1:
                next_image(0)
                if nb > 2:
                    with sp.Fori(1, nb - 1) as b:
                        with sp.Fori(0, HEADS) as g:
                            step(b * HEADS + g)
                        next_image(b)
                with sp.Fori((nb - 1) * HEADS, NHEAD - 1) as g:
                    step(g)
                step(NHEAD - 1, more=False)

        @block.gpsimd
        def _(pool):
            pool.memset(comb[:], 0.0).then_inc(made_pool, 1)
            pool.memset(low[:], 1.0).then_inc(made_pool, 1)
            pool.wait_ge(made_pool, 2)
            pool.affine_select(out=low[:], in_=low[:], compare_op=ALU.is_ge, fill=0.0, base=-HD, pattern=[[0, 1]],
                               channel_multiplier=1).then_inc(made_pool, 1)
            pool.affine_select(out=comb[:, 0:HD], in_=comb[:, 0:HD], compare_op=ALU.not_equal, fill=1.0, base=0,
                               pattern=[[-1, HD]], channel_multiplier=1).then_inc(made_pool, 1)
            pool.wait_ge(made_pool, 4)
            pool.affine_select(out=comb[:], in_=comb[:], compare_op=ALU.not_equal, fill=1.0, base=-HD,
                               pattern=[[-1, HD + 1]], channel_multiplier=1).then_inc(made_pool, 1)

            def body(h, par, main, prev, nxt):
                if not main:
                    return
                for n in POOL_SUBS:
                    pool.wait_ge(e_hi_made, h * STEPS + n + 1)
                    at_least(pool, o_done, h * STEPS + n - 2)
                    pool.tensor_tensor(e_lo[:, n % 3], e_full[:, n % 3], f32(e_hi[:, n % 3]),
                                       ALU.subtract).then_inc(lo_pool, 1)

            bodies(body, pool)

        @block.scalar
        def _(act):
            act.wait_ge(bias_in, 64)
            act.wait_ge(made_pool, 5)
            act.wait_ge(made_dve, 4)

            def project(h, par, n):
                kind, i, _s = JOBS[n]
                cols = slice(i * CHUNK, (i + 1) * CHUNK)
                if n == 0:
                    at_least(act, s_done, (h - 1) * STEPS)
                    act.wait_ge(bias_taken, h + 1)
                if kind == "k":
                    act.wait_ge(proj_done, h * NJ + n + 1)
                    act.activation(k_hi[0:ROW, par, cols], ps_x[0:ROW, 0:CHUNK], ACT.Identity,
                                   bias=bias[:, par, 1:2]).then_inc(k_hi_made, 1)
                else:
                    act.wait_ge(q_full_made, h * NCH + i + 1)
                    at_least(act, q_made, h * NCH + i - 1)
                    act.activation(f32r(q_hi[:, i % 2]), q_full[:, i % 2], ACT.Copy, scale=low[:, 0:1]).then_inc(q_hi_made, 1)

            def hi_of(h, n):
                act.wait_ge(e_made, h * STEPS + n + 1)
                at_least(act, o_done, h * STEPS + n - 2)
                act.activation(e_hi[:, n % 3], e_full[:, n % 3], ACT.Copy).then_inc(e_hi_made, 1)

            def take_out(h, c):
                act.wait_ge(o_done, h * STEPS + PAIRS * (c + 1))
                at_least(act, comb_done, h * NCH + c - 1)
                act.activation(o_t[:, c % 2], ps_o[0:ROW + 1, 0:CHUNK], ACT.Copy).then_inc(o_out, 1)

            def store(h, c):
                act.wait_ge(o_made, h * NCH + c + 1)
                at_least(act, stored, (h * NCH + c) * 16)
                act.dma_start(out_v[h // HEADS, h % HEADS, c], o_tok[:, c % 2]).then_inc(stored, 16)

            def body(h, par, main, prev, nxt):
                for n in range(STEPS):
                    c, r = divmod(n - LAG - 1, PAIRS)
                    if main and n >= LAG + PAIRS and r == PAIRS - 1:
                        take_out(h, c)
                    if prev and n == LAG:
                        take_out(h - 1, NCH - 1)
                    if main:
                        act.wait_ge(s_done, h * STEPS + n + 1)
                        at_least(act, e_hi_made, h * STEPS + n - 2)
                        p_h, p_n = back(h, n, 3)
                        if prev or n >= 3:
                            wait_lo(act, p_h, p_n)
                        act.activation(e_full[:, n % 3], ps_s[:, n % 2, :, 0:CHUNK], ACT.Exp,
                                       scale=float(HD) ** -0.5).then_inc(e_made, 1)
                        if n >= 1:
                            hi_of(h, n - 1)
                    if n == 0 and prev:
                        hi_of(h - 1, STEPS - 1)
                    if nxt and n == 0:
                        act.activation(bias[:, 1 - par], bias_all[:, bass.ds((h + 1) % HEADS, 1), :].rearrange("p o c -> p (o c)"),
                                       ACT.Copy).then_inc(bias_taken, 1)
                    if nxt and n in JOBS_AT:
                        project(h + 1, 1 - par, JOBS_AT[n])
                    if nxt and n in ROWS_AT:
                        half = ROWS_AT[n]
                        act.wait_ge(row_turned, (h + 1) * 2 + half + 1)
                        at_least(act, row_in[half], (h + 1) * 16)
                        act.activation(f32r(mx_row[:, half]), ps_x[0:HQ, 0:P], ACT.Copy, scale=-1.0).then_inc(row_out, 1)
                        act.wait_ge(row_out, (h + 1) * 2 + half + 1)
                        act.dma_start(f32(q[ROW:ROW + 1, 1 - par, half * (N // 2):(half + 1) * (N // 2)]).rearrange(
                            "o (t p) -> o t p", p=P), mx_row[:, half]).then_inc(row_in[half], 16)
                    if main and n - 4 in COMB_AT:
                        store(h, COMB_AT[n - 4])
                    if prev and n - 4 + STEPS in COMB_AT:
                        store(h - 1, COMB_AT[n - 4 + STEPS])

            bodies(body, act)
            act.wait_ge(stored, NHEAD * NCH * 16)

        @block.vector
        def _(dve):
            dve.memset(f32(k_hi[ROW:ROW + 1]), 1.0).then_inc(made_dve, 1)
            dve.memset(f32(k_lo[ROW:ROW + 1]), 0.0).then_inc(made_dve, 1)
            dve.memset(f32(v[:, :, :, ROW:ROW + 1]), 1.0).then_inc(made_dve, 1)
            dve.memset(f32(q[ROW:ROW + 1]), 0.0).then_inc(made_dve, 1)
            dve.wait_ge(bias_in, 64)

            def project(h, par, n):
                kind, i, _s = JOBS[n]
                cols = slice(i * CHUNK, (i + 1) * CHUNK)
                if kind == "k":
                    dve.wait_ge(k_hi_made, h * NCH + i + 1)
                    dve.scalar_tensor_tensor(out=k_lo[0:ROW, par, cols], in0=ps_x[0:ROW, 0:CHUNK],
                                             scalar=bias[:, par, 1:2], in1=f32(k_hi[0:ROW, par, cols]), op0=ALU.add,
                                             op1=ALU.subtract).then_inc(k_made, 1)
                else:
                    dve.wait_ge(proj_done, h * NJ + n + 1)
                    dve.wait_ge(bias_taken, h + 1)
                    at_least(dve, q_made, h * NCH + i - 1)
                    dve.scalar_tensor_tensor(out=q_full[:, i % 2], in0=ps_x[0:ROW, 0:CHUNK], scalar=bias[:, par, 0:1],
                                             in1=loc[:, par, cols], op0=ALU.add, op1=ALU.add).then_inc(q_full_made, 1)

            def split_q(h, par, i):
                dve.wait_ge(q_hi_made, h * NCH + i + 1)
                dve.tensor_tensor(q[0:ROW, par, i * CHUNK:(i + 1) * CHUNK], q_full[:, i % 2], q_hi[:, i % 2],
                                  ALU.subtract).then_inc(q_made, 1)

            def lo_of(h, n):
                dve.wait_ge(e_hi_made, h * STEPS + n + 1)
                at_least(dve, o_done, h * STEPS + n - 2)
                dve.tensor_tensor(e_lo[:, n % 3], e_full[:, n % 3], f32(e_hi[:, n % 3]), ALU.subtract).then_inc(lo_dve, 1)

            def maxima(h, par, m):
                t, k = divmod(m, len(PIECES))
                if m == 0:
                    at_least(dve, mx_fin, (h - 1) * 2)
                dve.wait_ge(mx_done, h * NMX + m + 1)
                dve.tensor_reduce(mx_part[:, par, t, k:k + 1], ps_m[:, m % 2, 0:PIECES[k][1]], AX.X,
                                  ALU.max).then_inc(mx_red, 1)

            def normalise(h, c):
                dve.wait_ge(comb_done, h * NCH + c + 1)
                at_least(dve, o_made, h * NCH + c - 1)
                sums = ps_x[:, 0:3 * (HD + 1)].rearrange("p (t d) -> p t d", d=HD + 1)
                dve.reciprocal(r_sum[:, c % 2, :].unsqueeze(2), sums[:, :, HD:HD + 1]).then_inc(r_made, 1)
                dve.wait_ge(r_made, h * NCH + c + 1)
                at_least(dve, stored, (h * NCH + c - 1) * 16)
                dve.tensor_tensor(o_tok[:, c % 2], sums[:, :, 0:HD],
                                  r_sum[:, c % 2, :].unsqueeze(2).to_broadcast([P, 3, HD]), ALU.mult).then_inc(o_made, 1)

            def body(h, par, main, prev, nxt):
                for n in range(STEPS):
                    if prev and n < 2:
                        l_n = n - 2 + STEPS
                        if l_n in ON_DVE:
                            lo_of(h - 1, l_n)
                    if main and n >= 2 and n - 2 in ON_DVE:
                        lo_of(h, n - 2)
                    if nxt and n in JOBS_AT:
                        project(h + 1, 1 - par, JOBS_AT[n])
                    if main and n in COMB_AT:
                        normalise(h, COMB_AT[n])
                    if prev and n + STEPS in COMB_AT:
                        normalise(h - 1, COMB_AT[n + STEPS])
                    if nxt and n in MAX_AT:
                        for m in MAX_AT[n]:
                            maxima(h + 1, 1 - par, m)
                    if nxt and n - 1 in JOBS_AT and JOBS[JOBS_AT[n - 1]][0] == "q":
                        split_q(h + 1, 1 - par, JOBS[JOBS_AT[n - 1]][1])
                    if nxt and n in ROWS_AT:
                        half = ROWS_AT[n]
                        tiles = slice(half * HQ, (half + 1) * HQ)
                        dve.wait_ge(mx_red, (h + 1) * NMX + (half + 1) * NMX // 2)
                        at_least(dve, row_turned, h * 2)
                        dve.tensor_reduce(mx[:, 1 - par, tiles], mx_part[:, 1 - par, tiles], AX.X,
                                          ALU.max).then_inc(mx_fin, 1)

            bodies(body, dve)

        @block.tensor
        def _(pe):
            pe.wait_ge(made_pool, 5)
            pe.wait_ge(made_dve, 4)
            free = [None]

            def take_ps_x(sem_, count):
                if free[0] is not None:
                    at_least(pe, *free[0])
                free[0] = (sem_, count)

            def project(h, par, n):
                kind, i, _s = JOBS[n]
                take_ps_x(k_made if kind == "k" else q_full_made, h * NCH + i + 1)
                if n == 0:
                    pe.wait_ge(head_in, (h + 1) * 64)
                pe.wait_ge(x_in[i], (h // HEADS + 1) * 32)
                off = 0 if kind == "q" else ROW
                cols = slice(i * CHUNK, (i + 1) * CHUNK)
                for j, (wp, xp) in enumerate(((0, x_hi), (0, x_lo), (1, x_hi))):
                    for c in range(CT):
                        last = pe.matmul(ps_x[0:ROW, 0:CHUNK], w[:, par, wp, c, off:off + ROW], xp[:, c, cols],
                                         start=j == 0 and c == 0, stop=j == 2 and c == CT - 1)
                last.then_inc(proj_done, 1)

            def maxima(h, par, m):
                t, k = divmod(m, len(PIECES))
                k0, kn = PIECES[k]
                if m == 0:
                    pe.wait_ge(k_made, (h + 1) * NCH)
                if m % (3 * len(PIECES)) == 0:
                    pe.wait_ge(q_made, h * NCH + t // 3 + 1)
                at_least(pe, mx_red, h * NMX + m - 1)
                pe.matmul(ps_m[:, m % 2, 0:kn], q[0:ROW, par, t * P:(t + 1) * P], k_hi[0:ROW, par, k0:k0 + kn],
                          start=True, stop=True).then_inc(mx_done, 1)

            def scores(h, par, n):
                c, r = divmod(n, PAIRS)
                if n in (0, STEPS // 2):
                    pe.wait_ge(row_in[n * 2 // STEPS], (h + 1) * 16)
                at_least(pe, e_made, h * STEPS + n - 1)
                for t in range(2):
                    for part in (k_hi, k_lo):
                        last = pe.matmul(ps_s[:, n % 2, t, 0:CHUNK],
                                         part[0:ROW + 1, par, (2 * r + t) * P:(2 * r + t + 1) * P],
                                         q[0:ROW + 1, par, c * CHUNK:(c + 1) * CHUNK],
                                         start=part is k_hi, stop=part is k_lo)
                last.then_inc(s_done, 1)

            def products(h, par, n):
                c, r = divmod(n, PAIRS)
                if n == 0:
                    pe.wait_ge(v_arrived, (h + 1) * 16)
                if r == 0:
                    at_least(pe, o_out, h * NCH + c)
                pe.wait_ge(e_hi_made, h * STEPS + n + 1)
                wait_lo(pe, h, n)
                for j, part in enumerate((e_hi, e_lo)):
                    for t in range(2):
                        last = pe.matmul(ps_o[0:ROW + 1, 0:CHUNK], v[:, par, 2 * r + t, 0:ROW + 1], part[:, n % 3, t],
                                         start=r == 0 and j == 0 and t == 0, stop=r == PAIRS - 1 and j == 1 and t == 1)
                last.then_inc(o_done, 1)

            def combine(h, c):
                take_ps_x(o_made, h * NCH + c + 1)
                pe.wait_ge(o_out, h * NCH + c + 1)
                for t in range(3):
                    last = pe.matmul(ps_x[:, t * (HD + 1):(t + 1) * (HD + 1)], o_t[:, c % 2, t * P:(t + 1) * P],
                                     comb[:], start=True, stop=True)
                last.then_inc(comb_done, 1)

            def body(h, par, main, prev, nxt):
                if main:
                    free[0] = (row_out, (h + 1) * 2)
                for n in range(STEPS):
                    if main:
                        scores(h, par, n)
                    if nxt and n in MAX_AT:
                        maxima(h + 1, 1 - par, MAX_AT[n][0])
                    if nxt and n in JOBS_AT:
                        project(h + 1, 1 - par, JOBS_AT[n])
                    if main and n in COMB_AT:
                        combine(h, COMB_AT[n])
                    if prev and n + STEPS in COMB_AT:
                        combine(h - 1, COMB_AT[n + STEPS])
                    if prev and n < LAG:
                        products(h - 1, 1 - par, n - LAG + STEPS)
                    if main and n >= LAG:
                        products(h, par, n - LAG)
                    if nxt and n in MAX_AT:
                        maxima(h + 1, 1 - par, MAX_AT[n][1])
                    if nxt and n in ROWS_AT:
                        half = ROWS_AT[n]
                        take_ps_x(row_out, (h + 1) * 2 + half + 1)
                        pe.wait_ge(mx_fin, (h + 1) * 2 + half + 1)
                        pe.transpose(ps_x[0:HQ, 0:P], mx[:, 1 - par, half * HQ:(half + 1) * HQ],
                                     ident[:]).then_inc(row_turned, 1)

            bodies(body, pe)


def project_stage(nc, ident, o, w_hi_in, w_lo_in, v_bias, p_bias, x, y, nb=B):
    S = nb * NCH
    T3 = CHUNK // P
    with ExitStack() as ctx:
        def sb(name, shape, dt=F32):
            return ctx.enter_context(nc.sbuf_tensor(f"p_{name}", shape, dt))

        def psum(name, shape):
            return ctx.enter_context(nc.psum_tensor(f"p_{name}", shape, F32))

        def sem(name):
            return ctx.enter_context(nc.semaphore(f"p_{name}"))

        w_hi = sb("w_hi", [P, CT, C], F32R)
        w_lo = sb("w_lo", [P, CT, C], F32R)
        vb = sb("vb", [P, CT])
        pb = sb("pb", [P, CT])
        o_tok = sb("o_tok", [P, 2, T3, C])
        res = sb("res", [P, 2, CT, CHUNK])
        o_hi = sb("o_hi", [P, 2, CT, CHUNK], F32R)
        o_lo = sb("o_lo", [P, 2, CT, CHUNK], F32R)
        yt = sb("yt", [P, 2, CT, CHUNK])
        ps_t = psum("ps_t", [P, CT, 512])
        ps_y = psum("ps_y", [P, CT, 512])
        par_in, in_, turned = sem("par_in"), sem("in"), sem("turned")
        hi_made, lo_made, y_done, y_made, stored = (sem("hi_made"), sem("lo_made"), sem("y_done"), sem("y_made"),
                                                    sem("stored"))
        o_v = o.rearrange("b (s t p) c -> (b s) p t c", t=T3, p=P)
        x_v = x.rearrange("b (t p) n -> b p t n", p=P)
        y_v = y.rearrange("b (t p) n -> b p t n", p=P)
        block = ctx.enter_context(nc.Block())

        @block.sync
        def _(sp):
            sp.dma_start(f32(w_hi[:]).rearrange("p t n -> p (t n)"), w_hi_in).then_inc(par_in, 16)
            sp.dma_start(f32(w_lo[:]).rearrange("p t n -> p (t n)"), w_lo_in).then_inc(par_in, 16)
            sp.dma_start(vb[:], v_bias.rearrange("(t p) -> p t", p=P), allow_slow_non_contiguous=True).then_inc(par_in, 16)
            sp.dma_start(pb[:], p_bias.rearrange("(t p) -> p t", p=P), allow_slow_non_contiguous=True).then_inc(par_in, 16)
            for a, z in segments(S + 2, [1, 2, 3, S]):
                with sp.Fori(a, z) as it:
                    if a < S:
                        if a >= 1:
                            sp.wait_ge(in_, it * 32)
                        if a >= 2:
                            sp.wait_ge(y_made, (it - 1) * CT)
                        sp.dma_start(o_tok[:, it % 2], o_v[it]).then_inc(in_, 16)
                        sp.dma_start(res[:, it % 2], x_v[it // NCH, :, :, bass.ds((it % NCH) * CHUNK, CHUNK)]).then_inc(in_, 16)
                    if a >= 2:
                        s = it - 2
                        if a >= 3:
                            sp.wait_ge(stored, s * 16)
                        sp.wait_ge(y_made, s * CT + CT)
                        sp.dma_start(y_v[s // NCH, :, :, bass.ds((s % NCH) * CHUNK, CHUNK)], yt[:, s % 2]).then_inc(stored, 16)
            sp.wait_ge(stored, S * 16)

        @block.scalar
        def _(act):
            act.wait_ge(par_in, 64)
            for a, z in segments(S, [2]):
                with act.Fori(a, z) as it:
                    if a >= 2:
                        act.wait_ge(y_done, (it - 1) * CT)
                    for t in range(CT):
                        act.wait_ge(turned, it * CT + t + 1)
                        act.activation(o_hi[:, it % 2, t], ps_t[:, t, 0:CHUNK], ACT.Identity,
                                       bias=vb[:, t:t + 1]).then_inc(hi_made, 1)

        @block.vector
        def _(dve):
            dve.wait_ge(par_in, 64)
            for a, z in segments(S + 1, [1, 2, 3, S]):
                with dve.Fori(a, z) as it:
                    if a < S:
                        for t in range(CT):
                            dve.wait_ge(hi_made, it * CT + t + 1)
                            dve.scalar_tensor_tensor(out=o_lo[:, it % 2, t], in0=ps_t[:, t, 0:CHUNK], scalar=vb[:, t:t + 1],
                                                     in1=f32(o_hi[:, it % 2, t]), op0=ALU.add,
                                                     op1=ALU.subtract).then_inc(lo_made, 1)
                    if a >= 1:
                        s = it - 1
                        if a >= 3:
                            dve.wait_ge(stored, (s - 1) * 16)
                        for t in range(CT):
                            dve.wait_ge(y_done, s * CT + t + 1)
                            dve.scalar_tensor_tensor(out=yt[:, s % 2, t], in0=ps_y[:, t, 0:CHUNK], scalar=pb[:, t:t + 1],
                                                     in1=res[:, s % 2, t], op0=ALU.add, op1=ALU.add).then_inc(y_made, 1)

        @block.tensor
        def _(pe):
            pe.wait_ge(par_in, 64)

            def turn(s, k):
                pe.wait_ge(in_, (s + 1) * 32)
                at_least(pe, lo_made, s * CT)
                for c in range(CT):
                    for t in range(T3):
                        last = pe.transpose(ps_t[:, c, t * P:(t + 1) * P], o_tok[:, k, t, c * P:(c + 1) * P], ident[:])
                    last.then_inc(turned, 1)

            def mul(s, k):
                pe.wait_ge(lo_made, (s + 1) * CT)
                for m in range(CT):
                    at_least(pe, y_made, (s - 1) * CT + m + 1)
                    for j, (wp, op) in enumerate(((w_hi, o_hi), (w_hi, o_lo), (w_lo, o_hi))):
                        for c in range(CT):
                            last = pe.matmul(ps_y[:, m, 0:CHUNK], wp[:, c, m * P:(m + 1) * P], op[:, k, c],
                                             start=j == 0 and c == 0, stop=j == 2 and c == CT - 1)
                    last.then_inc(y_done, 1)

            turn(0, 0)
            turn(1, 1)
            mul(0, 0)
            with pe.Fori(1, S // 2) as i:
                turn(i * 2, 0)
                mul(i * 2 - 1, 1)
                turn(i * 2 + 1, 1)
                mul(i * 2, 0)
            mul(S - 1, 1)


def mlp_stage(nc, ident, ones, n1, w1_hi_in, w1_lo_in, w2_hi_in, w2_lo_in, b1, grn_g, grn_b, b2, y, out, nb=B):
    with ExitStack() as ctx:
        def sb(name, shape, dt=F32):
            return ctx.enter_context(nc.sbuf_tensor(f"m_{name}", shape, dt))

        def psum(name, shape):
            return ctx.enter_context(nc.psum_tensor(f"m_{name}", shape, F32))

        def sem(name):
            return ctx.enter_context(nc.semaphore(f"m_{name}"))

        NF = NCH * FT
        NC3 = NCH * CT
        w1_hi, w1_lo = sb("w1_hi", [P, CT, FH], F32R), sb("w1_lo", [P, CT, FH], F32R)
        w2_hi, w2_lo = sb("w2_hi", [P, FT, C], F32R), sb("w2_lo", [P, FT, C], F32R)
        hid = sb("hid", [P, FT, N])
        io = sb("io", [P, CT, CHUNK])
        x_hi, x_lo = sb("x_hi", [P, CT, CHUNK], F32R), sb("x_lo", [P, CT, CHUNK], F32R)
        h_hi, h_lo = sb("h_hi", [P, 2, CHUNK], F32R), sb("h_lo", [P, 2, CHUNK], F32R)
        junk = sb("junk", [P, CHUNK])
        par = sb("par", [P, 3, FT])
        bias2 = sb("bias2", [P, CT])
        sq = sb("sq", [P, FT, NCH])
        tot, gx, nx, gn, scale = (sb(n, [P, FT]) for n in ("tot", "gx", "nx", "gn", "scale"))
        mean = sb("mean", [P, 3])
        ps_sum, ps_h, ps_y = psum("ps_sum", [P, FT]), psum("ps_h", [P, 2, 512]), psum("ps_y", [P, CT, 512])
        par_in, x_in, res_in = sem("par_in"), sem("x_in"), sem("res_in")
        x_hi_made, x_lo_made = sem("x_hi_made"), sem("x_lo_made")
        h_done, h_made, sq_made = sem("h_done"), sem("h_made"), sem("sq_made")
        tot_made, gx_made, gsum_done, grn_step = sem("tot_made"), sem("gx_made"), sem("gsum_done"), sem("grn_step")
        scaled, h_hi_made, h_lo_made = sem("scaled"), sem("h_hi_made"), sem("h_lo_made")
        h_used, y_done, y_made, stored = sem("h_used"), sem("y_done"), sem("y_made"), sem("stored")
        USES = FT - 1

        def slot_used(eng, b, n):
            c, f = divmod(n - 2, FT)
            if n < 2:
                at_least(eng, y_done, b * NC3)
            elif f == FT - 1:
                eng.wait_ge(y_done, (b * NCH + c + 1) * CT)
            else:
                eng.wait_ge(h_used, (b * NCH + c) * USES + f + 1)

        GRN = 6

        n1_v = n1.rearrange("b (t p) (s n) -> b s p t n", p=P, n=CHUNK)
        y_v = y.rearrange("b (t p) (s n) -> b s p t n", p=P, n=CHUNK)
        out_v = out.rearrange("b (t p) (s n) -> b s p t n", p=P, n=CHUNK)

        def images(eng, *parts):
            for part in parts:
                part(0)
            if nb > 1:
                with eng.Fori(1, nb) as b:
                    for part in parts:
                        with eng.Fori(b, b + 1) as own:
                            part(own)

        block = ctx.enter_context(nc.Block())

        @block.sync
        def _(sp):
            for dst, src in ((w1_hi, w1_hi_in), (w1_lo, w1_lo_in), (w2_hi, w2_hi_in), (w2_lo, w2_lo_in)):
                sp.dma_start(f32(dst[:]).rearrange("p t n -> p (t n)"), src).then_inc(par_in, 16)
            for i, src in enumerate((b1, grn_g, grn_b)):
                sp.dma_start(par[:, i], src.rearrange("(t p) -> p t", p=P), allow_slow_non_contiguous=True).then_inc(par_in, 16)
            sp.dma_start(bias2[:], b2.rearrange("(t p) -> p t", p=P), allow_slow_non_contiguous=True).then_inc(par_in, 16)

            def inputs(b):
                for c in range(NCH):
                    if c == 0:
                        at_least(sp, stored, b * NCH * 16)
                    else:
                        sp.wait_ge(x_lo_made, (b * NCH + c) * CT)
                    sp.dma_start(io[:], n1_v[b, c]).then_inc(x_in, 16)

            def results(b):
                for c in range(NCH):
                    if c == 0:
                        sp.wait_ge(x_lo_made, (b + 1) * NC3)
                    at_least(sp, stored, (b * NCH + c) * 16)
                    sp.dma_start(io[:], y_v[b, c]).then_inc(res_in, 16)
                    sp.wait_ge(y_made, b * NC3 + (c + 1) * CT)
                    sp.dma_start(out_v[b, c], io[:]).then_inc(stored, 16)

            images(sp, inputs, results)
            sp.wait_ge(stored, nb * NCH * 16)

        @block.scalar
        def _(act):
            act.wait_ge(par_in, 128)

            def up(b):
                for c in range(NCH):
                    at_least(act, h_done, (b * NCH + c) * FT)
                    act.wait_ge(x_in, (b * NCH + c + 1) * 16)
                    for t in range(CT):
                        act.activation(x_hi[:, t], io[:, t], ACT.Copy).then_inc(x_hi_made, 1)
                    if c == 0:
                        at_least(act, h_lo_made, b * NF)
                        at_least(act, h_hi_made, b * NF)
                    for f in range(FT):
                        n = c * FT + f
                        act.wait_ge(h_done, b * NF + n + 1)
                        act.activation(hid[:, f, c * CHUNK:(c + 1) * CHUNK], ps_h[:, f % 2, 0:CHUNK], ACT.Gelu,
                                       bias=par[:, 0, f:f + 1]).then_inc(h_made, 1)

            def down(b):
                act.wait_ge(tot_made, b + 1)
                act.activation(gx[:], tot[:], ACT.Sqrt).then_inc(gx_made, 1)
                for n in range(NF):
                    c, f = divmod(n, FT)
                    act.wait_ge(scaled, b * NF + n + 1)
                    slot_used(act, b, n)
                    act.activation(h_hi[:, n % 2], hid[:, f, c * CHUNK:(c + 1) * CHUNK], ACT.Copy).then_inc(h_hi_made, 1)

            images(act, up, down)

        @block.vector
        def _(dve):
            dve.wait_ge(par_in, 128)

            def grn(b):
                dve.wait_ge(sq_made, (b + 1) * NF)
                dve.tensor_reduce(tot[:], sq[:], AX.X, ALU.add).then_inc(tot_made, 1)
                dve.wait_ge(gsum_done, b + 1)
                dve.tensor_reduce(mean[:, 0:1], ps_sum[:], AX.X, ALU.add).then_inc(grn_step, 1)
                at = b * GRN
                dve.wait_ge(grn_step, at + 1)
                dve.tensor_scalar(mean[:, 1:2], mean[:, 0:1], 1.0 / FH, 1e-6, ALU.mult, ALU.add).then_inc(grn_step, 1)
                dve.wait_ge(grn_step, at + 2)
                dve.reciprocal(mean[:, 2:3], mean[:, 1:2]).then_inc(grn_step, 1)
                dve.wait_ge(grn_step, at + 3)
                dve.tensor_scalar(nx[:], gx[:], mean[:, 2:3], None, ALU.mult).then_inc(grn_step, 1)
                dve.wait_ge(grn_step, at + 4)
                dve.tensor_tensor(gn[:], nx[:], par[:, 1], ALU.mult).then_inc(grn_step, 1)
                dve.wait_ge(grn_step, at + 5)
                dve.tensor_scalar(scale[:], gn[:], 1.0, None, ALU.add).then_inc(grn_step, 1)

            def up(b):
                for c in range(NCH):
                    for t in range(CT):
                        dve.wait_ge(x_hi_made, (b * NCH + c) * CT + t + 1)
                        dve.tensor_tensor(x_lo[:, t], io[:, t], f32(x_hi[:, t]), ALU.subtract).then_inc(x_lo_made, 1)
                    for f in range(FT):
                        n = c * FT + f
                        dve.wait_ge(h_made, b * NF + n + 1)
                        at_least(dve, sq_made, b * NF + n)
                        part = hid[:, f, c * CHUNK:(c + 1) * CHUNK]
                        dve.tensor_tensor_reduce(junk[:], part, part, 1.0, 0.0, ALU.mult, ALU.add,
                                                 sq[:, f, c:c + 1]).then_inc(sq_made, 1)

            def affine(b, n):
                c, f = divmod(n, FT)
                part = hid[:, f, c * CHUNK:(c + 1) * CHUNK]
                dve.tensor_scalar(part, part, scale[:, f:f + 1], par[:, 2, f:f + 1], ALU.mult, ALU.add).then_inc(scaled, 1)

            def down(b):
                grn(b)
                dve.wait_ge(grn_step, (b + 1) * GRN)
                affine(b, 0)
                for c in range(NCH):
                    for f in range(FT):
                        n = c * FT + f
                        if n + 1 < NF:
                            affine(b, n + 1)
                        dve.wait_ge(h_hi_made, b * NF + n + 1)
                        slot_used(dve, b, n)
                        dve.tensor_tensor(h_lo[:, n % 2], hid[:, f, c * CHUNK:(c + 1) * CHUNK], f32(h_hi[:, n % 2]),
                                          ALU.subtract).then_inc(h_lo_made, 1)
                    dve.wait_ge(res_in, (b * NCH + c + 1) * 16)
                    for t in range(CT):
                        dve.wait_ge(y_done, (b * NCH + c) * CT + t + 1)
                        dve.scalar_tensor_tensor(out=io[:, t], in0=ps_y[:, t, 0:CHUNK], scalar=bias2[:, t:t + 1],
                                                 in1=io[:, t], op0=ALU.add, op1=ALU.add).then_inc(y_made, 1)

            images(dve, up, down)

        @block.tensor
        def _(pe):
            pe.wait_ge(par_in, 128)

            def up(b, c):
                for f in range(FT):
                    n = c * FT + f
                    if f == 0:
                        pe.wait_ge(x_lo_made, (b * NCH + c + 1) * CT)
                    at_least(pe, h_made, b * NF + n - 1)
                    for j, (wp, xp) in enumerate(((w1_hi, x_hi), (w1_hi, x_lo), (w1_lo, x_hi))):
                        for t in range(CT):
                            last = pe.matmul(ps_h[:, f % 2, 0:CHUNK], wp[:, t, f * P:(f + 1) * P], xp[:, t],
                                             start=j == 0 and t == 0, stop=j == 2 and t == CT - 1)
                    last.then_inc(h_done, 1)

            def down(b, c):
                for f in range(FT):
                    n = c * FT + f
                    pe.wait_ge(h_hi_made, b * NF + n + 1)
                    pe.wait_ge(h_lo_made, b * NF + n + 1)
                    for m in range(CT):
                        if f == 0:
                            at_least(pe, y_made, (b * NCH + c - 1) * CT + m + 1)
                        for j, (wp, hp) in enumerate(((w2_hi, h_hi), (w2_hi, h_lo), (w2_lo, h_hi))):
                            last = pe.matmul(ps_y[:, m, 0:CHUNK], wp[:, f, m * P:(m + 1) * P], hp[:, n % 2],
                                             start=f == 0 and j == 0, stop=f == FT - 1 and j == 2)
                        if f == FT - 1:
                            last.then_inc(y_done, 1)
                    if f < FT - 1:
                        last.then_inc(h_used, 1)

            def all_up(b):
                for c in range(NCH):
                    up(b, c)

            def all_down(b):
                pe.wait_ge(gx_made, b + 1)
                at_least(pe, grn_step, b * GRN)
                pe.matmul(ps_sum[:], ones[:], gx[:], start=True, stop=True).then_inc(gsum_done, 1)
                for c in range(NCH):
                    down(b, c)

            images(pe, all_up, all_down)


def build(nc, a, out):
    def scratch(name, shape):
        return nc.dram_tensor(name, shape, F32, kind="Internal").ap()

    x_hi, x_lo, v = scratch("x_hi", (B, C, N)), scratch("x_lo", (B, C, N)), scratch("v", (B, HEADS, N, 2 * HD))
    local, normed1 = scratch("local", (B, C, N)), scratch("normed1", (B, C, N))
    o, y = scratch("o", (B, N, C)), scratch("y", (B, C, N))
    pairs = {}
    for name in ("w_qk", "w_v", "w_proj", "w_up", "w_down"):
        pairs[name] = scratch(name + "_hi", a[name].shape), scratch(name + "_lo", a[name].shape)
    flat = a["x"].rearrange("b c h w -> b c (h w)")
    with ExitStack() as ctx:
        ident, cmask, ones = shared_consts(nc, ctx)
        split_stage(nc, "s", [(a["w_qk"][h], pairs["w_qk"][0][h], pairs["w_qk"][1][h]) for h in range(HEADS)]
                    + [(a[n], *pairs[n]) for n in ("w_v", "w_proj", "w_up", "w_down")])
        conv_stage(nc, "c0", ident, cmask, a["x"], a["taps0"],
                   [a["bn_gamma"], a["bn_beta"], a["bn_mean"], a["bn_var"]], a["ln0_g"], a["ln0_b"], local)
        norm_stage(nc, ident, flat, a["ln0_g"], a["ln0_b"], *pairs["w_v"], x_hi, x_lo, v)
        attend_stage(nc, ident, x_hi, x_lo, v, *pairs["w_qk"],
                     a["qkv_b"][0:C], a["qkv_b"][C:2 * C], local, o)
        project_stage(nc, ident, o, *pairs["w_proj"], a["qkv_b"][2 * C:3 * C], a["proj_b"], flat, y)
        conv_stage(nc, "c1", ident, cmask, y.rearrange("b c (h w) -> b c h w", w=W), a["taps1"], [a["dw_b"]],
                   a["ln1_g"], a["ln1_b"], normed1)
        mlp_stage(nc, ident, ones, normed1, *pairs["w_up"], *pairs["w_down"], a["b1"], a["grn_g"], a["grn_b"],
                  a["b2"], y, out.rearrange("b c h w -> b c (h w)"))


def kernel(**inputs):
    import concourse.bacc as bacc
    from concourse.bass_utils import run_bass_kernel_spmd as run

    def tiles(w):
        t = w.shape[0] // P
        return np.ascontiguousarray(w.reshape(t, P, -1).transpose(1, 0, 2).reshape(P, -1))

    i = {k: np.asarray(v) for k, v in inputs.items()}
    q, k, v = i["L0_conv_qkv_w"].reshape(3, HEADS, HD, C)
    qk = np.stack([q, q, k, k]).transpose(1, 3, 0, 2).reshape(HEADS, C, 4 * HD)
    arrays = {
        "x": i["x"],
        "w_qk": np.stack([tiles(w) for w in qk]),
        "w_v": tiles(v.reshape(C, C).T),
        "w_proj": tiles(i["L0_conv_proj_w"].T),
        "w_up": tiles(i["L1_conv_w1"]),
        "w_down": tiles(i["L1_conv_w2"]),
        "taps0": i["L0_conv_conv_w"][:, :, ::-1],
        "taps1": i["L1_conv_dw_w"][:, :, ::-1],
        "bn_gamma": i["L0_conv_bn_gamma"], "bn_beta": i["L0_conv_bn_beta"],
        "bn_mean": i["L0_conv_bn_mean"], "bn_var": i["L0_conv_bn_var"],
        "ln0_g": i["L0_conv_ln_gamma"], "ln0_b": i["L0_conv_ln_beta"],
        "qkv_b": i["L0_conv_qkv_b"], "proj_b": i["L0_conv_proj_b"],
        "dw_b": i["L1_conv_dw_b"], "ln1_g": i["L1_conv_ln_g"], "ln1_b": i["L1_conv_ln_b"],
        "b1": i["L1_conv_b1"], "grn_g": i["L1_conv_grn_g"], "grn_b": i["L1_conv_grn_b"], "b2": i["L1_conv_b2"],
    }
    arrays = {k: np.ascontiguousarray(v) for k, v in arrays.items()}
    nc = bacc.Bacc("TRN2", target_bir_lowering=False, num_devices=1)
    aps = {k: nc.dram_tensor("in_" + k, v.shape, F32, kind="ExternalInput").ap() for k, v in arrays.items()}
    out = nc.dram_tensor("out", (B, C, H, W), F32, kind="ExternalOutput").ap()
    build(nc, aps, out)
    r = run(nc, [{"in_" + k: v for k, v in arrays.items()}], core_ids=[0])
    return r.results[0]["out"]
```

```python
from contextlib import ExitStack

import numpy as np

import concourse.bass as bass
from concourse import mybir
from concourse.alu_op_type import AluOpType as ALU

F32 = mybir.dt.float32
F32R = mybir.dt.float32r
ACT = mybir.ActivationFunctionType
AX = mybir.AxisListType

B, C, H, W = 4, 384, 48, 48
N = H * W
P = 128
CT = C // P
HEADS, HD = 8, 48
CHUNK = 384
NCH = N // CHUNK
FH = 4 * C
FT = FH // P
QR = 8
GC = P // QR
NG = C // GC
HB = H // QR
KS = 7
NU = 2 * QR
LATE = KS // 2
JB = HB + 1
THIRDS = 3
TW = W // THIRDS
TT = JB * TW
assert THIRDS * QR == NG and QR + KS - 1 <= 2 * QR


def f32(ap):
    return ap.bitcast(F32)


def f32r(ap):
    return ap.bitcast(F32R)


def shared_consts(nc, ctx):
    ident = ctx.enter_context(nc.sbuf_tensor("ident", [P, P], F32))
    cmask = ctx.enter_context(nc.sbuf_tensor("cmask", [P, GC], F32))
    ones = ctx.enter_context(nc.sbuf_tensor("ones", [P, P], F32))
    made = ctx.enter_context(nc.semaphore("consts_made"))
    with nc.Block() as block:
        @block.gpsimd
        def _(pool):
            pool.memset(ident[:], 0.0).then_inc(made, 1)
            pool.memset(ones[:], 1.0).then_inc(made, 1)
            pool.wait_ge(made, 2)
            pool.affine_select(out=ident[:], in_=ident[:], compare_op=ALU.not_equal, fill=1.0, base=0,
                               pattern=[[-1, P]], channel_multiplier=1).then_inc(made, 1)
            pool.wait_ge(made, 3)
            pool.tensor_tensor(cmask[:], ident[:, 0:GC], ident[:, GC:2 * GC], ALU.add).then_inc(made, 1)
            for r in range(2, QR):
                pool.wait_ge(made, 2 + r)
                pool.tensor_tensor(cmask[:], cmask[:], ident[:, r * GC:(r + 1) * GC], ALU.add).then_inc(made, 1)
    return ident, cmask, ones


def segments(total, edges):
    cuts = sorted({0, total, *[e for e in edges if 0 < e < total]})
    return list(zip(cuts[:-1], cuts[1:]))


def at_least(eng, sem, count):
    if not isinstance(count, int) or count > 0:
        eng.wait_ge(sem, count)


def conv_stage(nc, tag, ident, cmask, src, taps, affine, ln_g, ln_b, dst, nb=B):
    S = nb * NG
    LE = 2
    LN = NG + 1
    LC = LN + 3
    COLS = JB * W
    with ExitStack() as ctx:
        def sb(name, shape, dt=F32):
            return ctx.enter_context(nc.sbuf_tensor(f"{tag}_{name}", shape, dt))

        def psum(name, shape):
            return ctx.enter_context(nc.psum_tensor(f"{tag}_{name}", shape, F32))

        def sem(name):
            return ctx.enter_context(nc.semaphore(f"{tag}_{name}"))

        tap_hi = sb("tap_hi", [P, NG, NU, KS], F32R)
        tap_lo = sb("tap_lo", [P, NG, NU, KS], F32R)
        band_hi = sb("band_hi", [P, 2, 2, KS, P], F32R)
        band_lo = sb("band_lo", [P, 2, 2, KS, P], F32R)
        x_raw = sb("x_raw", [P, 4, HB, W])
        x_hi = sb("x_hi", [P, 2, HB + 2, W + 6], F32R)
        x_lo = sb("x_lo", [P, 2, HB + 2, W + 6], F32R)
        par = sb("par", [P, affine.shape[0], NG])
        scale = sb("scale", [P, NG])
        shift = sb("shift", [P, NG])
        tmp = sb("tmp", [P, 3, NG])
        local = sb("local", [P, 2, THIRDS, JB, TW])
        tok = sb("tok", [TT, 2, THIRDS * QR, C])
        gam = sb("gam", [P, CT])
        bet = sb("bet", [P, CT])
        st = sb("st", [TT, 6])
        mv = sb("mv", [TT, 2])
        sd = sb("sd", [TT, 1])
        rs = sb("rs", [TT, 1])
        idle = sb("idle", [TT, 1])
        eps = sb("eps", [P, 1])
        eps_bn = sb("eps_bn", [P, 1])
        nrm = sb("nrm", [TT, 2, C])
        chan = sb("chan", [P, 2, CT, HB, QR, W])
        tap_raw = chan[:, 1].rearrange("p c k r w -> p (c k r w)")[:, 0:NG * NU * KS].rearrange(
            "p (g u d) -> p g u d", g=NG, u=NU)
        acc = psum("acc", [P, 2, 512])
        tps = psum("tps", [P, 2, 512])
        cps = psum("cps", [P, 2, 512])

        taps_in, par_in = sem("taps_in"), sem("par_in")
        zeroed, taps_hi, taps_lo = sem("zeroed"), sem("taps_hi"), sem("taps_lo")
        bn_sd, bn_dve = sem("bn_sd"), sem("bn_dve")
        x_in = [sem("x_in_even"), sem("x_in_odd")]
        hi_made, lo_made, bands_pool, bands_dve = sem("hi_made"), sem("lo_made"), sem("bands_pool"), sem("bands_dve")
        conv_done, local_made, turned, tok_made = sem("conv_done"), sem("local_made"), sem("turned"), sem("tok_made")
        sd_made, stats, rs_made, nrm_made = sem("sd_made"), sem("stats"), sem("rs_made"), sem("nrm_made")
        back, chan_made, stored = sem("back"), sem("chan_made"), sem("stored")

        groups = src.rearrange("b (g two c) (hb hi) w -> (b g) two hi c hb w", two=2, c=GC, hi=QR)
        tap_src = taps.rearrange("(g c) one kh kw -> c g (one kh kw)", c=GC)
        out_v = dst.rearrange("b (t p) n -> b t p n", p=P)
        batch_norm = affine.shape[0] == 4
        n_par = 16 * (QR + 2)

        ROTATED = [(slice(LATE, QR), slice(0, QR - LATE)), (slice(0, LATE), slice(QR - LATE, QR))]

        def by_block(table):
            return table.rearrange("p g (o r) d -> p (g o) r d", r=QR)

        def band(eng, parts, it, done):
            for mat, tap, o in parts:
                u0 = QR - QR * o
                taps_of = f32(tap[:, bass.ds(it % NG, 1), u0:u0 + QR, :]).rearrange("p one u d -> p (one d) u")
                last = eng.tensor_tensor(
                    mat[:, it % 2, o].rearrange("p d (u c) -> p d u c", c=GC),
                    taps_of.unsqueeze(3).to_broadcast([P, KS, QR, GC]),
                    cmask[:].unsqueeze(1).unsqueeze(1).to_broadcast([P, KS, QR, GC]), ALU.mult)
            last.then_inc(done, 1)

        block = ctx.enter_context(nc.Block())

        @block.sync
        def _(sp):
            def load(i):
                at_least(sp, lo_made, i * 2 - 2)
                for one in range(2):
                    at_least(sp, x_in[one], i * 16 * QR)
                    for hi in range(QR):
                        sp.dma_start(x_raw[hi * GC:(hi + 1) * GC, i % 2 * 2 + one], groups[i, one, hi]).then_inc(x_in[one], 16)

            def store(b):
                at_least(sp, stored, b * 16 * CT)
                sp.wait_ge(chan_made, (b + 1) * NG * CT)
                for c in range(CT):
                    sp.dma_start(out_v[b, c], chan[:, b % 2, c].rearrange("p k r w -> p (k r w)")).then_inc(stored, 16)

            sp.wait_ge(zeroed, 1)
            for hi in range(QR):
                sp.dma_start(tap_raw[hi * GC:(hi + 1) * GC, :, hi + 2:hi + 2 + KS, :].rearrange("c g u d -> c g (u d)"),
                             tap_src).then_inc(taps_in, 16)
            load(0)
            for hi in range(QR):
                sp.dma_start(par[hi * GC:(hi + 1) * GC], affine.rearrange("k (g c) -> c k g", c=GC),
                             allow_slow_non_contiguous=True).then_inc(par_in, 16)
            for part, v in ((gam, ln_g), (bet, ln_b)):
                sp.dma_start(part[:], v.rearrange("(t p) -> p t", p=P), allow_slow_non_contiguous=True).then_inc(par_in, 16)
            load(1)
            pairs, after = NG // 2, NG + 4
            with sp.Fori(2, min(S // 2, after)) as i:
                load(i)
            if nb > 3:
                with sp.Fori(0, nb - 3) as b:
                    store(b)
                    with sp.Fori(b * pairs + after, b * pairs + pairs + after) as i:
                        load(i)
            if nb > 2:
                store(nb - 3)
                with sp.Fori((nb - 3) * pairs + after, S // 2) as i:
                    load(i)
            store(nb - 2)
            store(nb - 1)
            sp.wait_ge(stored, nb * 16 * CT)

        @block.scalar
        def _(act):
            act.wait_ge(taps_in, 16 * QR)
            for to, of in ROTATED:
                act.activation(by_block(tap_hi[:])[:, :, to], by_block(tap_raw)[:, :, of], ACT.Copy).then_inc(taps_hi, 1)
            act.wait_ge(zeroed, 4)
            for a, z in segments(S + LC, [1, 2, 3, S, S + 1, LN, S + LN, LC, LC + 2 * NG]):
                if a == 1:
                    act.wait_ge(par_in, n_par)
                    if batch_norm:
                        act.activation(tmp[:, 0], par[:, 3], ACT.Sqrt, bias=eps_bn[:, 0:1]).then_inc(bn_sd, 1)
                    act.wait_ge(bn_dve, 4 if batch_norm else 2)
                with act.Fori(a, z) as it:
                    if a < S:
                        act.wait_ge(x_in[0], (it // 2 + 1) * 16 * QR)
                        if a >= 1:
                            act.wait_ge(x_in[1], (it + 1) // 2 * 16 * QR)
                        if a >= 2:
                            act.wait_ge(conv_done, it - 1)
                        act.activation(x_hi[:, it % 2, 1:HB + 1, 3:3 + W], x_raw[:, it % 4], ACT.Copy).then_inc(hi_made, 1)
                    if 1 <= a < S + 1:
                        s = it - 1
                        act.wait_ge(conv_done, it)
                        if a >= 3:
                            act.wait_ge(turned, it - 2)
                        act.activation(local[:, s % 2],
                                       acc[:, bass.ds(s % 2, 1), 0:COLS].rearrange("p one (j t w) -> p (one t) j w", t=THIRDS, w=TW),
                                       ACT.Identity, scale=scale[:, bass.ds(s % NG, 1)],
                                       bias=shift[:, bass.ds(s % NG, 1)]).then_inc(local_made, 1)
                    if a >= LC:
                        s = it - LC
                        if a >= LC + 2 * NG:
                            act.wait_ge(stored, (s - NG) // NG * 16 * CT)
                        act.wait_ge(back, s + 1)
                        row, third = s % QR, (s % NG) // QR
                        for c in range(CT):
                            act.activation(
                                chan[:, (s // NG) % 2, c, :, bass.ds(row, 1), bass.ds(third * TW, TW)].rearrange(
                                    "p k one w -> p (k one) w"),
                                cps[:, bass.ds(s % 2, 1), c * TT:(c + 1) * TT].rearrange("p one (j w) -> p (one j) w", w=TW)[
                                    :, bass.ds((row + QR - LATE) // QR, HB), :],
                                ACT.Identity, scale=gam[:, c:c + 1], bias=bet[:, c:c + 1]).then_inc(chan_made, 1)
                    if LN <= a < S + LN:
                        s = it - LN
                        act.wait_ge(stats, s * 2 + 2)
                        act.activation(sd[:], mv[:, 1:2], ACT.Sqrt, bias=eps[0:TT, 0:1]).then_inc(sd_made, 1)

        @block.vector
        def _(dve):
            def tile(s):
                return tok[:, (s // NG) % 2, bass.ds(s % NG, 1), :]

            dve.memset(tap_raw, 0.0).then_inc(zeroed, 1)
            dve.memset(eps[:], 1e-6).then_inc(zeroed, 1)
            dve.memset(eps_bn[:], 1e-5).then_inc(zeroed, 1)
            dve.memset(f32(x_hi[:]), 0.0)
            dve.memset(f32(x_lo[:]), 0.0).then_inc(zeroed, 1)
            dve.wait_ge(taps_hi, 2)
            for to, of in ROTATED:
                dve.tensor_tensor(by_block(tap_lo[:])[:, :, to], by_block(tap_raw)[:, :, of], by_block(f32(tap_hi[:]))[:, :, to],
                                  ALU.subtract).then_inc(taps_lo, 1)
            dve.wait_ge(taps_lo, 2)
            for a, z in segments(S + LN + 1, [1, 2, S, S + LE, LN, LN + 1, LN + 2, LN + 3, S + LN]):
                if a == 1:
                    dve.wait_ge(par_in, n_par)
                    if batch_norm:
                        dve.wait_ge(bn_sd, 1)
                        dve.reciprocal(tmp[:, 1], tmp[:, 0]).then_inc(bn_dve, 1)
                        dve.wait_ge(bn_dve, 1)
                        dve.tensor_tensor(scale[:], par[:, 0], tmp[:, 1], ALU.mult).then_inc(bn_dve, 1)
                        dve.wait_ge(bn_dve, 2)
                        dve.tensor_tensor(tmp[:, 2], par[:, 2], scale[:], ALU.mult).then_inc(bn_dve, 1)
                        dve.wait_ge(bn_dve, 3)
                        dve.tensor_tensor(shift[:], par[:, 1], tmp[:, 2], ALU.subtract).then_inc(bn_dve, 1)
                    else:
                        dve.memset(scale[:], 1.0).then_inc(bn_dve, 1)
                        dve.tensor_copy(shift[:], par[:, 0]).then_inc(bn_dve, 1)
                with dve.Fori(a, z) as it:
                    if a < S:
                        dve.wait_ge(hi_made, it + 1)
                        if a >= 2:
                            dve.wait_ge(conv_done, it - 1)
                        dve.tensor_tensor(x_lo[:, it % 2, 1:HB + 1, 3:3 + W], x_raw[:, it % 4],
                                          f32(x_hi[:, it % 2, 1:HB + 1, 3:3 + W]), ALU.subtract).then_inc(lo_made, 1)
                        band(dve, [(band_lo, tap_lo, 1)], it, bands_dve)
                    if a >= LN + 2:
                        dve.wait_ge(nrm_made, it - LN - 1)
                    if LE <= a < S + LE:
                        s = it - LE
                        dve.wait_ge(turned, s + 1)
                        dve.tensor_copy(
                            tok[:, (s // NG) % 2, :, bass.ds((s % NG) * GC, GC)],
                            tps[0:TT, bass.ds(s % 2, 1), 0:THIRDS * P].rearrange("p one (t c) -> p (one t) c", c=GC)).then_inc(tok_made, 1)
                    if LN <= a < S + LN:
                        s = it - LN
                        dve.wait_ge(tok_made, it - 1 if a < S + LE else S)
                        if a >= LN + 1:
                            dve.wait_ge(stats, s * 2)
                        dve.bn_stats(st[:], tile(s)).then_inc(stats, 1)
                    if a >= LN + 1:
                        f = it - LN - 1
                        dve.wait_ge(sd_made, f + 1)
                        dve.reciprocal(rs[:], sd[:]).then_inc(rs_made, 1)
                        if a >= LN + 3:
                            dve.wait_ge(back, f - 1)
                        dve.wait_ge(rs_made, f + 1)
                        dve.tensor_scalar(nrm[:, f % 2], tile(f), mv[:, 0:1], rs[:], ALU.subtract, ALU.mult).then_inc(nrm_made, 1)
                    if LN <= a < S + LN:
                        if a >= LN + 1:
                            dve.wait_ge(nrm_made, s)
                        dve.wait_ge(stats, s * 2 + 1)
                        dve.memset(idle[:], 0.0)
                        dve.bn_aggr(mv[:], st[:]).then_inc(stats, 1)

        @block.gpsimd
        def _(pool):
            pool.wait_ge(taps_lo, 2)
            for a, z in segments(S, [2]):
                with pool.Fori(a, z) as it:
                    if a >= 2:
                        pool.wait_ge(conv_done, it - 1)
                    band(pool, [(band_hi, tap_hi, 0), (band_hi, tap_hi, 1), (band_lo, tap_lo, 0)], it, bands_pool)

        @block.tensor
        def _(pe):
            def conv(s, k, wait_acc=True):
                pe.wait_ge(bands_pool, s + 1)
                pe.wait_ge(bands_dve, s + 1)
                pe.wait_ge(lo_made, s + 1)
                if wait_acc:
                    pe.wait_ge(local_made, s - 1)
                for o in range(2):
                    for d in range(KS):
                        for mat, x in ((band_hi, x_hi), (band_hi, x_lo), (band_lo, x_hi)):
                            last = pe.matmul(acc[:, k, 0:COLS], mat[:, k, o, d, :], x[:, k, o:o + JB, d:d + W],
                                             start=o == 0 and d == 0 and mat is band_hi and x is x_hi,
                                             stop=o == 1 and d == KS - 1 and mat is band_lo)
                last.then_inc(conv_done, 1)

            def turn(s, k, wait_tok=True):
                pe.wait_ge(local_made, s + 1)
                if wait_tok:
                    pe.wait_ge(tok_made, s - 1)
                for t in range(THIRDS):
                    last = pe.transpose(tps[0:TT, k, t * P:(t + 1) * P], local[:, k, t].rearrange("p j w -> p (j w)"), ident[:])
                last.then_inc(turned, 1)

            def to_channels(s, k):
                pe.wait_ge(nrm_made, s + 1)
                at_least(pe, chan_made, (s - 1) * CT)
                for c in range(CT):
                    last = pe.transpose(cps[:, k, c * TT:(c + 1) * TT], nrm[:, k, c * P:(c + 1) * P], ident[0:TT, 0:TT])
                last.then_inc(back, 1)

            conv(0, 0, False)
            conv(1, 1, False)
            turn(0, 0, False)
            conv(2, 0)
            turn(1, 1, False)
            conv(3, 1)
            turn(2, 0)
            with pe.Fori(2, LC // 2) as i:
                conv(i * 2, 0)
                turn(i * 2 - 1, 1)
                conv(i * 2 + 1, 1)
                turn(i * 2, 0)
            for it in range(LC, LC + 2):
                to_channels(it - LC, it % 2)
                conv(it, it % 2)
                turn(it - 1, 1 - it % 2)
            with pe.Fori(LC // 2 + 1, S // 2) as i:
                to_channels(i * 2 - LC, 0)
                conv(i * 2, 0)
                turn(i * 2 - 1, 1)
                to_channels(i * 2 + 1 - LC, 1)
                conv(i * 2 + 1, 1)
                turn(i * 2, 0)
            turn(S - 1, 1)
            with pe.Fori(S // 2, (S + LC) // 2) as i:
                to_channels(i * 2 - LC, 0)
                to_channels(i * 2 + 1 - LC, 1)


def split_stage(nc, tag, items):
    with ExitStack() as ctx:
        def sb(name, shape, dt=F32):
            return ctx.enter_context(nc.sbuf_tensor(f"{tag}_{name}", shape, dt))

        def sem(name):
            return ctx.enter_context(nc.semaphore(f"{tag}_{name}"))

        loaded = [sem(f"loaded{n}") for n in range(len(items))]
        hi_made, lo_made, stored = sem("hi_made"), sem("lo_made"), sem("stored")
        raw = [sb(f"raw{n}", [P, it[0].shape[1]]) for n, it in enumerate(items)]
        hi = [sb(f"hi{n}", [P, it[0].shape[1]], F32R) for n, it in enumerate(items)]
        lo = [sb(f"lo{n}", [P, it[0].shape[1]], F32R) for n, it in enumerate(items)]
        block = ctx.enter_context(nc.Block())

        @block.sync
        def _(sp):
            for n, (src, _h, _l) in enumerate(items):
                sp.dma_start(raw[n][:], src).then_inc(loaded[n], 16)
            for n, (_s, hi_out, lo_out) in enumerate(items):
                sp.wait_ge(hi_made, n + 1)
                sp.dma_start(hi_out, f32(hi[n][:])).then_inc(stored, 16)
                sp.wait_ge(lo_made, n + 1)
                sp.dma_start(lo_out, f32(lo[n][:])).then_inc(stored, 16)
            sp.wait_ge(stored, 32 * len(items))

        @block.scalar
        def _(act):
            for n in range(len(items)):
                act.wait_ge(loaded[n], 16)
                act.activation(hi[n][:], raw[n][:], ACT.Copy).then_inc(hi_made, 1)

        @block.vector
        def _(dve):
            for n in range(len(items)):
                dve.wait_ge(hi_made, n + 1)
                dve.tensor_tensor(lo[n][:], raw[n][:], f32(hi[n][:]), ALU.subtract).then_inc(lo_made, 1)


def norm_stage(nc, ident, x, ln_g, ln_b, w_in, x_hi_out, x_lo_out, v_out, nb=B):
    S = nb * NCH
    NT = CHUNK // P
    with ExitStack() as ctx:
        def sb(name, shape, dt=F32):
            return ctx.enter_context(nc.sbuf_tensor(f"n_{name}", shape, dt))

        def psum(name, shape):
            return ctx.enter_context(nc.psum_tensor(f"n_{name}", shape, F32))

        def sem(name):
            return ctx.enter_context(nc.semaphore(f"n_{name}"))

        xc = sb("xc", [P, 2, CT, CHUNK])
        st = sb("st", [P, NT, 6])
        mv = sb("mv", [P, NT, 2])
        sd = sb("sd", [P, NT])
        rs = sb("rs", [P, NT])
        nrm = sb("nrm", [P, 2, NT, C])
        w_hi, w_lo = sb("w_hi", [P, CT, C], F32R), sb("w_lo", [P, CT, C], F32R)
        v = sb("v", [P, 2, NT, HEADS, 2, HD])
        full = sb("full", [P, 2, CT, CHUNK])
        hi = sb("hi", [P, 2, CT, CHUNK], F32R)
        lo = sb("lo", [P, 2, CT, CHUNK], F32R)
        gam = sb("gam", [P, CT])
        bet = sb("bet", [P, CT])
        eps = sb("eps", [P, 1])
        idle = sb("idle", [P, 1])
        ps_tok = psum("ps_tok", [P, NT, 512])
        ps_ch = psum("ps_ch", [P, CT, 512])
        ps_v = psum("ps_v", [P, 2, 512])
        v_done, v_hi_made, v_made, v_stored = sem("v_done"), sem("v_hi_made"), sem("v_made"), sem("v_stored")
        x_in, par_in, eps_made = sem("x_in"), sem("par_in"), sem("eps_made")
        w_raw = sb("w_raw", [P, CT * C])
        w_split, w_ready = sem("w_split"), sem("w_ready")
        to_tok, to_ch, stats, sd_made, rs_made = sem("to_tok"), sem("to_ch"), sem("stats"), sem("sd_made"), sem("rs_made")
        normed, full_made, hi_made, lo_made, stored = (sem("normed"), sem("full_made"), sem("hi_made"), sem("lo_made"),
                                                       sem("stored"))
        xs = x.rearrange("b (t p) n -> b p t n", p=P)
        his = x_hi_out.rearrange("b (t p) n -> b p t n", p=P)
        los = x_lo_out.rearrange("b (t p) n -> b p t n", p=P)
        v_v = v_out.rearrange("b (s t p) n -> b s p t n", t=NT, p=P)
        block = ctx.enter_context(nc.Block())

        @block.sync
        def _(sp):
            sp.dma_start(gam[:], ln_g.rearrange("(t p) -> p t", p=P), allow_slow_non_contiguous=True).then_inc(par_in, 16)
            sp.dma_start(bet[:], ln_b.rearrange("(t p) -> p t", p=P), allow_slow_non_contiguous=True).then_inc(par_in, 16)
            sp.dma_start(w_raw[:], w_in).then_inc(par_in, 16)
            for a, z in segments(S + 4, [1, 2, 3, 4, 5, S, S + 3]):
                with sp.Fori(a, z) as it:
                    if a < S:
                        if a >= 1:
                            sp.wait_ge(x_in, it * 16)
                        if a >= 2:
                            sp.wait_ge(to_tok, (it - 1) * NT)
                        sp.dma_start(xc[:, it % 2], xs[it // NCH, :, :, bass.ds((it % NCH) * CHUNK, CHUNK)]).then_inc(x_in, 16)
                    if 3 <= a < S + 3:
                        s = it - 3
                        if a >= 4:
                            sp.wait_ge(stored, s * 32)
                        sp.wait_ge(lo_made, s * CT + CT)
                        for part, out in ((hi, his), (lo, los)):
                            sp.dma_start(out[s // NCH, :, :, bass.ds((s % NCH) * CHUNK, CHUNK)],
                                         f32(part[:, s % 2])).then_inc(stored, 16)
                    if a >= 4:
                        s = it - 4
                        if a >= 5:
                            sp.wait_ge(v_stored, s * 16)
                        sp.wait_ge(v_made, s * NT + NT)
                        sp.dma_start(v_v[s // NCH, s % NCH], v[:, s % 2].rearrange("p t h two d -> p t (h two d)")).then_inc(v_stored, 16)
            sp.wait_ge(stored, S * 32)
            sp.wait_ge(v_stored, S * 16)

        @block.vector
        def _(dve):
            dve.memset(eps[:], 1e-6).then_inc(eps_made, 1)
            dve.wait_ge(w_split, 1)
            dve.tensor_tensor(w_lo[:].rearrange("p t n -> p (t n)"), w_raw[:], f32(w_hi[:]).rearrange("p t n -> p (t n)"),
                              ALU.subtract).then_inc(w_ready, 1)

            def values(s):
                for t in range(NT):
                    dve.wait_ge(v_hi_made, s * NT + t + 1)
                    dve.tensor_tensor(f32r(v[:, s % 2, t, :, 1, :]),
                                      ps_v[:, bass.ds((s * NT + t) % 2, 1), 0:C].rearrange("p one (h d) -> p (one h) d", d=HD),
                                      v[:, s % 2, t, :, 0, :], ALU.subtract).then_inc(v_made, 1)

            for a, z in segments(S + 2, [1, 2, S]):
                with dve.Fori(a, z) as it:
                    if a >= S:
                        values(it - 2)
                        continue
                    for t in range(NT):
                        dve.wait_ge(to_tok, it * NT + t + 1)
                        dve.bn_stats(st[:, t], ps_tok[:, t, 0:C]).then_inc(stats, 1)
                    dve.wait_ge(stats, it * 2 * NT + NT)
                    dve.memset(idle[:], 0.0)
                    for t in range(NT):
                        dve.bn_aggr(mv[:, t], st[:, t]).then_inc(stats, 1)
                    dve.wait_ge(sd_made, it + 1)
                    dve.reciprocal(rs[:], sd[:]).then_inc(rs_made, 1)
                    if a >= 2:
                        dve.wait_ge(to_ch, (it - 1) * CT)
                    dve.wait_ge(rs_made, it + 1)
                    for t in range(NT):
                        dve.tensor_scalar(nrm[:, it % 2, t], ps_tok[:, t, 0:C], mv[:, t, 0:1], rs[:, t:t + 1],
                                          ALU.subtract, ALU.mult).then_inc(normed, 1)
                    if a >= 2:
                        values(it - 2)

        @block.scalar
        def _(act):
            act.wait_ge(eps_made, 1)
            act.wait_ge(par_in, 48)
            act.activation(w_hi[:].rearrange("p t n -> p (t n)"), w_raw[:], ACT.Copy).then_inc(w_split, 1)

            def values(s, t):
                act.wait_ge(v_done, s * NT + t + 1)
                act.activation(f32r(v[:, s % 2, t, :, 0, :]),
                               ps_v[:, bass.ds((s * NT + t) % 2, 1), 0:C].rearrange("p one (h d) -> p (one h) d", d=HD),
                               ACT.Copy).then_inc(v_hi_made, 1)

            for a, z in segments(S + 2, [1, 2, 3, 4, S, S + 1]):
                with act.Fori(a, z) as it:
                    if a < S:
                        act.wait_ge(stats, it * 2 * NT + 2 * NT)
                        act.activation(sd[:], mv[:, :, 1], ACT.Sqrt, bias=eps[:, 0:1]).then_inc(sd_made, 1)
                    if 1 <= a < S + 1:
                        s = it - 1
                        if a >= 3:
                            act.wait_ge(lo_made, (s - 1) * CT)
                            act.wait_ge(stored, (s - 1) * 32)
                        for t in range(CT):
                            act.wait_ge(to_ch, s * CT + t + 1)
                            act.activation(full[:, s % 2, t], ps_ch[:, t, 0:CHUNK], ACT.Identity,
                                           scale=gam[:, t:t + 1], bias=bet[:, t:t + 1]).then_inc(full_made, 1)
                    if a >= 2:
                        if a >= 4:
                            act.wait_ge(v_stored, (it - 3) * 16)
                        values(it - 2, 0)
                        values(it - 2, 1)
                    if 1 <= a < S + 1:
                        s = it - 1
                        if a >= 3:
                            act.wait_ge(v_done, (s - 1) * NT)
                        for t in range(CT):
                            act.wait_ge(full_made, s * CT + t + 1)
                            act.activation(hi[:, s % 2, t], full[:, s % 2, t], ACT.Copy).then_inc(hi_made, 1)
                    if a >= 2:
                        values(it - 2, 2)

        @block.gpsimd
        def _(pool):
            for a, z in segments(S, [2]):
                with pool.Fori(a, z) as it:
                    if a >= 2:
                        pool.wait_ge(stored, (it - 1) * 32)
                        pool.wait_ge(v_done, (it - 1) * NT)
                    for t in range(CT):
                        pool.wait_ge(hi_made, it * CT + t + 1)
                        pool.tensor_tensor(lo[:, it % 2, t], full[:, it % 2, t], f32(hi[:, it % 2, t]),
                                           ALU.subtract).then_inc(lo_made, 1)

        @block.tensor
        def _(pe):
            def tokens(s, k):
                pe.wait_ge(x_in, (s + 1) * 16)
                at_least(pe, normed, s * NT)
                for t in range(NT):
                    for c in range(CT):
                        last = pe.transpose(ps_tok[:, t, c * P:(c + 1) * P], xc[:, k, c, t * P:(t + 1) * P], ident[:])
                    last.then_inc(to_tok, 1)

            def channels(s, k):
                pe.wait_ge(normed, (s + 1) * NT)
                at_least(pe, full_made, s * CT)
                for c in range(CT):
                    for t in range(NT):
                        last = pe.transpose(ps_ch[:, c, t * P:(t + 1) * P], nrm[:, k, t, c * P:(c + 1) * P], ident[:])
                    last.then_inc(to_ch, 1)

            def values(s, k):
                pe.wait_ge(hi_made, (s + 1) * CT)
                pe.wait_ge(lo_made, (s + 1) * CT)
                for t in range(NT):
                    at_least(pe, v_made, s * NT + t - 1)
                    tok = slice(t * P, (t + 1) * P)
                    for j, (xp, wp) in enumerate(((hi, w_hi), (lo, w_hi), (hi, w_lo))):
                        for c in range(CT):
                            last = pe.matmul(ps_v[:, (k * NT + t) % 2, 0:C], xp[:, k, c, tok], wp[:, c, :],
                                             start=j == 0 and c == 0, stop=j == 2 and c == CT - 1)
                    last.then_inc(v_done, 1)

            pe.wait_ge(w_ready, 1)
            tokens(0, 0)
            tokens(1, 1)
            channels(0, 0)
            tokens(2, 0)
            channels(1, 1)
            values(0, 0)
            tokens(3, 1)
            channels(2, 0)
            values(1, 1)
            with pe.Fori(2, S // 2) as i:
                tokens(i * 2, 0)
                channels(i * 2 - 1, 1)
                values(i * 2 - 2, 0)
                tokens(i * 2 + 1, 1)
                channels(i * 2, 0)
                values(i * 2 - 1, 1)
            channels(S - 1, 1)
            values(S - 2, 0)
            values(S - 1, 1)


def attend_stage(nc, ident, x_hi_in, x_lo_in, v_in, w_hi_in, w_lo_in, qb, kb, local, out, nb=B):
    NHEAD = nb * HEADS
    KT = N // P
    PAIRS = KT // 2
    STEPS = NCH * PAIRS
    LAG = 4
    SLOTS = 4
    QT = N // P
    PIECES = [(k * 512, min(512, N - k * 512)) for k in range((N + 511) // 512)]
    NMX = QT * len(PIECES)
    ROW = 2 * HD
    KB = 64
    MROW = KB + HD
    JOB_STEPS = [0, 1, 2, 3, 4, 6]
    JOBS_AT = {s: i for i, s in enumerate(JOB_STEPS)}
    MAX_AT = {8 + m // 2: (m, m + 1) for m in range(0, NMX, 2)}
    ROW_0_AT = 32
    ROW_1_AT = 8
    HQ = QT // 2
    COMB_AT = {PAIRS * c + PAIRS - 1 + LAG + 2: c for c in range(NCH)}
    POOL_SUBS = [n for n in range(STEPS) if n % 2 == 0]
    ON_POOL = {n: i for i, n in enumerate(POOL_SUBS)}
    DVE_SUBS = [n for n in range(STEPS) if n not in ON_POOL]
    ON_DVE = {n: i for i, n in enumerate(DVE_SUBS)}
    NP_, ND_ = len(POOL_SUBS), len(DVE_SUBS)

    with ExitStack() as ctx:
        def sb(name, shape, dt=F32):
            return ctx.enter_context(nc.sbuf_tensor(f"a_{name}", shape, dt))

        def psum(name, shape):
            return ctx.enter_context(nc.psum_tensor(f"a_{name}", shape, F32))

        def sem(name):
            return ctx.enter_context(nc.semaphore(f"a_{name}"))

        x_hi = sb("x_hi", [P, CT, N], F32R)
        x_lo = sb("x_lo", [P, CT, N], F32R)
        w = sb("w", [P, 2, 2, CT, MROW], F32R)
        q = sb("q", [P, 2, N], F32R)
        k_hi = sb("k_hi", [P, 2, N], F32R)
        k_lo = sb("k_lo", [P, 2, N], F32R)
        v = sb("v", [P, 2, KT, ROW + 2], F32R)
        loc = sb("loc", [MROW, 2, N])
        full = sb("full", [MROW, 2, CHUNK])
        e_full = sb("e_full", [P, SLOTS, 2, CHUNK])
        e_hi = sb("e_hi", [P, SLOTS, 2, CHUNK], F32R)
        e_lo = sb("e_lo", [P, SLOTS, 2, CHUNK], F32R)
        o_t = sb("o_t", [ROW + 1, 2, CHUNK])
        r_sum = sb("r_sum", [P, 2, 3])
        o_tok = sb("o_tok", [P, 2, 3, HD])
        mx_part = sb("mx_part", [P, 2, QT, len(PIECES)])
        mx = sb("mx", [P, 2, QT])
        mx_row = sb("mx_row", [HQ, 2, P])
        bias_all = sb("bias_all", [MROW, HEADS])
        bias = sb("bias", [MROW, 2])
        comb = sb("comb", [ROW + 1, HD + 1])

        ps_s = psum("ps_s", [P, 2, 2, 512])
        ps_o = psum("ps_o", [P, 512])
        ps_m = psum("ps_m", [P, 2, 512])
        ps_x = psum("ps_x", [P, 512])

        x_in = [sem(f"x_in{c}") for c in range(NCH)]
        head_in, v_arrived, bias_in, bias_taken = sem("head_in"), sem("v_arrived"), sem("bias_in"), sem("bias_taken")
        made_pool, made_dve = sem("made_pool"), sem("made_dve")
        proj_done, full_made, hi_made, lo_made = sem("proj_done"), sem("full_made"), sem("hi_made"), sem("lo_made")
        mx_done, mx_red, mx_fin = sem("mx_done"), sem("mx_red"), sem("mx_fin")
        row_turned, row_out, row_in = sem("row_turned"), sem("row_out"), [sem("row_in0"), sem("row_in1")]
        s_done, e_made, e_hi_made = sem("s_done"), sem("e_made"), sem("e_hi_made")
        lo_dve, lo_pool = sem("lo_dve"), sem("lo_pool")
        o_done, o_out, comb_done, r_made, o_made, stored = (sem("o_done"), sem("o_out"), sem("comb_done"),
                                                            sem("r_made"), sem("o_made"), sem("stored"))

        x_parts = [(x_hi, x_hi_in.rearrange("b (t p) n -> b p t n", p=P)),
                   (x_lo, x_lo_in.rearrange("b (t p) n -> b p t n", p=P))]
        loc_in = local.rearrange("b (h d) n -> b h d n", d=HD)
        v_v = v_in.rearrange("b (t p) (h n) -> b h p t n", p=P, h=HEADS)
        out_v = out.rearrange("b (c t p) (h d) -> b h c p t d", p=P, t=3, d=HD)

        def wait_lo(eng, h, n):
            if n in ON_POOL:
                at_least(eng, lo_pool, h * NP_ + ON_POOL[n] + 1)
            else:
                at_least(eng, lo_dve, h * ND_ + ON_DVE[n] + 1)

        def slot(par, n):
            return (par * STEPS + n) % SLOTS

        def back(h, n, d):
            return (h, n - d) if n >= d else (h - 1, n - d + STEPS)

        def bodies(body, eng):
            body(-1, 1, main=False, prev=False, nxt=True)
            body(0, 0, main=True, prev=False, nxt=True)
            if NHEAD > 2:
                with eng.Fori(0, (NHEAD - 2) // 2) as i:
                    body(i * 2 + 1, 1, main=True, prev=True, nxt=True)
                    body(i * 2 + 2, 0, main=True, prev=True, nxt=True)
            body(NHEAD - 1, 1, main=True, prev=True, nxt=False)
            body(NHEAD, 0, main=False, prev=True, nxt=False)

        block = ctx.enter_context(nc.Block())

        @block.sync
        def _(sp):
            def load_weights(h):
                for part, src in ((0, w_hi_in), (1, w_lo_in)):
                    sp.dma_start(f32(w[:, h % 2, part]), src[h % HEADS]).then_inc(head_in, 16)

            def load_local(h):
                sp.dma_start(loc[0:HD, h % 2], loc_in[h // HEADS, h % HEADS]).then_inc(head_in, 16)

            def load_chunk(b, c):
                for part, src in x_parts:
                    sp.dma_start(f32(part[:, :, c * CHUNK:(c + 1) * CHUNK]),
                                 src[b, :, :, c * CHUNK:(c + 1) * CHUNK]).then_inc(x_in[c], 16)

            load_weights(0)
            load_chunk(0, 0)
            sp.wait_ge(made_pool, 2)
            for first, src in ((0, qb), (KB, kb)):
                sp.dma_start(bias_all[first:first + HD], src.rearrange("(h d) -> d h", d=HD),
                             allow_slow_non_contiguous=True).then_inc(bias_in, 16)
            load_local(0)
            for c in range(1, NCH):
                load_chunk(0, c)

            def step(g, more=True, first=False):
                if more:
                    if not first:
                        sp.wait_ge(full_made, g * NCH)
                    sp.wait_ge(head_in, (g + 1) * 48)
                    load_weights(g + 1)
                    load_local(g + 1)
                if not first:
                    sp.wait_ge(v_arrived, g * 16)
                    at_least(sp, o_done, (g - 1) * STEPS)
                sp.dma_start(f32(v[:, g % 2, :, 0:ROW]), v_v[g // HEADS, g % HEADS]).then_inc(v_arrived, 16)

            def next_image(b):
                last = (b + 1) * HEADS - 1
                for c in range(NCH):
                    sp.wait_ge(proj_done, last * NCH + c + 1)
                    load_chunk(b + 1, c)

            step(0, first=True)
            step(1)
            with sp.Fori(2, HEADS - 1) as g:
                step(g)
            step(HEADS - 1, more=nb > 1)
            if nb > 1:
                next_image(0)
                if nb > 2:
                    with sp.Fori(1, nb - 1) as b:
                        with sp.Fori(0, HEADS) as g:
                            step(b * HEADS + g)
                        next_image(b)
                with sp.Fori((nb - 1) * HEADS, NHEAD - 1) as g:
                    step(g)
                step(NHEAD - 1, more=False)

        @block.gpsimd
        def _(pool):
            pool.memset(bias_all[:], 0.0).then_inc(made_pool, 1)
            pool.memset(loc[:], 0.0).then_inc(made_pool, 1)
            pool.memset(comb[:], 0.0).then_inc(made_pool, 1)
            pool.wait_ge(made_pool, 3)
            pool.affine_select(out=comb[:, 0:HD], in_=comb[:, 0:HD], compare_op=ALU.not_equal, fill=1.0, base=0,
                               pattern=[[-1, HD]], channel_multiplier=1).then_inc(made_pool, 1)
            pool.wait_ge(made_pool, 4)
            pool.affine_select(out=comb[:], in_=comb[:], compare_op=ALU.not_equal, fill=1.0, base=-HD,
                               pattern=[[-1, HD + 1]], channel_multiplier=1).then_inc(made_pool, 1)

            def body(h, par, main, prev, nxt):
                for n in range(STEPS):
                    if main and n in ON_POOL:
                        pool.wait_ge(e_hi_made, h * STEPS + n + 1)
                        at_least(pool, o_done, h * STEPS + n - SLOTS + 1)
                        e = slot(par, n)
                        pool.tensor_tensor(e_lo[:, e], e_full[:, e], f32(e_hi[:, e]), ALU.subtract).then_inc(lo_pool, 1)

            bodies(body, pool)

        @block.scalar
        def _(act):
            act.wait_ge(bias_in, 32)
            act.wait_ge(made_pool, 5)
            act.wait_ge(made_dve, 3)

            def split(h, par, i):
                cols = slice(i * CHUNK, (i + 1) * CHUNK)
                if i == 0:
                    at_least(act, s_done, (h - 1) * STEPS)
                act.wait_ge(full_made, h * NCH + i + 1)
                for part, first, whole in ((k_hi, KB, KB), (q, 0, 0), (k_hi, 0, KB)):
                    act.activation(part[first:first + HD, par, cols], full[whole:whole + HD, i % 2],
                                   ACT.Copy).then_inc(hi_made, 1)

            def hi_of(h, par, n):
                act.wait_ge(e_made, h * STEPS + n + 1)
                at_least(act, o_done, h * STEPS + n - SLOTS + 1)
                act.activation(e_hi[:, slot(par, n)], e_full[:, slot(par, n)], ACT.Copy).then_inc(e_hi_made, 1)

            def take_out(h, c):
                act.wait_ge(o_done, h * STEPS + PAIRS * (c + 1))
                at_least(act, comb_done, h * NCH + c - 1)
                act.activation(o_t[:, c % 2], ps_o[0:ROW + 1, 0:CHUNK], ACT.Copy).then_inc(o_out, 1)

            def store(h, c):
                act.wait_ge(o_made, h * NCH + c + 1)
                at_least(act, stored, (h * NCH + c) * 16)
                act.dma_start(out_v[h // HEADS, h % HEADS, c], o_tok[:, c % 2]).then_inc(stored, 16)

            def row_of_maxima(h, par, half):
                act.wait_ge(row_turned, h * 2 + half + 1)
                at_least(act, row_in[half], h * 16)
                act.activation(f32r(mx_row[:, half]), ps_x[0:HQ, 0:P], ACT.Copy, scale=-1.0).then_inc(row_out, 1)
                act.wait_ge(row_out, h * 2 + half + 1)
                act.dma_start(f32(q[MROW:MROW + 1, par, half * (N // 2):(half + 1) * (N // 2)]).rearrange(
                    "o (t p) -> o t p", p=P), mx_row[:, half]).then_inc(row_in[half], 16)

            def body(h, par, main, prev, nxt):
                for n in range(STEPS):
                    c, r = divmod(n - LAG - 1, PAIRS)
                    if main and n >= LAG + PAIRS and r == PAIRS - 1:
                        take_out(h, c)
                    if prev and n == LAG:
                        take_out(h - 1, NCH - 1)
                    if main:
                        act.wait_ge(s_done, h * STEPS + n + 1)
                        at_least(act, e_hi_made, h * STEPS + n - SLOTS + 1)
                        p_h, p_n = back(h, n, SLOTS)
                        if prev or n >= SLOTS:
                            wait_lo(act, p_h, p_n)
                        act.activation(e_full[:, slot(par, n)], ps_s[:, n % 2, :, 0:CHUNK], ACT.Exp,
                                       scale=float(HD) ** -0.5).then_inc(e_made, 1)
                        if n >= 1:
                            hi_of(h, par, n - 1)
                    if n == 0 and prev:
                        hi_of(h - 1, 1 - par, STEPS - 1)
                    if nxt and n == 0:
                        act.activation(bias[:, 1 - par:2 - par], bias_all[:, bass.ds((h + 1) % HEADS, 1)], ACT.Copy).then_inc(bias_taken, 1)
                    if nxt and n in JOBS_AT:
                        split(h + 1, 1 - par, JOBS_AT[n])
                    if nxt and n == ROW_0_AT:
                        row_of_maxima(h + 1, 1 - par, 0)
                    if main and n == ROW_1_AT:
                        row_of_maxima(h, par, 1)
                    if main and n - 4 in COMB_AT:
                        store(h, COMB_AT[n - 4])
                    if prev and n - 4 + STEPS in COMB_AT:
                        store(h - 1, COMB_AT[n - 4 + STEPS])

            bodies(body, act)
            act.wait_ge(stored, NHEAD * NCH * 16)

        @block.vector
        def _(dve):
            dve.memset(f32(v[:, :, :, ROW:ROW + 1]), 1.0).then_inc(made_dve, 1)
            dve.memset(f32(q[:]), 0.0).then_inc(made_dve, 1)
            dve.memset(f32(k_hi[:]), 1.0)
            dve.memset(f32(k_lo[:]), 0.0).then_inc(made_dve, 1)

            def whole(h, par, i):
                dve.wait_ge(proj_done, h * NCH + i + 1)
                if i == 0:
                    dve.wait_ge(bias_taken, h + 1)
                at_least(dve, hi_made, (h * NCH + i - 1) * 3)
                at_least(dve, lo_made, (h * NCH + i - 1) * 3)
                dve.scalar_tensor_tensor(out=full[:, i % 2], in0=ps_x[0:MROW, 0:CHUNK], scalar=bias[:, par:par + 1],
                                         in1=loc[:, par, i * CHUNK:(i + 1) * CHUNK], op0=ALU.add,
                                         op1=ALU.add).then_inc(full_made, 1)

            def split(h, par, i):
                cols = slice(i * CHUNK, (i + 1) * CHUNK)
                for n, (part, first, whole, hi) in enumerate(((k_lo, KB, KB, k_hi), (q, KB, 0, q), (k_lo, 0, KB, k_hi))):
                    if n < 2:
                        dve.wait_ge(hi_made, (h * NCH + i) * 3 + n + 1)
                    dve.tensor_tensor(part[first:first + HD, par, cols], full[whole:whole + HD, i % 2],
                                      f32(hi[whole:whole + HD, par, cols]), ALU.subtract).then_inc(lo_made, 1)

            def lo_of(h, par, n):
                dve.wait_ge(e_hi_made, h * STEPS + n + 1)
                at_least(dve, o_done, h * STEPS + n - SLOTS + 1)
                e = slot(par, n)
                dve.tensor_tensor(e_lo[:, e], e_full[:, e], f32(e_hi[:, e]), ALU.subtract).then_inc(lo_dve, 1)

            def maxima(h, par, m):
                t, k = divmod(m, len(PIECES))
                if m == 0:
                    at_least(dve, mx_fin, (h - 1) * 2)
                dve.wait_ge(mx_done, h * NMX + m + 1)
                dve.tensor_reduce(mx_part[:, par, t, k:k + 1], ps_m[:, m % 2, 0:PIECES[k][1]], AX.X,
                                  ALU.max).then_inc(mx_red, 1)

            def fold(h, par, half):
                tiles = slice(half * HQ, (half + 1) * HQ)
                dve.wait_ge(mx_red, h * NMX + (half + 1) * NMX // 2)
                at_least(dve, row_turned, (h - 1) * 2)
                dve.tensor_reduce(mx[:, par, tiles], mx_part[:, par, tiles], AX.X, ALU.max).then_inc(mx_fin, 1)

            def normalise(h, c):
                dve.wait_ge(comb_done, h * NCH + c + 1)
                at_least(dve, o_made, h * NCH + c - 1)
                sums = ps_x[:, 0:3 * (HD + 1)].rearrange("p (t d) -> p t d", d=HD + 1)
                dve.reciprocal(r_sum[:, c % 2, :].unsqueeze(2), sums[:, :, HD:HD + 1]).then_inc(r_made, 1)
                dve.wait_ge(r_made, h * NCH + c + 1)
                at_least(dve, stored, (h * NCH + c - 1) * 16)
                dve.tensor_tensor(o_tok[:, c % 2], sums[:, :, 0:HD],
                                  r_sum[:, c % 2, :].unsqueeze(2).to_broadcast([P, 3, HD]), ALU.mult).then_inc(o_made, 1)

            def body(h, par, main, prev, nxt):
                for n in range(STEPS):
                    if prev and n < 2:
                        l_n = n - 2 + STEPS
                        if l_n in ON_DVE:
                            lo_of(h - 1, 1 - par, l_n)
                    if main and n >= 2 and n - 2 in ON_DVE:
                        lo_of(h, par, n - 2)
                    if nxt and n in JOBS_AT:
                        whole(h + 1, 1 - par, JOBS_AT[n])
                    if main and n in COMB_AT:
                        normalise(h, COMB_AT[n])
                    if prev and n + STEPS in COMB_AT:
                        normalise(h - 1, COMB_AT[n + STEPS])
                    if nxt and n - 1 in JOBS_AT:
                        split(h + 1, 1 - par, JOBS_AT[n - 1])
                    if nxt and n in MAX_AT:
                        for m in MAX_AT[n]:
                            maxima(h + 1, 1 - par, m)
                    if nxt and n == ROW_0_AT - 1:
                        fold(h + 1, 1 - par, 0)
                    if main and n == ROW_1_AT - 1:
                        fold(h, par, 1)

            bodies(body, dve)

        @block.tensor
        def _(pe):
            pe.wait_ge(made_pool, 5)
            pe.wait_ge(made_dve, 3)
            free = [None]

            def take_ps_x(sem_, count):
                if free[0] is not None:
                    at_least(pe, *free[0])
                free[0] = (sem_, count)

            def project(h, par, i):
                take_ps_x(full_made, h * NCH + i + 1)
                if i == 0:
                    pe.wait_ge(head_in, (h + 1) * 48)
                pe.wait_ge(x_in[i], (h // HEADS + 1) * 32)
                cols = slice(i * CHUNK, (i + 1) * CHUNK)
                for j, (wp, xp) in enumerate(((0, x_hi), (0, x_lo), (1, x_hi))):
                    for c in range(CT):
                        last = pe.matmul(ps_x[0:MROW, 0:CHUNK], w[:, par, wp, c, :], xp[:, c, cols],
                                         start=j == 0 and c == 0, stop=j == 2 and c == CT - 1)
                last.then_inc(proj_done, 1)

            def maxima(h, par, m):
                t, k = divmod(m, len(PIECES))
                k0, kn = PIECES[k]
                last = (k0 + kn - 1) // CHUNK
                if t == 0 and last > (k0 - 1) // CHUNK:
                    pe.wait_ge(hi_made, (h * NCH + last + 1) * 3)
                if m % (3 * len(PIECES)) == 0:
                    pe.wait_ge(lo_made, (h * NCH + t // 3) * 3 + 2)
                at_least(pe, mx_red, h * NMX + m - 1)
                pe.matmul(ps_m[:, m % 2, 0:kn], q[0:MROW, par, t * P:(t + 1) * P], k_hi[0:MROW, par, k0:k0 + kn],
                          start=True, stop=True).then_inc(mx_done, 1)

            def scores(h, par, n):
                c, r = divmod(n, PAIRS)
                if n == 0:
                    pe.wait_ge(lo_made, (h + 1) * NCH * 3)
                if n in (0, STEPS // 2):
                    pe.wait_ge(row_in[n * 2 // STEPS], (h + 1) * 16)
                at_least(pe, e_made, h * STEPS + n - 1)
                for t in range(2):
                    for part in (k_hi, k_lo):
                        last = pe.matmul(ps_s[:, n % 2, t, 0:CHUNK],
                                         part[0:MROW + 1, par, (2 * r + t) * P:(2 * r + t + 1) * P],
                                         q[0:MROW + 1, par, c * CHUNK:(c + 1) * CHUNK],
                                         start=part is k_hi, stop=part is k_lo)
                last.then_inc(s_done, 1)

            def products(h, par, n):
                c, r = divmod(n, PAIRS)
                if n == 0:
                    pe.wait_ge(v_arrived, (h + 1) * 16)
                if r == 0:
                    at_least(pe, o_out, h * NCH + c)
                pe.wait_ge(e_hi_made, h * STEPS + n + 1)
                wait_lo(pe, h, n)
                for j, part in enumerate((e_hi, e_lo)):
                    for t in range(2):
                        last = pe.matmul(ps_o[0:ROW + 1, 0:CHUNK], v[:, par, 2 * r + t, 0:ROW + 1], part[:, slot(par, n), t],
                                         start=r == 0 and j == 0 and t == 0, stop=r == PAIRS - 1 and j == 1 and t == 1)
                last.then_inc(o_done, 1)

            def combine(h, c):
                take_ps_x(o_made, h * NCH + c + 1)
                pe.wait_ge(o_out, h * NCH + c + 1)
                for t in range(3):
                    last = pe.matmul(ps_x[:, t * (HD + 1):(t + 1) * (HD + 1)], o_t[:, c % 2, t * P:(t + 1) * P],
                                     comb[:], start=True, stop=True)
                last.then_inc(comb_done, 1)

            def turn(h, par, half):
                take_ps_x(row_out, h * 2 + half + 1)
                pe.wait_ge(mx_fin, h * 2 + half + 1)
                pe.transpose(ps_x[0:HQ, 0:P], mx[:, par, half * HQ:(half + 1) * HQ], ident[:]).then_inc(row_turned, 1)

            def body(h, par, main, prev, nxt):
                if prev:
                    free[0] = (o_made, (h - 1) * NCH + NCH - 1)
                for n in range(STEPS):
                    if main:
                        scores(h, par, n)
                    if nxt and n in MAX_AT:
                        maxima(h + 1, 1 - par, MAX_AT[n][0])
                    if nxt and n in JOBS_AT:
                        project(h + 1, 1 - par, JOBS_AT[n])
                    if main and n in COMB_AT:
                        combine(h, COMB_AT[n])
                    if prev and n + STEPS in COMB_AT:
                        combine(h - 1, COMB_AT[n + STEPS])
                    if prev and n < LAG:
                        products(h - 1, 1 - par, n - LAG + STEPS)
                    if main and n >= LAG:
                        products(h, par, n - LAG)
                    if nxt and n in MAX_AT:
                        maxima(h + 1, 1 - par, MAX_AT[n][1])
                    if nxt and n == ROW_0_AT:
                        turn(h + 1, 1 - par, 0)
                    if main and n == ROW_1_AT:
                        turn(h, par, 1)

            bodies(body, pe)


def project_stage(nc, ident, o, w_in, v_bias, p_bias, x, y, nb=B):
    S = nb * NCH
    T3 = CHUNK // P
    with ExitStack() as ctx:
        def sb(name, shape, dt=F32):
            return ctx.enter_context(nc.sbuf_tensor(f"p_{name}", shape, dt))

        def psum(name, shape):
            return ctx.enter_context(nc.psum_tensor(f"p_{name}", shape, F32))

        def sem(name):
            return ctx.enter_context(nc.semaphore(f"p_{name}"))

        w_hi = sb("w_hi", [P, CT, C], F32R)
        w_lo = sb("w_lo", [P, CT, C], F32R)
        vb = sb("vb", [P, CT])
        pb = sb("pb", [P, CT])
        o_tok = sb("o_tok", [P, 2, T3, C])
        res = sb("res", [P, 3, CT, CHUNK])
        o_hi = sb("o_hi", [P, 2, CT, CHUNK], F32R)
        o_lo = sb("o_lo", [P, 2, CT, CHUNK], F32R)
        yt = sb("yt", [P, 2, CT, CHUNK])
        ps_t = psum("ps_t", [P, CT, 512])
        ps_y = psum("ps_y", [P, CT, 512])
        par_in, o_in, res_in, turned = sem("par_in"), sem("o_in"), sem("res_in"), sem("turned")
        w_raw = sb("w_raw", [P, CT * C])
        w_split, w_ready = sem("w_split"), sem("w_ready")
        hi_made, lo_made, y_done, y_made, stored = (sem("hi_made"), sem("lo_made"), sem("y_done"), sem("y_made"),
                                                    sem("stored"))
        o_v = o.rearrange("b (s t p) c -> (b s) p t c", t=T3, p=P)
        x_v = x.rearrange("b (t p) n -> b p t n", p=P)
        y_v = y.rearrange("b (t p) n -> b p t n", p=P)
        block = ctx.enter_context(nc.Block())

        @block.sync
        def _(sp):
            sp.dma_start(w_raw[:], w_in).then_inc(par_in, 16)
            sp.dma_start(vb[:], v_bias.rearrange("(t p) -> p t", p=P), allow_slow_non_contiguous=True).then_inc(par_in, 16)
            sp.dma_start(pb[:], p_bias.rearrange("(t p) -> p t", p=P), allow_slow_non_contiguous=True).then_inc(par_in, 16)
            for a, z in segments(S + 2, [1, 2, 3, S]):
                with sp.Fori(a, z) as it:
                    if a < S:
                        if a >= 1:
                            sp.wait_ge(o_in, it * 16)
                        if a >= 2:
                            sp.wait_ge(turned, (it - 1) * CT)
                        sp.dma_start(o_tok[:, it % 2], o_v[it]).then_inc(o_in, 16)
                        if a >= 1:
                            sp.wait_ge(res_in, it * 16)
                        if a >= 3:
                            sp.wait_ge(y_made, (it - 2) * CT)
                        sp.dma_start(res[:, it % 3], x_v[it // NCH, :, :, bass.ds((it % NCH) * CHUNK, CHUNK)]).then_inc(res_in, 16)
                    if a >= 2:
                        s = it - 2
                        sp.wait_ge(y_made, s * CT + CT)
                        sp.dma_start(y_v[s // NCH, :, :, bass.ds((s % NCH) * CHUNK, CHUNK)], yt[:, s % 2]).then_inc(stored, 16)
            sp.wait_ge(stored, S * 16)

        @block.scalar
        def _(act):
            act.wait_ge(par_in, 48)
            act.activation(w_hi[:].rearrange("p t n -> p (t n)"), w_raw[:], ACT.Copy).then_inc(w_split, 1)
            for a, z in segments(S, [2]):
                with act.Fori(a, z) as it:
                    if a >= 2:
                        act.wait_ge(y_done, (it - 1) * CT)
                    for t in range(CT):
                        act.wait_ge(turned, it * CT + t + 1)
                        act.activation(o_hi[:, it % 2, t], ps_t[:, t, 0:CHUNK], ACT.Identity,
                                       bias=vb[:, t:t + 1]).then_inc(hi_made, 1)

        @block.vector
        def _(dve):
            dve.wait_ge(w_split, 1)
            dve.tensor_tensor(w_lo[:].rearrange("p t n -> p (t n)"), w_raw[:], f32(w_hi[:]).rearrange("p t n -> p (t n)"),
                              ALU.subtract).then_inc(w_ready, 1)
            for a, z in segments(S + 1, [1, 2, 3, S]):
                with dve.Fori(a, z) as it:
                    if a < S:
                        for t in range(CT):
                            dve.wait_ge(hi_made, it * CT + t + 1)
                            dve.scalar_tensor_tensor(out=o_lo[:, it % 2, t], in0=ps_t[:, t, 0:CHUNK], scalar=vb[:, t:t + 1],
                                                     in1=f32(o_hi[:, it % 2, t]), op0=ALU.add,
                                                     op1=ALU.subtract).then_inc(lo_made, 1)
                    if a >= 1:
                        s = it - 1
                        if a >= 2:
                            dve.wait_ge(stored, s * 16)
                        dve.wait_ge(res_in, (s + 1) * 16)
                        for t in range(CT):
                            dve.wait_ge(y_done, s * CT + t + 1)
                            dve.scalar_tensor_tensor(out=yt[:, s % 2, t], in0=ps_y[:, t, 0:CHUNK], scalar=pb[:, t:t + 1],
                                                     in1=res[:, s % 3, t], op0=ALU.add, op1=ALU.add).then_inc(y_made, 1)

        @block.tensor
        def _(pe):
            pe.wait_ge(w_ready, 1)

            def turn(s, k):
                pe.wait_ge(o_in, (s + 1) * 16)
                at_least(pe, lo_made, s * CT)
                for c in range(CT):
                    for t in range(T3):
                        last = pe.transpose(ps_t[:, c, t * P:(t + 1) * P], o_tok[:, k, t, c * P:(c + 1) * P], ident[:])
                    last.then_inc(turned, 1)

            def mul(s, k):
                pe.wait_ge(lo_made, (s + 1) * CT)
                for m in range(CT):
                    at_least(pe, y_made, (s - 1) * CT + m + 1)
                    for j, (wp, op) in enumerate(((w_hi, o_hi), (w_hi, o_lo), (w_lo, o_hi))):
                        for c in range(CT):
                            last = pe.matmul(ps_y[:, m, 0:CHUNK], wp[:, c, m * P:(m + 1) * P], op[:, k, c],
                                             start=j == 0 and c == 0, stop=j == 2 and c == CT - 1)
                    last.then_inc(y_done, 1)

            turn(0, 0)
            turn(1, 1)
            mul(0, 0)
            with pe.Fori(1, S // 2) as i:
                turn(i * 2, 0)
                mul(i * 2 - 1, 1)
                turn(i * 2 + 1, 1)
                mul(i * 2, 0)
            mul(S - 1, 1)


def mlp_stage(nc, ident, ones, n1, w1_src, w2_src, b1, grn_g, grn_b, b2, y, out, nb=B):
    with ExitStack() as ctx:
        def sb(name, shape, dt=F32):
            return ctx.enter_context(nc.sbuf_tensor(f"m_{name}", shape, dt))

        def psum(name, shape):
            return ctx.enter_context(nc.psum_tensor(f"m_{name}", shape, F32))

        def sem(name):
            return ctx.enter_context(nc.semaphore(f"m_{name}"))

        NF = NCH * FT
        NC3 = NCH * CT
        w1_hi, w1_lo = sb("w1_hi", [P, CT, FH], F32R), sb("w1_lo", [P, CT, FH], F32R)
        w2_hi, w2_lo = sb("w2_hi", [P, FT, C], F32R), sb("w2_lo", [P, FT, C], F32R)
        hid = sb("hid", [P, FT, N])
        io = sb("io", [P, CT, CHUNK])
        x_hi, x_lo = sb("x_hi", [P, CT, CHUNK], F32R), sb("x_lo", [P, CT, CHUNK], F32R)
        h_hi, h_lo = sb("h_hi", [P, 2, CHUNK], F32R), sb("h_lo", [P, 2, CHUNK], F32R)
        junk = sb("junk", [P, CHUNK])
        par = sb("par", [P, 3, FT])
        bias2 = sb("bias2", [P, CT])
        sq = sb("sq", [P, FT, NCH])
        tot, gx, nx, gn, scale = (sb(n, [P, FT]) for n in ("tot", "gx", "nx", "gn", "scale"))
        mean = sb("mean", [P, 3])
        ps_sum, ps_h, ps_y = psum("ps_sum", [P, FT]), psum("ps_h", [P, 2, 512]), psum("ps_y", [P, CT, 512])
        PIECE = FH // 4
        w1_in = [sem(f"w1_in{n}") for n in range(4)]
        w_split, w_ready = sem("w_split"), sem("w_ready")
        w2_in, par_in, x_in, res_in = sem("w2_in"), sem("par_in"), sem("x_in"), sem("res_in")
        x_hi_made, x_lo_made = sem("x_hi_made"), sem("x_lo_made")
        h_done, h_made, sq_made = sem("h_done"), sem("h_made"), sem("sq_made")
        tot_made, gx_made, gsum_done, grn_step = sem("tot_made"), sem("gx_made"), sem("gsum_done"), sem("grn_step")
        scaled, h_hi_made, h_lo_made = sem("scaled"), sem("h_hi_made"), sem("h_lo_made")
        h_used, y_done, y_made, stored = sem("h_used"), sem("y_done"), sem("y_made"), sem("stored")
        USES = FT - 1

        def slot_used(eng, b, n):
            c, f = divmod(n - 2, FT)
            if n < 2:
                at_least(eng, y_done, b * NC3)
            elif f == FT - 1:
                eng.wait_ge(y_done, (b * NCH + c + 1) * CT)
            else:
                eng.wait_ge(h_used, (b * NCH + c) * USES + f + 1)

        SPLIT_AT = {0: 1, FT // 4: 2, FT // 2: 3, 2 * FT: 4}
        GRN = 6

        n1_v = n1.rearrange("b (t p) (s n) -> b s p t n", p=P, n=CHUNK)
        y_v = y.rearrange("b (t p) (s n) -> b s p t n", p=P, n=CHUNK)
        out_v = out.rearrange("b (t p) (s n) -> b s p t n", p=P, n=CHUNK)

        def images(eng, *parts):
            for part in parts:
                part(0)
            if nb > 1:
                with eng.Fori(1, nb) as b:
                    for part in parts:
                        with eng.Fori(b, b + 1) as own:
                            part(own)

        def weights(n):
            if n == 4:
                return w2_hi[:], w2_lo[:], w2_raw, w2_in
            cols = slice(n * PIECE, (n + 1) * PIECE)
            return w1_hi[:, :, cols], w1_lo[:, :, cols], w1_raw[n], w1_in[n]

        w1_raw = [hid[:, n:FT:4, 5 * CHUNK:6 * CHUNK] for n in range(4)]
        w2_raw = hid[:, :, 4 * CHUNK:5 * CHUNK]
        first_raw = hid[:, 0:CT, CHUNK:2 * CHUNK]
        assert PIECE == CHUNK and C == CHUNK and CT * 4 == FT

        block = ctx.enter_context(nc.Block())

        @block.sync
        def _(sp):
            def first(b):
                sp.dma_start(first_raw, n1_v[b, 0]).then_inc(x_in, 16)

            def w1_piece(n):
                cols = slice(n * PIECE, (n + 1) * PIECE)
                sp.dma_start(w1_raw[n], w1_src.rearrange("p (t n) -> p t n", t=CT)[:, :, cols]).then_inc(w1_in[n], 16)

            def chunk(b, c):
                if c == 1:
                    at_least(sp, stored, b * NCH * 16)
                sp.wait_ge(x_lo_made, (b * NCH + c) * CT)
                sp.dma_start(io[:], n1_v[b, c]).then_inc(x_in, 16)

            def inputs(b):
                for c in range(1, NCH):
                    chunk(b, c)

            def results(b, more=True):
                for c in range(NCH):
                    if c == 0:
                        sp.wait_ge(x_lo_made, (b + 1) * NC3)
                    at_least(sp, stored, (b * NCH + c) * 16)
                    sp.dma_start(io[:], y_v[b, c]).then_inc(res_in, 16)
                    sp.wait_ge(y_made, b * NC3 + (c + 1) * CT)
                    sp.dma_start(out_v[b, c], io[:]).then_inc(stored, 16)
                    if c == 1 and more:
                        sp.wait_ge(h_lo_made, b * NF + 2 * FT)
                        first(b + 1)

            first(0)
            w1_piece(0)
            for i, src in enumerate((b1, grn_g, grn_b)):
                sp.dma_start(par[:, i], src.rearrange("(t p) -> p t", p=P), allow_slow_non_contiguous=True).then_inc(par_in, 16)
            sp.dma_start(bias2[:], b2.rearrange("(t p) -> p t", p=P), allow_slow_non_contiguous=True).then_inc(par_in, 16)
            for n in range(1, 4):
                w1_piece(n)
            chunk(0, 1)
            sp.dma_start(w2_raw, w2_src.rearrange("p (t n) -> p t n", t=FT)).then_inc(w2_in, 16)
            for c in range(2, NCH):
                chunk(0, c)
            if nb > 1:
                with sp.Fori(1, nb) as b:
                    for part, image in ((results, b - 1), (inputs, b)):
                        with sp.Fori(image, image + 1) as own:
                            part(own)
            results(nb - 1, more=False)
            sp.wait_ge(stored, nb * NCH * 16)

        @block.scalar
        def _(act):
            act.wait_ge(par_in, 64)

            def split(n):
                hi, _lo, whole, arrived = weights(n)
                act.wait_ge(arrived, 16)
                act.activation(hi, whole, ACT.Copy).then_inc(w_split, 1)

            split(0)

            def up(b):
                for c in range(NCH):
                    at_least(act, h_done, (b * NCH + c) * FT)
                    act.wait_ge(x_in, (b * NCH + c + 1) * 16)
                    for t in range(CT):
                        act.activation(x_hi[:, t], first_raw[:, t] if c == 0 else io[:, t], ACT.Copy).then_inc(x_hi_made, 1)
                    if c == 0:
                        at_least(act, h_lo_made, b * NF)
                        at_least(act, h_hi_made, b * NF)
                    for f in range(FT):
                        n = c * FT + f
                        if isinstance(b, int) and n in SPLIT_AT:
                            split(SPLIT_AT[n])
                        act.wait_ge(h_done, b * NF + n + 1)
                        act.activation(hid[:, f, c * CHUNK:(c + 1) * CHUNK], ps_h[:, f % 2, 0:CHUNK], ACT.Gelu,
                                       bias=par[:, 0, f:f + 1]).then_inc(h_made, 1)

            def down(b):
                act.wait_ge(tot_made, b + 1)
                act.activation(gx[:], tot[:], ACT.Sqrt).then_inc(gx_made, 1)
                for n in range(NF):
                    c, f = divmod(n, FT)
                    act.wait_ge(scaled, b * NF + n + 1)
                    slot_used(act, b, n)
                    act.activation(h_hi[:, n % 2], hid[:, f, c * CHUNK:(c + 1) * CHUNK], ACT.Copy).then_inc(h_hi_made, 1)

            images(act, up, down)

        @block.vector
        def _(dve):
            dve.wait_ge(par_in, 64)

            def grn(b):
                dve.wait_ge(sq_made, (b + 1) * NF)
                dve.tensor_reduce(tot[:], sq[:], AX.X, ALU.add).then_inc(tot_made, 1)
                dve.wait_ge(gsum_done, b + 1)
                dve.tensor_reduce(mean[:, 0:1], ps_sum[:], AX.X, ALU.add).then_inc(grn_step, 1)
                at = b * GRN
                dve.wait_ge(grn_step, at + 1)
                dve.tensor_scalar(mean[:, 1:2], mean[:, 0:1], 1.0 / FH, 1e-6, ALU.mult, ALU.add).then_inc(grn_step, 1)
                dve.wait_ge(grn_step, at + 2)
                dve.reciprocal(mean[:, 2:3], mean[:, 1:2]).then_inc(grn_step, 1)
                dve.wait_ge(grn_step, at + 3)
                dve.tensor_scalar(nx[:], gx[:], mean[:, 2:3], None, ALU.mult).then_inc(grn_step, 1)
                dve.wait_ge(grn_step, at + 4)
                dve.tensor_tensor(gn[:], nx[:], par[:, 1], ALU.mult).then_inc(grn_step, 1)
                dve.wait_ge(grn_step, at + 5)
                dve.tensor_scalar(scale[:], gn[:], 1.0, None, ALU.add).then_inc(grn_step, 1)

            def split(n):
                hi, lo, whole, _arrived = weights(n)
                dve.wait_ge(w_split, n + 1)
                dve.tensor_tensor(lo, whole, f32(hi), ALU.subtract).then_inc(w_ready, 1)

            split(0)

            def up(b):
                for c in range(NCH):
                    for t in range(CT):
                        dve.wait_ge(x_hi_made, (b * NCH + c) * CT + t + 1)
                        dve.tensor_tensor(x_lo[:, t], first_raw[:, t] if c == 0 else io[:, t], f32(x_hi[:, t]),
                                          ALU.subtract).then_inc(x_lo_made, 1)
                    for f in range(FT):
                        n = c * FT + f
                        if isinstance(b, int) and n in SPLIT_AT:
                            split(SPLIT_AT[n])
                        dve.wait_ge(h_made, b * NF + n + 1)
                        at_least(dve, sq_made, b * NF + n)
                        part = hid[:, f, c * CHUNK:(c + 1) * CHUNK]
                        dve.tensor_tensor_reduce(junk[:], part, part, 1.0, 0.0, ALU.mult, ALU.add,
                                                 sq[:, f, c:c + 1]).then_inc(sq_made, 1)

            def sums(b, c):
                dve.wait_ge(res_in, (b * NCH + c + 1) * 16)
                for t in range(CT):
                    dve.wait_ge(y_done, (b * NCH + c) * CT + t + 1)
                    dve.scalar_tensor_tensor(out=io[:, t], in0=ps_y[:, t, 0:CHUNK], scalar=bias2[:, t:t + 1],
                                             in1=io[:, t], op0=ALU.add, op1=ALU.add).then_inc(y_made, 1)

            def affine(b, n):
                c, f = divmod(n, FT)
                part = hid[:, f, c * CHUNK:(c + 1) * CHUNK]
                dve.tensor_scalar(part, part, scale[:, f:f + 1], par[:, 2, f:f + 1], ALU.mult, ALU.add).then_inc(scaled, 1)

            def down(b):
                grn(b)
                dve.wait_ge(grn_step, (b + 1) * GRN)
                affine(b, 0)
                for c in range(NCH):
                    for f in range(FT):
                        n = c * FT + f
                        if n + 1 < NF:
                            affine(b, n + 1)
                        dve.wait_ge(h_hi_made, b * NF + n + 1)
                        slot_used(dve, b, n)
                        dve.tensor_tensor(h_lo[:, n % 2], hid[:, f, c * CHUNK:(c + 1) * CHUNK], f32(h_hi[:, n % 2]),
                                          ALU.subtract).then_inc(h_lo_made, 1)
                        if f == 0 and c > 0:
                            sums(b, c - 1)
                sums(b, NCH - 1)

            images(dve, up, down)

        @block.tensor
        def _(pe):
            def up(b, c):
                for f in range(FT):
                    n = c * FT + f
                    at_least(pe, h_made, b * NF + n - 1)
                    if isinstance(b, int) and c == 0 and f % (FT // 4) == 0:
                        pe.wait_ge(w_ready, f // (FT // 4) + 1)
                    for j, (wp, xp) in enumerate(((w1_hi, x_hi), (w1_lo, x_hi), (w1_hi, x_lo))):
                        for t in range(CT):
                            if f == 0 and j != 1:
                                pe.wait_ge(x_lo_made if j else x_hi_made, (b * NCH + c) * CT + t + 1)
                            last = pe.matmul(ps_h[:, f % 2, 0:CHUNK], wp[:, t, f * P:(f + 1) * P], xp[:, t],
                                             start=j == 0 and t == 0, stop=j == 2 and t == CT - 1)
                    last.then_inc(h_done, 1)

            def down(b, c):
                for f in range(FT):
                    n = c * FT + f
                    pe.wait_ge(h_hi_made, b * NF + n + 1)
                    pe.wait_ge(h_lo_made, b * NF + n + 1)
                    for m in range(CT):
                        if f == 0:
                            at_least(pe, y_made, (b * NCH + c - 1) * CT + m + 1)
                        for j, (wp, hp) in enumerate(((w2_hi, h_hi), (w2_hi, h_lo), (w2_lo, h_hi))):
                            last = pe.matmul(ps_y[:, m, 0:CHUNK], wp[:, f, m * P:(m + 1) * P], hp[:, n % 2],
                                             start=f == 0 and j == 0, stop=f == FT - 1 and j == 2)
                        if f == FT - 1:
                            last.then_inc(y_done, 1)
                    if f < FT - 1:
                        last.then_inc(h_used, 1)

            def all_up(b):
                for c in range(NCH):
                    up(b, c)

            def all_down(b):
                pe.wait_ge(w_ready, 5)
                pe.wait_ge(gx_made, b + 1)
                at_least(pe, grn_step, b * GRN)
                pe.matmul(ps_sum[:], ones[:], gx[:], start=True, stop=True).then_inc(gsum_done, 1)
                for c in range(NCH):
                    down(b, c)

            images(pe, all_up, all_down)


def build(nc, a, out):
    def scratch(name, shape):
        return nc.dram_tensor(name, shape, F32, kind="Internal").ap()

    x_hi, x_lo, v = scratch("x_hi", (B, C, N)), scratch("x_lo", (B, C, N)), scratch("v", (B, N, HEADS * 2 * HD))
    local, normed1 = scratch("local", (B, C, N)), scratch("normed1", (B, C, N))
    o, y = scratch("o", (B, N, C)), scratch("y", (B, C, N))
    w_hi, w_lo = scratch("w_qk_hi", a["w_qk"].shape), scratch("w_qk_lo", a["w_qk"].shape)
    flat = a["x"].rearrange("b c h w -> b c (h w)")
    with ExitStack() as ctx:
        ident, cmask, ones = shared_consts(nc, ctx)
        split_stage(nc, "s", [(a["w_qk"][h], w_hi[h], w_lo[h]) for h in range(HEADS)])
        conv_stage(nc, "c0", ident, cmask, a["x"], a["taps0"], a["affine0"], a["ln0_g"], a["ln0_b"], local)
        norm_stage(nc, ident, flat, a["ln0_g"], a["ln0_b"], a["w_v"], x_hi, x_lo, v)
        attend_stage(nc, ident, x_hi, x_lo, v, w_hi, w_lo, a["qkv_b"][0:C], a["qkv_b"][C:2 * C], local, o)
        project_stage(nc, ident, o, a["w_proj"], a["qkv_b"][2 * C:3 * C], a["proj_b"], flat, y)
        conv_stage(nc, "c1", ident, cmask, y.rearrange("b c (h w) -> b c h w", w=W), a["taps1"], a["affine1"],
                   a["ln1_g"], a["ln1_b"], normed1)
        mlp_stage(nc, ident, ones, normed1, a["w_up"], a["w_down"], a["b1"], a["grn_g"], a["grn_b"],
                  a["b2"], y, out.rearrange("b c h w -> b c (h w)"))


def kernel(**inputs):
    import concourse.bacc as bacc
    from concourse.bass_utils import run_bass_kernel_spmd as run

    def tiles(w):
        t = w.shape[0] // P
        return np.ascontiguousarray(w.reshape(t, P, -1).transpose(1, 0, 2).reshape(P, -1))

    i = {k: np.asarray(v) for k, v in inputs.items()}
    q, k, v = i["L0_conv_qkv_w"].reshape(3, HEADS, HD, C)
    qk = np.concatenate([q, q[:, :64 - HD], k], axis=1).transpose(0, 2, 1)
    arrays = {
        "x": i["x"],
        "w_qk": np.stack([tiles(w) for w in qk]),
        "w_v": tiles(v.reshape(C, C).T),
        "w_proj": tiles(i["L0_conv_proj_w"].T),
        "w_up": tiles(i["L1_conv_w1"]),
        "w_down": tiles(i["L1_conv_w2"]),
        "taps0": i["L0_conv_conv_w"][:, :, ::-1],
        "taps1": i["L1_conv_dw_w"][:, :, ::-1],
        "affine0": np.stack([i["L0_conv_bn_" + n] for n in ("gamma", "beta", "mean", "var")]),
        "ln0_g": i["L0_conv_ln_gamma"], "ln0_b": i["L0_conv_ln_beta"],
        "qkv_b": i["L0_conv_qkv_b"], "proj_b": i["L0_conv_proj_b"],
        "affine1": i["L1_conv_dw_b"].reshape(1, C), "ln1_g": i["L1_conv_ln_g"], "ln1_b": i["L1_conv_ln_b"],
        "b1": i["L1_conv_b1"], "grn_g": i["L1_conv_grn_g"], "grn_b": i["L1_conv_grn_b"], "b2": i["L1_conv_b2"],
    }
    arrays = {k: np.ascontiguousarray(v) for k, v in arrays.items()}
    nc = bacc.Bacc("TRN2", target_bir_lowering=False, num_devices=1)
    aps = {k: nc.dram_tensor("in_" + k, v.shape, F32, kind="ExternalInput").ap() for k, v in arrays.items()}
    out = nc.dram_tensor("out", (B, C, H, W), F32, kind="ExternalOutput").ap()
    build(nc, aps, out)
    r = run(nc, [{"in_" + k: v for k, v in arrays.items()}], core_ids=[0])
    return r.results[0]["out"]
```
